# Optimizing a Trainium2 kernel written in Bass

```python
import numpy as np
import jax
import jax.numpy as jnp

def _softmax(x, axis=-1):
    return jax.nn.softmax(x, axis=axis)

def _gelu(x):
    return jax.nn.gelu(x, approximate=True)

def _silu(x):
    return jax.nn.silu(x)

def _sigmoid(x):
    return jax.nn.sigmoid(x)

def _layernorm(x, axis=-1, eps=1e-05):
    m = jnp.mean(x, axis=axis, keepdims=True)
    v = jnp.var(x, axis=axis, keepdims=True)
    return (x - m) / jnp.sqrt(v + eps)

def _scatter_add(tgt, idx, src, axis=0):
    return tgt.at[idx].add(src)

def _segment_sum(src, seg, n):
    return jax.ops.segment_sum(src, seg, n)
kernel_name = 'mk_adj_ffn_d2_adj_r2_0a456a'

def setup_inputs(seed: int=0):
    np.random.seed(seed)
    _w = jnp.asarray

    def _rec_inputs():
        import jax
        import jax.numpy as jnp
        _gk = jax.random.key(seed)
        x = -0.0005207 + 1.001 * jax.random.normal(jax.random.fold_in(_gk, 1), (1354, 256), jnp.float32)
        _w = (1.0 + jnp.arange(1354, dtype=jnp.float32)) ** (-0.5)
        _w = _w / _w.mean()
        _pij = jnp.clip(0.0118168 * _w[:, None] * _w[None, :], 0.0, 1.0)
        _a = jax.random.uniform(jax.random.fold_in(_gk, 2), (1354, 1354)) < _pij
        _af = _a.astype(jnp.float32)
        adj = _af
        return (x, adj)
    x, adj = _rec_inputs()

    def _L0_gnn_setup():
        import jax, jax.numpy as jnp
        import numpy as np
        ALPHA = 0.2
        NEG_INF = -1000000000000.0
        key = jax.random.key(seed)
        k1, k2, k3, k4, k5 = jax.random.split(key, 5)
        N, F = (2048, 256)
        inp = jax.random.normal(k1, (N, F), dtype=jnp.float32)
        adj = jax.random.randint(k2, (N, N), 0, 2).astype(jnp.float32)
        W = jax.random.normal(k3, (F, F), dtype=jnp.float32) * (1.414 / np.sqrt(F))
        a = jax.random.normal(k4, (2 * F, 1), dtype=jnp.float32) * 0.05
        wtrans = jax.random.normal(k5, (2 * F, F), dtype=jnp.float32) * (1.414 / np.sqrt(1.5 * F))
        return {'inp': inp, 'adj': adj, 'W': W, 'a': a, 'wtrans': wtrans}
    _L0_gnn_all = _L0_gnn_setup()
    _L0_gnn_in = {k: v for k, v in _L0_gnn_all.items() if k in ('W', 'a', 'wtrans')}
    del _L0_gnn_all

    def _L0_ffn_setup():
        import jax, jax.numpy as jnp
        import numpy as np
        B, T, D, F, E, TOP_K = (8, 2048, 256, 1024, 8, 2)

        def _moe_forward(x, Wr, W1, W2):
            b, t, d = x.shape
            e = Wr.shape[1]
            xf = x.reshape(-1, d)
            n = xf.shape[0]
            logits = xf @ Wr
            probs = jax.nn.softmax(logits, axis=-1)
            w, idx = jax.lax.top_k(probs, TOP_K)
            w = w.astype(xf.dtype)
            gates = jnp.zeros((n, e), xf.dtype).at[jnp.arange(n)[:, None], idx].add(w)

            def body(acc, expert):
                w1, w2, g = expert
                h = jax.nn.gelu(xf @ w1, approximate=False)
                return (acc + g[:, None] * (h @ w2), None)
            out, _ = jax.lax.scan(body, jnp.zeros_like(xf), (W1, W2, gates.T))
            return out.reshape(b, t, d)
        key = jax.random.key(seed)
        k1, k2, k3, k4 = jax.random.split(key, 4)
        x = jax.random.normal(k1, (B, T, D), jnp.float32)
        Wr = jax.random.normal(k2, (D, E), jnp.float32) * (1.0 / np.sqrt(D))
        W1 = jax.random.normal(k3, (E, D, F), jnp.float32) * (1.0 / np.sqrt(D))
        W2 = jax.random.normal(k4, (E, F, D), jnp.float32) * (1.0 / np.sqrt(F))
        return {'x': x, 'Wr': Wr, 'W1': W1, 'W2': W2}
    _L0_ffn_all = _L0_ffn_setup()
    _L0_ffn_in = {k: v for k, v in _L0_ffn_all.items() if k in ('Wr', 'W1', 'W2')}
    del _L0_ffn_all

    def _L1_gnn_setup():
        import jax, jax.numpy as jnp
        import numpy as np
        N, NFEAT, NHID = (4096, 256, 512)

        def _gc(x, adj, W, b):
            return adj @ (x @ W) + b
        key = jax.random.key(seed)
        ks = jax.random.split(key, 8)

        def glorot(k, shape):
            bound = 1.0 / np.sqrt(shape[0])
            return jax.random.uniform(k, shape, jnp.float32, -bound, bound)
        return {'x': jax.random.normal(ks[0], (N, NFEAT), jnp.float32), 'adj': jax.random.uniform(ks[1], (N, N), jnp.float32), 'W1': glorot(ks[2], (NFEAT, NHID)), 'b1': glorot(ks[3], (NHID,)), 'W2': glorot(ks[4], (NHID, NHID)), 'b2': glorot(ks[5], (NHID,)), 'W3': glorot(ks[6], (NHID, NFEAT)), 'b3': glorot(ks[7], (NFEAT,))}
    _L1_gnn_all = _L1_gnn_setup()
    _L1_gnn_in = {k: v for k, v in _L1_gnn_all.items() if k in ('W1', 'b1', 'W2', 'b2', 'W3', 'b3')}
    del _L1_gnn_all

    def _L1_ffn_setup():
        import jax, jax.numpy as jnp
        import numpy as np
        B, S, H, E, K, DF, SH = (8, 2048, 256, 8, 2, 128, 256)
        key = jax.random.key(seed)
        ks = jax.random.split(key, 10)
        n = lambda i, shape, sc: jax.random.normal(ks[i], shape, jnp.float32) * sc
        return {'hidden_states': n(0, (B, S, H), 1.0), 'gate_w': n(1, (E, H), 0.05), 'w1': n(2, (E, H, DF), 0.05), 'b1': n(3, (E, DF), 0.01), 'w2': n(4, (E, DF, H), 0.05), 'b2': n(5, (E, H), 0.01), 'sw1': n(6, (H, SH), 0.05), 'sb1': n(7, (SH,), 0.01), 'sw2': n(8, (SH, H), 0.05), 'sb2': n(9, (H,), 0.01)}
    _L1_ffn_all = _L1_ffn_setup()
    _L1_ffn_in = {k: v for k, v in _L1_ffn_all.items() if k in ('gate_w', 'w1', 'b1', 'w2', 'b2', 'sw1', 'sb1', 'sw2', 'sb2')}
    del _L1_ffn_all
    return {'x': x, 'adj': adj, 'L0_gnn_W': _L0_gnn_in['W'], 'L0_gnn_a': _L0_gnn_in['a'], 'L0_gnn_wtrans': _L0_gnn_in['wtrans'], 'L0_ffn_Wr': _L0_ffn_in['Wr'], 'L0_ffn_W1': _L0_ffn_in['W1'], 'L0_ffn_W2': _L0_ffn_in['W2'], 'L1_gnn_W1': _L1_gnn_in['W1'], 'L1_gnn_b1': _L1_gnn_in['b1'], 'L1_gnn_W2': _L1_gnn_in['W2'], 'L1_gnn_b2': _L1_gnn_in['b2'], 'L1_gnn_W3': _L1_gnn_in['W3'], 'L1_gnn_b3': _L1_gnn_in['b3'], 'L1_ffn_gate_w': _L1_ffn_in['gate_w'], 'L1_ffn_w1': _L1_ffn_in['w1'], 'L1_ffn_b1': _L1_ffn_in['b1'], 'L1_ffn_w2': _L1_ffn_in['w2'], 'L1_ffn_b2': _L1_ffn_in['b2'], 'L1_ffn_sw1': _L1_ffn_in['sw1'], 'L1_ffn_sb1': _L1_ffn_in['sb1'], 'L1_ffn_sw2': _L1_ffn_in['sw2'], 'L1_ffn_sb2': _L1_ffn_in['sb2']}

def reference(x, adj, L0_gnn_W, L0_gnn_a, L0_gnn_wtrans, L0_ffn_Wr, L0_ffn_W1, L0_ffn_W2, L1_gnn_W1, L1_gnn_b1, L1_gnn_W2, L1_gnn_b2, L1_gnn_W3, L1_gnn_b3, L1_ffn_gate_w, L1_ffn_w1, L1_ffn_b1, L1_ffn_w2, L1_ffn_b2, L1_ffn_sw1, L1_ffn_sb1, L1_ffn_sw2, L1_ffn_sb2):
    import jax
    import jax.numpy as jnp

    def _L0_gnn_ref(inp, adj, W, a, wtrans):
        import jax, jax.numpy as jnp
        import numpy as np
        ALPHA = 0.2
        NEG_INF = -1000000000000.0
        F_out = W.shape[1]
        h = inp @ W
        Wh1 = h @ a[:F_out, :]
        Wh2 = h @ a[F_out:, :]
        e = jax.nn.leaky_relu(Wh1 + Wh2.T, ALPHA)
        mask = adj > 0
        attention = jax.nn.softmax(jnp.where(mask, e, NEG_INF), axis=1)
        negative_attention = -jax.nn.softmax(jnp.where(mask, -e, NEG_INF), axis=1)
        h_prime = attention @ inp
        h_prime_negative = negative_attention @ inp
        h_prime_double = jnp.concatenate([h_prime, h_prime_negative], axis=1)
        new_h_prime = h_prime_double @ wtrans
        return jax.nn.elu(new_h_prime)

    def _L0_ffn_ref(x, Wr, W1, W2):
        import jax, jax.numpy as jnp
        import numpy as np
        B, T, D, F, E, TOP_K = (8, 2048, 256, 1024, 8, 2)

        def _moe_forward(x, Wr, W1, W2):
            b, t, d = x.shape
            e = Wr.shape[1]
            xf = x.reshape(-1, d)
            n = xf.shape[0]
            logits = xf @ Wr
            probs = jax.nn.softmax(logits, axis=-1)
            w, idx = jax.lax.top_k(probs, TOP_K)
            w = w.astype(xf.dtype)
            gates = jnp.zeros((n, e), xf.dtype).at[jnp.arange(n)[:, None], idx].add(w)

            def body(acc, expert):
                w1, w2, g = expert
                h = jax.nn.gelu(xf @ w1, approximate=False)
                return (acc + g[:, None] * (h @ w2), None)
            out, _ = jax.lax.scan(body, jnp.zeros_like(xf), (W1, W2, gates.T))
            return out.reshape(b, t, d)
        return _moe_forward(x, Wr, W1, W2)

    def _L1_gnn_ref(x, adj, W1, b1, W2, b2, W3, b3):
        import jax, jax.numpy as jnp
        import numpy as np
        N, NFEAT, NHID = (4096, 256, 512)

        def _gc(x, adj, W, b):
            return adj @ (x @ W) + b
        h = jax.nn.relu(_gc(x, adj, W1, b1))
        h = jax.nn.relu(_gc(h, adj, W2, b2))
        return _gc(h, adj, W3, b3)

    def _L1_ffn_ref(hidden_states, gate_w, w1, b1, w2, b2, sw1, sb1, sw2, sb2):
        import jax, jax.numpy as jnp
        import numpy as np
        B, S, H, E, K, DF, SH = (8, 2048, 256, 8, 2, 128, 256)
        x = hidden_states
        xf = x.reshape(-1, x.shape[-1])
        T = xf.shape[0]
        scores = jax.nn.softmax(xf @ gate_w.T, axis=-1)
        topk_w, topk_i = jax.lax.top_k(scores, K)
        topk_w = topk_w / (topk_w.sum(-1, keepdims=True) + 1e-20)
        combine = jnp.zeros((T, E), xf.dtype).at[jnp.arange(T)[:, None], topk_i].add(topk_w)
        h1 = jax.nn.relu(jnp.einsum('th,ehf->tef', xf, w1) + b1)
        eo = jnp.einsum('tef,efh->teh', h1, w2) + b2
        y = jnp.einsum('te,teh->th', combine, eo)
        shared = jax.nn.relu(xf @ sw1 + sb1) @ sw2 + sb2
        return (y + shared).reshape(x.shape)
    x = x + _L0_gnn_ref(_layernorm(x, axis=-1), adj, L0_gnn_W, L0_gnn_a, L0_gnn_wtrans)
    x = x + _L0_ffn_ref(_layernorm(x, axis=-1)[None], L0_ffn_Wr, L0_ffn_W1, L0_ffn_W2)[0]
    x = x + _L1_gnn_ref(_layernorm(x, axis=-1), adj, L1_gnn_W1, L1_gnn_b1, L1_gnn_W2, L1_gnn_b2, L1_gnn_W3, L1_gnn_b3)
    x = x + _L1_ffn_ref(_layernorm(x, axis=-1)[None], L1_ffn_gate_w, L1_ffn_w1, L1_ffn_b1, L1_ffn_w2, L1_ffn_b2, L1_ffn_sw1, L1_ffn_sb1, L1_ffn_sw2, L1_ffn_sb2)[0]
    return x

_drawn_inputs = setup_inputs


def setup_inputs(seed=0):
    import zlib

    import numpy as np

    out = dict(_drawn_inputs(seed))
    spreads = {}
    factors = {'L1_gnn_b1': 7.398,
     'L1_gnn_b2': 64.0,
     'L1_gnn_b3': 200.0,
     'L1_ffn_gate_w': 8.0,
     'L1_ffn_w1': 8.0,
     'L1_ffn_b1': 200.0,
     'L1_ffn_w2': 8.0,
     'L1_ffn_b2': 200.0,
     'L1_ffn_sw1': 8.0,
     'L1_ffn_sb1': 200.0,
     'L1_ffn_sw2': 8.0,
     'L1_ffn_sb2': 200.0}
    for name, (base, spread) in spreads.items():
        noise = np.random.default_rng([zlib.crc32(name.encode()), seed]).standard_normal(out[name].shape)
        drawn = base * np.exp(spread * noise) if base else spread * noise
        out[name] = jnp.asarray(drawn.astype(out[name].dtype))
    for name, factor in factors.items():
        out[name] = (out[name] * factor).astype(out[name].dtype)
    return out
```

```python
import concourse.bass as bass
from concourse import mybir
from contextlib import ExitStack

F32 = mybir.dt.float32
I32 = mybir.dt.int32
ALU = mybir.AluOpType
ACT = mybir.ActivationFunctionType
AX = mybir.AxisListType.X


def gat_moe_gcn_moe_kernel(nc, x, adj, gat_W, gat_a, gat_wtrans, moe_Wr, moe_W1, moe_W2,
                           gcn_W1, gcn_b1, gcn_W2, gcn_b2, gcn_W3, gcn_b3,
                           ffn_gate, ffn_w1, ffn_b1, ffn_w2, ffn_b2, ffn_sw1, ffn_sb1, ffn_sw2, ffn_sb2, out):
    P = 128
    N, D = x.shape
    NT = -(-N // P)
    NP = NT * P
    KD = D // P
    E, _, F = moe_W1.shape
    FK = F // P
    HID = gcn_W1.shape[1]
    HK = HID // P
    E2, _, DF = ffn_w1.shape
    SH = ffn_sw1.shape[1]
    SK = SH // P
    EPS = 1e-5
    BIG = 1e30
    ALPHA = 0.2
    NC = 3
    CW = -(-N // NC)
    CW += CW % 2
    CHUNKS = [(c * CW, min(CW, N - c * CW)) for c in range(NC)]
    GROUPS = [(0, 3), (3, 3), (6, 3), (9, 2)]
    GW = 3 * P
    MROWS = [(s, t, 4 * ((s * (-(-NT // 4)) + t // 4) % 2) + t % 4) for s in range(2) for t in range(NT)]
    SLOTS = (2 * N + E * (P - 1)) // P
    PSB = 512
    full = N // P
    tail = N - full * P

    def rows(t):
        return min(P, N - t * P)

    xs = nc.dram_tensor("routed_rows", (SLOTS * P, D), F32).ap()
    ys = nc.dram_tensor("expert_rows", (SLOTS * P, D), F32).ap()

    ctx = ExitStack()
    with ctx:
        def sb(name, shape, dt=F32):
            return ctx.enter_context(nc.sbuf_tensor(name, shape, dt))

        def sem(name):
            return ctx.enter_context(nc.semaphore(name))

        X = sb("X", [P, NT, D])
        Nn = sb("Nn", [P, NT, D])
        NTr = sb("NTr", [P, KD, NP])
        AT = sb("AT", [P, NT, N])
        ident = sb("ident", [P, P])
        ones = sb("ones", [P, P])
        upper = sb("upper", [P, P])
        stats = sb("stats", [P, NT, 6])
        mv = sb("mv", [P, NT, 2])
        rstd = sb("rstd", [P, NT])
        neghalf = sb("neghalf", [P, NT])
        logits = sb("logits", [P, NT, E])
        probs = sb("probs", [P, NT, E])
        eq = sb("eq", [P, NT, E])
        oh1 = sb("oh1", [P, NT, E])
        oh2 = sb("oh2", [P, NT, E])
        probs2 = sb("probs2", [P, NT, E])
        rtmp = sb("rtmp", [P, NT])
        p1 = sb("p1", [P, NT])
        p2 = sb("p2", [P, NT])
        rev = sb("rev", [P, E])
        valid = sb("valid", [P, NT])
        arena = nc.sbuf_base
        arena = -(-arena // 64) * 64

        class Place:
            def __init__(self, at):
                self.at = at

            def __call__(self, name, shape, dt=F32):
                n = 4
                for s in shape[1:]:
                    n *= s
                t = nc.alloc_sbuf_tensor_at(name, shape, dt, offset=self.at)
                self.at += -(-n // 32) * 32
                return t

        pl = Place(arena)
        adjn = [pl(f"adjn{i}", [P, NP]) for i in range(2)]
        negn = pl("negn", [P, N])
        junk = pl("junk", [P, N])
        gW = pl("gW", [P, KD, D])
        gWT = pl("gWT", [P, KD, D])
        a2 = pl("a2", [P, 2, KD])
        wtr = pl("wtr", [P, KD, 2, D])
        Wa = pl("Wa", [P, KD, 2])
        WaB = pl("WaB", [P, 2, KD, P])
        Wh = pl("Wh", [P, NT, 2])
        Wrow = [pl("W1row", [P, N]), pl("W2row", [P, N])]
        mx = pl("mx", [P, 2, NT])
        ms = pl("ms", [P, 2, NT])
        m2 = pl("m2", [P, 2, NT])
        after_scan = Place(pl.at)
        pa = Place(arena)
        nm = [pa(f"nm{i}", [P, 2, GW]) for i in range(2)]
        ss = [pa(f"ss{i}", [P, GW]) for i in range(2)]
        zz = [pa(f"zz{i}", [P, 2, GW]) for i in range(2)]
        pp = [pa(f"pp{i}", [P, 2, GW]) for i in range(2)]
        assert pa.at <= arena + 4 * 4 * 2 * NP
        neg = after_scan("neg", [P, GW])
        leaky = after_scan("leaky", [P, GW])
        G = after_scan("G", [P, NT, 2, D + 2])
        mrow = [after_scan("mrow0", [P, NP]), after_scan("mrow1", [P, NP])]
        mB = after_scan("mB", [P, 8, P])
        nsum = after_scan("nsum", [P, KD])
        nsumB = after_scan("nsumB", [P, KD, P])
        Cs = after_scan("Cs", [P, 2, D])
        den = after_scan("den", [P, 2])
        emp = after_scan("emp", [P, 2])
        T1 = after_scan("T1", [P, 2, D])
        V = after_scan("V", [P, 3, D])
        V2 = after_scan("V2", [P, 3, D])
        Vm = after_scan("Vm", [P, NT, D])

        pb = Place(arena)
        W1b = pb("W1b", [P, 2, KD * F])
        W2b = pb("W2b", [P, 2, FK * D])
        Wr = pb("Wr", [P, KD, E])
        zero = pb("zero", [P, D])
        Msel = pb("Msel", [P, NT, E])
        Mpre = pb("Mpre", [P, NT + 1, E])
        rank = pb("rank", [P, NT + 1, E])
        kval = pb("kval", [P, NT])
        cmpk = pb("cmpk", [P, E, NT])
        cnt = pb("cnt", [P, E])
        cum = pb("cum", [P, E + 1])
        cumI = pb("cumI", [P, E + 1], I32)
        sval = pb("sval", [P, SLOTS])
        sexp = pb("sexp", [P, SLOTS, E])
        slot_e = pb("slot_e", [P, SLOTS])
        slot_eI = pb("slot_eI", [P, SLOTS], I32)
        slot_p = pb("slot_p", [P, SLOTS])
        slot_q = pb("slot_q", [P, SLOTS])
        slot_pI = pb("slot_pI", [P, SLOTS], I32)
        posf = pb("posf", [P, NT, E])
        pos = pb("pos", [P, 2, NT])
        posI = pb("posI", [P, 2, NT], I32)
        xg = pb("xg", [P, D])
        xgT = pb("xgT", [P, KD, P])
        hn = pb("hn", [P, F])
        hT = pb("hT", [P, FK, P])
        yrow = pb("yrow", [P, D])
        yg = pb("yg", [P, 2, NT, D])

        pc = Place(arena)
        cW1 = pc("cW1", [P, KD, HID])
        cW2 = pc("cW2", [P, HK, HID])
        cW3 = pc("cW3", [P, HK, D])
        cb1 = pc("cb1", [P, HK])
        cb2 = pc("cb2", [P, HK])
        cb3 = pc("cb3", [P, D])
        Z1T = pc("Z1T", [P, KD, N])
        H1T = pc("H1T", [P, HK, N])
        Y2 = pc("Y2", [P, NT, HID])
        H2T = pc("H2T", [P, HK, N])
        Y3 = pc("Y3", [P, NT, D])

        pd = Place(arena)
        gw = pd("gw", [E2, D])
        gT = pd("gT", [P, KD, E2])
        dW1 = pd("dW1", [P, E2, KD, DF])
        dW2 = pd("dW2", [P, E2, D])
        db1 = pd("db1", [P, E2])
        db2 = pd("db2", [E2, D])
        sW1 = pd("sW1", [P, KD, SH])
        sW2 = pd("sW2", [P, SK, D])
        sb1 = pd("sb1", [P, SK])
        sb2 = pd("sb2", [1, D])
        comb = pd("comb", [P, NT, E2])
        combT = pd("combT", [E2, NP])
        hE = [pd(f"hE{i}", [P, N]) for i in range(2)]
        hS = pd("hS", [P, SK, N])

        banks = [ctx.enter_context(nc.psum_tensor(f"bank{i}", [P, PSB], F32)) for i in range(8)]
        act_banks, dve_banks = banks[0:4], banks[4:8]

        s_x = sem("x_loaded")
        s_gw = sem("gat_weights_loaded")
        s_gw2 = sem("gat_score_weights_loaded")
        s_adj = [sem(f"adj_rows_loaded{i}") for i in range(2)]
        s_zero = sem("zeros_ready")
        s_xsz = sem("routed_rows_zeroed")
        s_id = sem("constant_steps")
        s_const = sem("constants_ready")
        s_dw2 = sem("dense_last_bias_loaded")
        s_fin = sem("result_ready")
        s_pad = sem("pads_cleared")
        act_full = sem("act_bank_full")
        act_done = sem("act_bank_done")
        dve_full = sem("dve_bank_full")
        dve_done = sem("dve_bank_done")
        chain = sem("vector_chain")
        s_var = sem("variance_ready")
        s_rstd = sem("inverse_deviation_ready")
        s_norm = sem("norm_tiles_ready")
        s_wab = sem("wa_broadcast_ready")
        s_scan = sem("adj_tile_scanned")
        s_mB = sem("m_broadcast_ready")
        s_nsum = sem("norm_sum_ready")
        s_neg0 = sem("edge_mask_ready")
        s_neg = sem("neg_mask_ready")
        s_t = sem("leaky_ready")
        s_z = sem("shifted_ready")
        s_p = sem("attention_weights_ready")
        s_used = sem("attention_weights_used")
        s_attd = sem("attention_group_done")
        s_vm = sem("elu_argument_ready")
        s_ve = sem("elu_exp_ready")
        s_x1 = sem("attention_added")
        s_we = [sem(f"expert_weights_loaded{i}") for i in range(2)]
        s_wfree = sem("expert_weights_free")
        s_wrdy = sem("expert_weights_ready")
        s_wr = sem("router_weights_loaded")
        s_lc = sem("logits_centred")
        s_le = sem("logits_exp")
        s_msel = sem("selection_ready")
        s_route = sem("routes_ready")
        s_scat = sem("rows_scattered")
        s_xg = sem("slot_rows_loaded")
        s_xt = sem("slot_rows_transposed")
        s_xtd = sem("slot_transpose_copied")
        s_h = sem("hidden_sums_ready")
        s_hd = sem("hidden_gelu_ready")
        s_ht = sem("hidden_transposed")
        s_htd = sem("hidden_transpose_copied")
        s_y = sem("slots_finished")
        s_yd = sem("slot_output_copied")
        s_yw = sem("slot_output_written")
        s_yg = sem("expert_rows_gathered")
        s_cw = sem("gcn_weights_loaded")
        s_mix = sem("mixture_added")
        s_dw = sem("dense_weights_loaded")
        s_gwt = sem("gate_loaded")
        s_comb = sem("combine_weights_ready")
        s_out = sem("output_written")

        block = ctx.enter_context(nc.Block())
        mark = {}

        @block.tensor
        def _(pe):
            na = [0]
            nv = [0]

            def act_bank():
                n = na[0]
                if n >= 4:
                    pe.wait_ge(act_done, n - 3)
                return act_banks[n % 4]

            def to_act(mm):
                na[0] += 1
                mm.then_inc(act_full, 1)
                return na[0]

            def dve_bank():
                n = nv[0]
                if n >= 4:
                    pe.wait_ge(dve_done, n - 3)
                return dve_banks[n % 4]

            def to_dve(mm):
                nv[0] += 1
                mm.then_inc(dve_full, 1)
                return nv[0]

            def transpose_norm(layer):
                for q in range(-(-NT // 2)):
                    tiles = range(2 * q, min(2 * q + 2, NT))
                    pe.wait_ge(s_norm, NT * layer + tiles[-1] + 1)
                    b = act_bank()
                    for i, t in enumerate(tiles):
                        for k in range(KD):
                            mm = pe.transpose(b[:, (k * 2 + i) * P:(k * 2 + i + 1) * P],
                                              Nn[:, t, k * P:(k + 1) * P], ident[:, :])
                    last = to_act(mm)
                return last

            def router(W):
                b = dve_bank()
                for t in range(NT):
                    r = rows(t)
                    for k in range(KD):
                        mm = pe.matmul(b[0:r, t * E:(t + 1) * E], NTr[:, k, t * P:t * P + r], W[:, k, :],
                                       start=(k == 0), stop=(k == KD - 1))
                return to_dve(mm)

            pe.wait_ge(s_const, 1)
            pe.wait_ge(s_gw, 16 * 2)
            pe.wait_ge(s_gw2, 16 * 2)
            b = act_bank()
            for fo in range(KD):
                for fi in range(KD):
                    mm = pe.transpose(b[:, (fo * KD + fi) * P:(fo * KD + fi + 1) * P],
                                      gW[:, fi, fo * P:(fo + 1) * P], ident[:, :])
            j = to_act(mm)
            pe.wait_ge(act_done, j)
            b = dve_bank()
            for fi in range(KD):
                for fo in range(KD):
                    mm = pe.matmul(b[:, 2 * fi:2 * fi + 2], gWT[:, fo, fi * P:(fi + 1) * P], a2[:, :, fo],
                                   start=(fo == 0), stop=(fo == KD - 1))
            to_dve(mm)
            j = transpose_norm(0)
            pe.wait_ge(act_done, j)
            pe.wait_ge(s_wab, 2 * KD)
            for w in (1, 0):
                for c0, cw in CHUNKS:
                    b = act_bank()
                    for k in range(KD):
                        mm = pe.matmul(b[:, 0:cw], WaB[:, w, k, :], NTr[:, k, c0:c0 + cw],
                                       start=(k == 0), stop=(k == KD - 1))
                    mark["row", w] = to_act(mm)
            b = dve_bank()
            for t in range(NT):
                r = rows(t)
                for k in range(KD):
                    mm = pe.matmul(b[0:r, 2 * t:2 * t + 2], NTr[:, k, t * P:t * P + r], Wa[:, k, :],
                                   start=(k == 0), stop=(k == KD - 1))
            mark["Wh"] = to_dve(mm)
            for t in range(NT):
                r = rows(t)
                pe.wait_ge(s_adj[t % 2], 16 * (t // 2 + 1))
                for j0 in range(0, NT, 4):
                    js = range(j0, min(j0 + 4, NT))
                    b = act_bank()
                    for i, j in enumerate(js):
                        mm = pe.transpose(b[:, i * P:i * P + r], adjn[t % 2][0:r, j * P:(j + 1) * P],
                                          ident[0:r, 0:r])
                    mark["adjT", t] = to_act(mm)
            for t in range(NT):
                r = rows(t)
                b = act_bank()
                for k in range(KD):
                    mm = pe.matmul(b[0:r, :], NTr[:, k, t * P:t * P + r], wtr[:, k, :, :],
                                   start=(k == 0), stop=(k == KD - 1))
                jG = to_act(mm)
            mark["G"] = jG
            pe.wait_ge(s_nsum, 1)
            b = dve_bank()
            for k in range(KD):
                mm = pe.matmul(b[:, :], nsumB[:, k, :], wtr[:, k, :, :], start=(k == 0), stop=(k == KD - 1))
            to_dve(mm)
            n = 0
            for s in range(2):
                for t0 in range(0, NT, 4):
                    b = dve_bank()
                    for t in range(t0, min(t0 + 4, NT)):
                        r = rows(t)
                        pe.wait_ge(s_mB, n + 1)
                        mm = pe.matmul(b[:, (t - t0) * P:(t - t0) * P + r],
                                       mB[0:r, MROWS[n][2], :], ident[0:r, 0:r], start=True, stop=True)
                        n += 1
                    mark["mrow"] = to_dve(mm)
            pe.wait_ge(act_done, na[0])
            pe.wait_ge(dve_done, nv[0])
            step = 0
            for g, (t0, nt) in enumerate(GROUPS):
                if g:
                    pe.wait_ge(s_attd, g)
                for j in range(NT):
                    r = rows(j)
                    step += 1
                    pe.wait_ge(s_p, step)
                    for i in range(nt):
                        q = rows(t0 + i)
                        for s in range(2):
                            mm = pe.matmul(banks[2 * i + s][0:q, 0:D + 1], pp[step % 2][0:r, s, i * P:i * P + q],
                                           G[0:r, j, s, 0:D + 1], start=(j == 0), stop=(j == NT - 1))
                    mm.then_inc(s_used, 1)
            pe.wait_ge(s_attd, len(GROUPS))

            j = transpose_norm(1)
            pe.wait_ge(act_done, j)
            pe.wait_ge(s_wr, 16)
            router(Wr)
            pe.wait_ge(s_msel, 1)
            b = dve_bank()
            pe.matmul(b[:, 0:(NT + 1) * E], ones[:, :], Mpre[:, :, :], start=True, stop=False)
            mm = pe.matmul(b[:, 0:NT * E], upper[:, :], Msel[:, :, :], start=False, stop=True)
            to_dve(mm)
            pe.wait_ge(act_done, na[0])
            pe.wait_ge(dve_done, nv[0])
            pe.wait_ge(s_route, 1)

            def rows_T(s):
                pe.wait_ge(s_xg, 16 * s + 16)
                for k in range(KD):
                    mm = pe.transpose(banks[0][:, k * P:(k + 1) * P], xg[:, k * P:(k + 1) * P], ident[:, :])
                mm.then_inc(s_xt, 1)

            def weights_of(s):
                return (pe.value_load(slot_eI[0:1, bass.ds(s, 1)], min_val=1, max_val=E),
                        pe.value_load(slot_pI[0:1, bass.ds(s, 1)], min_val=0, max_val=1))

            def up(s, e, par):
                pe.wait_ge(s_wrdy, e)
                pe.wait_ge(s_xtd, s + 1)
                w1 = W1b[:, :, :].rearrange("p b n -> p (b n)")
                for h in range(2):
                    for k in range(KD):
                        mm = pe.matmul(banks[1 + h][:, :], xgT[:, k, :],
                                       w1[:, bass.ds(par * (KD * F) + (k * F + h * PSB), PSB)],
                                       start=(k == 0), stop=(k == KD - 1))
                    mm.then_inc(s_h, 1)

            def hidden_T(s):
                for h in range(2):
                    pe.wait_ge(s_hd, 2 * s + h + 1)
                    for i in range(4):
                        f = 4 * h + i
                        mm = pe.transpose(banks[3 + h][:, i * P:(i + 1) * P], hn[:, f * P:(f + 1) * P], ident[:, :])
                    mm.then_inc(s_ht, 1)

            def down(s, par):
                w2 = W2b[:, :, :].rearrange("p b n -> p (b n)")
                for f in range(FK):
                    if f % 4 == 0:
                        pe.wait_ge(s_htd, 2 * s + f // 4 + 1)
                    mm = pe.matmul(banks[5][:, 0:D], hT[:, f, :],
                                   w2[:, bass.ds(par * (FK * D) + f * D, D)],
                                   start=(f == 0), stop=(f == FK - 1))
                mm.then_inc(s_y, 1)

            e0, par0 = weights_of(0)
            e1, par1 = weights_of(1)
            rows_T(0)
            up(0, e0, par0)
            rows_T(1)
            hidden_T(0)
            up(1, e1, par1)
            rows_T(2)
            down(0, par0)
            with pe.Fori(1, SLOTS - 2) as s:
                _, par = weights_of(s)
                e_next, par_next = weights_of(s + 1)
                hidden_T(s)
                up(s + 1, e_next, par_next)
                rows_T(s + 2)
                pe.wait_ge(s_yd, s)
                down(s, par)
            _, par = weights_of(SLOTS - 2)
            e_next, par_next = weights_of(SLOTS - 1)
            hidden_T(SLOTS - 2)
            up(SLOTS - 1, e_next, par_next)
            pe.wait_ge(s_yd, SLOTS - 2)
            down(SLOTS - 2, par)
            hidden_T(SLOTS - 1)
            pe.wait_ge(s_yd, SLOTS - 1)
            down(SLOTS - 1, par_next)

            pe.wait_ge(s_norm, 3 * NT)
            pe.wait_ge(s_cw, 16 * 6)
            pe.wait_ge(s_yd, SLOTS)
            for c0, cw in CHUNKS:
                for f in range(KD):
                    b = act_bank()
                    for j in range(NT):
                        r = rows(j)
                        mm = pe.matmul(b[:, 0:cw], Nn[0:r, j, f * P:(f + 1) * P], AT[0:r, j, c0:c0 + cw],
                                       start=(j == 0), stop=(j == NT - 1))
                    jz = to_act(mm)
            pe.wait_ge(act_done, jz)
            for c0, cw in CHUNKS:
                for h in range(HK):
                    b = act_bank()
                    for k in range(KD):
                        mm = pe.matmul(b[:, 0:cw], cW1[:, k, h * P:(h + 1) * P], Z1T[:, k, c0:c0 + cw],
                                       start=(k == 0), stop=(k == KD - 1))
                    jz = to_act(mm)
            pe.wait_ge(act_done, jz)
            for t in range(NT):
                r = rows(t)
                b = dve_bank()
                for k in range(HK):
                    mm = pe.matmul(b[0:r, 0:HID], H1T[:, k, t * P:t * P + r], cW2[:, k, :],
                                   start=(k == 0), stop=(k == HK - 1))
                jy = to_dve(mm)
            pe.wait_ge(dve_done, jy)
            for c0, cw in CHUNKS:
                for h in range(HK):
                    b = act_bank()
                    for j in range(NT):
                        r = rows(j)
                        mm = pe.matmul(b[:, 0:cw], Y2[0:r, j, h * P:(h + 1) * P], AT[0:r, j, c0:c0 + cw],
                                       start=(j == 0), stop=(j == NT - 1))
                    jz = to_act(mm)
            pe.wait_ge(act_done, jz)
            for t in range(NT):
                r = rows(t)
                b = dve_bank()
                for k in range(HK):
                    mm = pe.matmul(b[0:r, 0:D], H2T[:, k, t * P:t * P + r], cW3[:, k, :],
                                   start=(k == 0), stop=(k == HK - 1))
                jy = to_dve(mm)
            pe.wait_ge(dve_done, jy)
            for t in range(NT):
                q = rows(t)
                b = dve_bank()
                for j in range(NT):
                    r = rows(j)
                    mm = pe.matmul(b[0:q, 0:D], AT[0:r, j, t * P:t * P + q], Y3[0:r, j, :],
                                   start=(j == 0), stop=(j == NT - 1))
                to_dve(mm)
            mark["gcn_last_dve"] = nv[0]

            pe.wait_ge(s_gwt, 16)
            b = dve_bank()
            for k in range(KD):
                mm = pe.transpose(b[:, k * E2:(k + 1) * E2], gw[0:E2, k * P:(k + 1) * P], ident[0:E2, 0:E2])
            jg = to_dve(mm)
            jt = transpose_norm(3)
            pe.wait_ge(dve_done, jg)
            pe.wait_ge(act_done, jt)
            router(gT)
            pe.wait_ge(s_dw, 16 * 8)
            pe.wait_ge(s_dw2, 16)

            def expert_up(e):
                for c0, cw in CHUNKS:
                    b = act_bank()
                    for k in range(KD):
                        mm = pe.matmul(b[:, 0:cw], dW1[:, e, k, :], NTr[:, k, c0:c0 + cw],
                                       start=(k == 0), stop=(k == KD - 1))
                    j = to_act(mm)
                return j

            js = [expert_up(0), expert_up(1)]
            for f in range(SK):
                for c0, cw in CHUNKS:
                    b = act_bank()
                    for k in range(KD):
                        mm = pe.matmul(b[:, 0:cw], sW1[:, k, f * P:(f + 1) * P], NTr[:, k, c0:c0 + cw],
                                       start=(k == 0), stop=(k == KD - 1))
                    jsh = to_act(mm)
            pe.wait_ge(s_comb, 1)
            for t0 in range(0, NT, 4):
                b = dve_bank()
                for t in range(t0, min(t0 + 4, NT)):
                    mm = pe.transpose(b[0:E2, (t - t0) * P:(t - t0 + 1) * P], comb[:, t, :], ident[:, :])
                jc = to_dve(mm)
            for e in range(E2):
                pe.wait_ge(act_done, js[e])
                for t in range(NT):
                    r = rows(t)
                    b = dve_bank()
                    mm = pe.matmul(b[0:r, 0:D], hE[e % 2][:, t * P:t * P + r], dW2[:, e, :], start=True, stop=True)
                    to_dve(mm)
                mark["hE_used", e] = nv[0]
                if e + 2 < E2:
                    js.append(expert_up(e + 2))
            pe.wait_ge(act_done, jsh)
            pe.wait_ge(dve_done, jc)
            for t in range(NT):
                r = rows(t)
                b = dve_bank()
                for k in range(SK):
                    pe.matmul(b[0:r, 0:D], hS[:, k, t * P:t * P + r], sW2[:, k, :], start=(k == 0), stop=False)
                pe.matmul(b[0:r, 0:D], combT[0:E2, t * P:t * P + r], db2[0:E2, :], start=False, stop=False)
                mm = pe.matmul(b[0:r, 0:D], ones[0:1, 0:r], sb2[0:1, :], start=False, stop=True)
                to_dve(mm)

        @block.sync
        def _(sp):
            sp.wait_ge(s_pad, 1)
            sp.dma_start(X[:, 0:full, :], x[0:full * P, :].rearrange("(t p) d -> p t d", p=P)).then_inc(s_x, 16)
            sp.dma_start(X[0:tail, full, :], x[full * P:N, :]).then_inc(s_x, 16)
            sp.dma_start(wtr[:, :, 0, :], gat_wtrans[0:D, :].rearrange("(k p) d -> p k d", p=P)).then_inc(s_gw, 16)
            sp.dma_start(wtr[:, :, 1, :], gat_wtrans[D:2 * D, :].rearrange("(k p) d -> p k d", p=P)).then_inc(s_gw, 16)
            sp.wait_ge(s_pad, 3)
            for t in range(NT):
                r = rows(t)
                if t >= 2:
                    sp.wait_ge(s_scan, t - 1)
                    sp.wait_ge(act_full, mark["adjT", t - 2])
                sp.dma_start(adjn[t % 2][0:r, 0:N], adj[t * P:t * P + r, :]).then_inc(s_adj[t % 2], 16)
            sp.wait_ge(s_x1, 1)
            sp.dma_start(Wr[:, :, :], moe_Wr.rearrange("(k p) e -> p k e", p=P)).then_inc(s_wr, 16)
            sp.wait_ge(s_scat, 16 * 2 * NT)
            for s in range(2):
                if s:
                    sp.wait_ge(s_xt, s)
                sp.dma_start(xg[:, :], xs[s * P:(s + 1) * P, :]).then_inc(s_xg, 16)
            sp.wait_ge(s_xt, 2)
            sp.dma_start(xg[:, :], xs[2 * P:3 * P, :]).then_inc(s_xg, 16)
            sp.wait_ge(s_yd, 1)
            sp.dma_start(ys[0:P, :], yrow[:, :]).then_inc(s_yw, 16)
            with sp.Fori(1, SLOTS - 2) as s:
                sp.wait_ge(s_xt, s + 2)
                sp.dma_start(xg[:, :], xs[bass.ds(s * P + 2 * P, P), :]).then_inc(s_xg, 16)
                sp.wait_ge(s_yd, s + 1)
                sp.dma_start(ys[bass.ds(s * P, P), :], yrow[:, :]).then_inc(s_yw, 16)
            for s in (SLOTS - 2, SLOTS - 1):
                sp.wait_ge(s_yd, s + 1)
                sp.dma_start(ys[s * P:(s + 1) * P, :], yrow[:, :]).then_inc(s_yw, 16)
            sp.wait_ge(s_mix, 1)
            sp.dma_start(cW1[:, :, :], gcn_W1.rearrange("(k p) d -> p k d", p=P)).then_inc(s_cw, 16)
            sp.dma_start(cW2[:, :, :], gcn_W2.rearrange("(k p) d -> p k d", p=P)).then_inc(s_cw, 16)
            sp.dma_start(cW3[:, :, :], gcn_W3.rearrange("(k p) d -> p k d", p=P)).then_inc(s_cw, 16)
            with nc.allow_non_contiguous_dma(reason="bias columns"):
                sp.dma_start(cb1[:, :], gcn_b1.rearrange("(h p) -> p h", p=P)).then_inc(s_cw, 16)
                sp.dma_start(cb2[:, :], gcn_b2.rearrange("(h p) -> p h", p=P)).then_inc(s_cw, 16)
            sp.dma_start(cb3[:, :], gcn_b3.rearrange("(o d) -> o d", o=1).to_broadcast([P, D])).then_inc(s_cw, 16)
            sp.wait_ge(dve_done, mark["gcn_last_dve"])
            sp.dma_start(gw[:, :], ffn_gate).then_inc(s_gwt, 16)
            with nc.allow_non_contiguous_dma(reason="bias columns"):
                sp.dma_start(db1[:, :], ffn_b1.rearrange("e p -> p e")).then_inc(s_dw, 16)
                sp.dma_start(sb1[:, :], ffn_sb1.rearrange("(h p) -> p h", p=P)).then_inc(s_dw, 16)
            for k in range(KD):
                sp.dma_start(dW1[:, :, k, :], ffn_w1[:, k * P:(k + 1) * P, :].rearrange("e p f -> p e f")).then_inc(s_dw, 16)
            sp.dma_start(dW2[:, :, :], ffn_w2.rearrange("e f d -> f e d")).then_inc(s_dw, 16)
            sp.dma_start(db2[:, :], ffn_b2).then_inc(s_dw, 16)
            sp.dma_start(sW1[:, :, :], ffn_sw1.rearrange("(k p) d -> p k d", p=P)).then_inc(s_dw, 16)
            sp.dma_start(sW2[:, :, :], ffn_sw2.rearrange("(k p) d -> p k d", p=P)).then_inc(s_dw, 16)
            sp.dma_start(sb2[:, :], ffn_sb2.rearrange("(o d) -> o d", o=1)).then_inc(s_dw2, 16)
            sp.wait_ge(s_fin, 1)
            sp.dma_start(out[0:full * P, :].rearrange("(t p) d -> p t d", p=P), X[:, 0:full, :]).then_inc(s_out, 16)
            sp.dma_start(out[full * P:N, :], X[0:tail, full, :]).then_inc(s_out, 16)
            sp.wait_ge(s_out, 32)

        @block.gpsimd
        def _(pool):
            pool.memset(X[64:P, NT - 1, :], 0.0).then_inc(s_pad, 1)
            pool.wait_ge(s_pad, 1)
            pool.memset(adjn[0][:, N:NP], 0.0).then_inc(s_pad, 1)
            pool.memset(adjn[1][:, N:NP], 0.0).then_inc(s_pad, 1)
            pool.memset(ident[:, :], 0.0).then_inc(s_id, 1)
            pool.memset(ones[:, :], 1.0).then_inc(s_id, 1)
            pool.memset(valid[:, :], 1.0).then_inc(s_id, 1)
            pool.memset(neghalf[:, :], -0.5).then_inc(s_id, 1)
            pool.iota(rev[:, :], pattern=[[-1, E]], base=E, channel_multiplier=0,
                      allow_small_or_imprecise_dtypes=True).then_inc(s_id, 1)
            pool.wait_ge(s_id, 5)
            pool.affine_select(out=upper[:, :], in_=ones[:, :], compare_op=ALU.is_gt, fill=0.0,
                               base=0, pattern=[[1, P]], channel_multiplier=-1).then_inc(s_id, 1)
            pool.affine_select(out=valid[:, :], in_=valid[:, :], compare_op=ALU.is_gt, fill=0.0,
                               base=N, pattern=[[-P, NT]], channel_multiplier=-1).then_inc(s_id, 1)
            pool.memset(G[:, :, :, D:D + 2], 1.0).then_inc(s_id, 1)
            pool.wait_ge(s_id, 8)
            pool.affine_select(out=ident[:, :], in_=ident[:, :], compare_op=ALU.not_equal, fill=1.0,
                               base=0, pattern=[[-1, P]], channel_multiplier=1).then_inc(s_const, 1)
            pool.dma_start(gW[:, :, :], gat_W.rearrange("(k p) d -> p k d", p=P)).then_inc(s_gw2, 16)
            with nc.allow_non_contiguous_dma(reason="two vectors"):
                pool.dma_start(a2[:, :, :].rearrange("p w k -> p (w k)"), gat_a.rearrange("(c p) o -> p (c o)", p=P)).then_inc(s_gw2, 16)
            def deviation(k):
                pool.wait_ge(s_var, k)
                pool.tensor_tensor(rstd[:, :], rstd[:, :], neghalf[:, :], ALU.pow).then_inc(s_rstd, 1)

            deviation(1)
            pool.wait_ge(act_full, mark["adjT", NT - 1])
            pool.wait_ge(s_scan, NT)
            pool.wait_ge(dve_done, mark["mrow"])
            step = 0
            for t0, nt in GROUPS:
                c0 = t0 * P
                w = min(GW, N - c0)
                for j in range(NT):
                    if step >= 2:
                        pool.wait_ge(s_z, step - 1)
                    elif step == 0:
                        pool.wait_ge(act_done, mark["adjT", NT - 1])
                    pool.tensor_scalar(neg[:, 0:w], AT[:, j, c0:c0 + w], 0.0, -BIG,
                                       ALU.is_le, ALU.mult).then_inc(s_neg0, 1)
                    pool.wait_ge(s_neg0, step + 1)
                    for s in range(2):
                        pool.tensor_tensor(nm[step % 2][:, s, 0:w], neg[:, 0:w], mrow[s][:, c0:c0 + w],
                                           ALU.subtract).then_inc(s_neg, 1)
                        pool.wait_ge(s_neg, 2 * step + s + 1)
                    step += 1
            pool.wait_ge(s_x1, 1)
            pool.memset(zero[:, :], 0.0).then_inc(s_zero, 1)
            pool.iota(kval[:, :], pattern=[[P, NT]], base=0, channel_multiplier=0,
                      allow_small_or_imprecise_dtypes=True).then_inc(s_zero, 1)
            pool.iota(sval[:, :], pattern=[[1, SLOTS]], base=0, channel_multiplier=0,
                      allow_small_or_imprecise_dtypes=True).then_inc(s_zero, 1)
            pool.wait_ge(s_zero, 3)
            pool.dma_start(xs.rearrange("(s p) d -> p s d", p=P),
                           zero[:, :].unsqueeze(1).to_broadcast([P, SLOTS, D])).then_inc(s_xsz, 16)

            def load_expert(e):
                pool.dma_start(W1b[:, e % 2, :].rearrange("p (k f) -> p k f", k=KD),
                               moe_W1[e, :, :].rearrange("(k p) f -> p k f", p=P)).then_inc(s_we[e % 2], 16)
                pool.dma_start(W2b[:, e % 2, :].rearrange("p (k f) -> p k f", k=FK),
                               moe_W2[e, :, :].rearrange("(k p) f -> p k f", p=P)).then_inc(s_we[e % 2], 16)

            load_expert(0)
            load_expert(1)
            deviation(2)
            pool.wait_ge(s_xsz, 16)
            pool.wait_ge(s_route, 1)
            for t in range(NT):
                r = rows(t)
                for c in range(2):
                    pool.indirect_dma_start(out=xs, out_offset=bass.IndirectOffsetOnAxis(ap=posI[0:r, c, t:t + 1], axis=0),
                                            in_=Nn[0:r, t, :], in_offset=None).then_inc(s_scat, 16)
            for e in range(E):
                pool.wait_ge(s_we[e % 2], 32 * (e // 2 + 1))
                pool.sem_inc(s_wrdy, 1)
                if 1 <= e < E - 1:
                    upto = pool.value_load(cumI[0:1, e:e + 1], min_val=1, max_val=SLOTS)
                    pool.wait_ge(s_y, upto)
                    pool.sem_inc(s_wfree, 1)
                    load_expert(e + 1)
            pool.wait_ge(s_yw, 16 * SLOTS)
            for t in range(NT):
                r = rows(t)
                for c in range(2):
                    pool.indirect_dma_start(out=yg[0:r, c, t, :], out_offset=None, in_=ys,
                                            in_offset=bass.IndirectOffsetOnAxis(ap=posI[0:r, c, t:t + 1], axis=0)
                                            ).then_inc(s_yg, 16)
            deviation(3)
            deviation(4)

        @block.scalar
        def _(act):
            n = [0]

            def bank():
                act.wait_ge(act_full, n[0] + 1)
                b = act_banks[n[0] % 4]
                n[0] += 1
                return b

            def transpose_norm():
                for q in range(-(-NT // 2)):
                    w = min(2, NT - 2 * q)
                    b = bank()
                    act.activation(NTr[:, :, 2 * q * P:(2 * q + w) * P],
                                   b[:, :].rearrange("p (k n) -> p k n", k=KD)[:, :, 0:w * P],
                                   ACT.Copy).then_inc(act_done, 1)

            b = bank()
            act.activation(gWT[:, :, :], b[:, :].rearrange("p (k n) -> p k n", k=KD), ACT.Copy).then_inc(act_done, 1)
            transpose_norm()
            for w in (1, 0):
                for c0, cw in CHUNKS:
                    b = bank()
                    act.activation(Wrow[w][:, c0:c0 + cw], b[:, 0:cw], ACT.Copy).then_inc(act_done, 1)
            for t in range(NT):
                r = rows(t)
                for j0 in range(0, NT, 4):
                    nj = min(4, NT - j0)
                    b = bank()
                    act.activation(AT[:, j0:j0 + nj, t * P:t * P + r],
                                   b[:, 0:nj * P].rearrange("p (j i) -> p j i", i=P)[:, :, 0:r],
                                   ACT.Copy).then_inc(act_done, 1)
            act.wait_ge(s_const, 1)
            for t in range(NT):
                r = rows(t)
                b = bank()
                act.activation(G[0:r, t, :, 0:D], b[0:r, :].rearrange("p (s d) -> p s d", s=2),
                               ACT.Copy).then_inc(act_done, 1)
            act.wait_ge(dve_done, mark["Wh"])
            act.wait_ge(s_scan, NT)
            steps = [(t0, nt, j) for t0, nt in GROUPS for j in range(NT)]

            def exp_step(i):
                t0, nt, _ = steps[i]
                w = min(GW, N - t0 * P)
                act.wait_ge(s_z, i + 1)
                if i >= 2:
                    act.wait_ge(s_used, i - 1)
                act.activation(pp[(i + 1) % 2][:, :, 0:w], zz[i % 2][:, :, 0:w], ACT.Exp).then_inc(s_p, 1)

            def elu_exp(g):
                t0, nt = GROUPS[g]
                act.wait_ge(s_vm, g + 1)
                act.activation(Vm[:, t0:t0 + nt, :], Vm[:, t0:t0 + nt, :], ACT.Exp).then_inc(s_ve, 1)

            for i, (t0, nt, j) in enumerate(steps):
                w = min(GW, N - t0 * P)
                if i >= 2:
                    act.wait_ge(s_z, i - 1)
                act.activation(ss[i % 2][:, 0:w], Wrow[0][:, t0 * P:t0 * P + w], ACT.Identity,
                               bias=Wh[:, j, 1:2]).then_inc(s_t, 1)
                if i:
                    exp_step(i - 1)
                if j == 2 and t0:
                    elu_exp(i // NT - 1)
            exp_step(len(steps) - 1)
            elu_exp(len(GROUPS) - 1)
            transpose_norm()
            act.wait_ge(s_lc, 1)
            act.activation(probs[:, :, :], logits[:, :, :], ACT.Exp).then_inc(s_le, 1)

            def gelu(s):
                for h in range(2):
                    act.wait_ge(s_h, 2 * s + h + 1)
                    act.activation(hn[:, h * PSB:(h + 1) * PSB], banks[1 + h][:, :], ACT.Gelu).then_inc(s_hd, 1)

            def copy_rows_T(s):
                act.wait_ge(s_xt, s + 1)
                act.activation(xgT[:, :, :], banks[0][:, 0:KD * P].rearrange("p (k n) -> p k n", k=KD),
                               ACT.Copy).then_inc(s_xtd, 1)

            copy_rows_T(0)
            gelu(0)
            copy_rows_T(1)
            with act.Fori(1, SLOTS - 1) as s:
                gelu(s)
                copy_rows_T(s + 1)
            gelu(SLOTS - 1)
            for c0, cw in CHUNKS:
                for f in range(KD):
                    b = bank()
                    act.activation(Z1T[:, f, c0:c0 + cw], b[:, 0:cw], ACT.Copy).then_inc(act_done, 1)
            for HT_, bias in ((H1T, cb1), (H2T, cb2)):
                for c0, cw in CHUNKS:
                    for h in range(HK):
                        b = bank()
                        act.activation(HT_[:, h, c0:c0 + cw], b[:, 0:cw], ACT.Relu,
                                       bias=bias[:, h:h + 1]).then_inc(act_done, 1)
            transpose_norm()

            def hidden(dst, bias):
                for c0, cw in CHUNKS:
                    b = bank()
                    act.activation(dst[:, c0:c0 + cw], b[:, 0:cw], ACT.Relu, bias=bias).then_inc(act_done, 1)

            act.wait_ge(s_lc, 2)
            act.activation(probs[:, :, :], logits[:, :, :], ACT.Exp).then_inc(s_le, 1)
            act.wait_ge(s_dw, 16 * 8)
            hidden(hE[0], db1[:, 0:1])
            hidden(hE[1], db1[:, 1:2])
            for f in range(SK):
                hidden(hS[:, f, :], sb1[:, f:f + 1])
            for e in range(2, E2):
                act.wait_ge(dve_full, mark["hE_used", e - 2])
                hidden(hE[e % 2], db1[:, e:e + 1])

        @block.vector
        def _(dve):
            n = [0]
            links = [0]
            lns = [0]

            def bank():
                dve.wait_ge(dve_full, n[0] + 1)
                b = dve_banks[n[0] % 4]
                n[0] += 1
                return b

            def link(ins):
                links[0] += 1
                ins.then_inc(chain, 1)

            def settle():
                dve.wait_ge(chain, links[0])

            def layer_norm():
                for t in range(NT):
                    link(dve.bn_stats(stats[:, t, :], X[:, t, :]))
                settle()
                for t in range(NT):
                    link(dve.bn_aggr(mv[:, t, :], stats[:, t, :]))
                settle()
                lns[0] += 1
                dve.tensor_scalar(rstd[:, :], mv[:, :, 1], EPS, None, ALU.add).then_inc(s_var, 1)
                dve.wait_ge(s_rstd, lns[0])
                for t in range(NT):
                    dve.tensor_scalar(Nn[:, t, :], X[:, t, :], mv[:, t, 0:1], rstd[:, t:t + 1],
                                      ALU.subtract, ALU.mult).then_inc(s_norm, 1)

            def over_e(ap):
                return ap.unsqueeze(2).to_broadcast([P, NT, E])

            revb = rev[:, :].unsqueeze(1).to_broadcast([P, NT, E])

            def top2(k):
                b = bank()
                src = b[:, 0:NT * E].rearrange("p (t e) -> p t e", e=E)
                link(dve.memset(logits[:, NT - 1, :], 0.0))
                settle()
                link(dve.tensor_copy(logits[0:tail, NT - 1, :], src[0:tail, NT - 1, :]))
                dve.tensor_copy(logits[:, 0:NT - 1, :], src[:, 0:NT - 1, :]).then_inc(dve_done, 1)
                settle()
                dve.wait_ge(dve_done, n[0])
                link(dve.tensor_reduce(rtmp[:, :], logits[:, :, :], AX, ALU.max))
                settle()
                dve.tensor_tensor(logits[:, :, :], logits[:, :, :], over_e(rtmp[:, :]), ALU.subtract).then_inc(s_lc, 1)
                dve.wait_ge(s_le, k)
                link(dve.tensor_reduce(rtmp[:, :], probs[:, :, :], AX, ALU.add))
                settle()
                link(dve.reciprocal(rtmp[:, :], rtmp[:, :]))
                settle()
                link(dve.tensor_tensor(probs[:, :, :], probs[:, :, :], over_e(rtmp[:, :]), ALU.mult))
                src_p = probs
                for p, oh in ((p1, oh1), (p2, oh2)):
                    settle()
                    link(dve.tensor_reduce(p[:, :], src_p[:, :, :], AX, ALU.max))
                    settle()
                    link(dve.tensor_tensor(eq[:, :, :], src_p[:, :, :], over_e(p[:, :]), ALU.is_equal))
                    settle()
                    link(dve.tensor_tensor(eq[:, :, :], eq[:, :, :], revb, ALU.mult))
                    settle()
                    link(dve.tensor_reduce(rtmp[:, :], eq[:, :, :], AX, ALU.max))
                    settle()
                    link(dve.tensor_tensor(oh[:, :, :], revb, over_e(rtmp[:, :]), ALU.is_equal))
                    settle()
                    if oh is oh1:
                        link(dve.scalar_tensor_tensor(probs2[:, :, :], oh1[:, :, :], -2.0, probs[:, :, :],
                                                      ALU.mult, ALU.add))
                        src_p = probs2

            dve.wait_ge(s_x, 32)
            layer_norm()
            b = bank()
            dve.tensor_copy(Wa[:, :, :], b[:, 0:2 * KD].rearrange("p (k w) -> p k w", w=2)).then_inc(dve_done, 1)
            dve.wait_ge(dve_done, n[0])
            dve.wait_ge(s_const, 1)
            for w in range(2):
                for k in range(KD):
                    dve.tensor_scalar(WaB[:, w, k, :], ones[:, :], Wa[:, k, w:w + 1], None,
                                      ALU.mult).then_inc(s_wab, 1)
            b = bank()
            src = b[:, 0:2 * NT].rearrange("p (t w) -> p t w", w=2)
            link(dve.memset(Wh[:, NT - 1, :], 0.0))
            link(dve.memset(mx[:, :, :], 0.0))
            settle()
            link(dve.tensor_copy(Wh[0:tail, NT - 1, :], src[0:tail, NT - 1, :]))
            dve.tensor_copy(Wh[:, 0:NT - 1, :], src[:, 0:NT - 1, :]).then_inc(dve_done, 1)
            settle()
            dve.wait_ge(dve_done, n[0])
            dve.wait_ge(act_done, mark["row", 1])
            for t in range(NT):
                r = rows(t)
                dve.wait_ge(s_adj[t % 2], 16 * (t // 2 + 1))
                link(dve.tensor_scalar(negn[0:r, :], adjn[t % 2][0:r, 0:N], 0.0, -BIG, ALU.is_le, ALU.mult))
                settle()
                link(dve.tensor_tensor_reduce(out=junk[0:r, :], in0=negn[0:r, :], in1=Wrow[1][0:r, :], scale=1.0,
                                              scalar=-2 * BIG, op0=ALU.add, op1=ALU.max, accum_out=mx[0:r, 0, t:t + 1]))
                settle()
                dve.tensor_tensor_reduce(out=junk[0:r, :], in0=negn[0:r, :], in1=Wrow[1][0:r, :], scale=1.0,
                                         scalar=-2 * BIG, op0=ALU.subtract, op1=ALU.max,
                                         accum_out=mx[0:r, 1, t:t + 1]).then_inc(s_scan, 1)
                dve.wait_ge(s_scan, t + 1)
            link(dve.tensor_tensor(ms[:, 0, :], Wh[:, :, 0], mx[:, 0, :], ALU.add))
            link(dve.tensor_tensor(ms[:, 1, :], Wh[:, :, 0], mx[:, 1, :], ALU.subtract))
            settle()
            link(dve.scalar_tensor_tensor(m2[:, :, :], ms[:, :, :], ALPHA, ms[:, :, :], ALU.mult, ALU.max))
            settle()
            link(dve.tensor_scalar(m2[:, 1, :], m2[:, 1, :], -1.0, None, ALU.mult))
            link(dve.tensor_reduce(nsum[:, :], NTr[:, :, :], AX, ALU.add))
            settle()
            link(dve.tensor_scalar(nsumB[:, 0, :], ones[:, :], nsum[:, 0:1], None, ALU.mult))
            settle()
            dve.tensor_scalar(nsumB[:, 1, :], ones[:, :], nsum[:, 1:2], None, ALU.mult).then_inc(s_nsum, 1)
            b = bank()
            dve.tensor_copy(Cs[:, :, :], b[:, :].rearrange("p (s d) -> p s d", s=2)).then_inc(dve_done, 1)
            at = [0]

            def spread_m(s, t0):
                for t in range(t0, min(t0 + 4, NT)):
                    dve.tensor_scalar(mB[:, MROWS[at[0]][2], :], ones[:, :], m2[:, s, t:t + 1], None,
                                      ALU.mult).then_inc(s_mB, 1)
                    at[0] += 1

            turns = [(s, t0) for s in range(2) for t0 in range(0, NT, 4)]
            spread_m(*turns[0])
            for i, (s, t0) in enumerate(turns):
                if i + 1 < len(turns):
                    spread_m(*turns[i + 1])
                b = bank()
                w = min(4 * P, N - t0 * P)
                dve.tensor_copy(mrow[s][:, t0 * P:t0 * P + w], b[:, 0:w]).then_inc(dve_done, 1)
            dve.wait_ge(dve_done, n[0])
            i = 0
            for g, (t0, nt) in enumerate(GROUPS):
                c0 = t0 * P
                w = min(GW, N - c0)
                for j in range(NT):
                    r2 = i % 2
                    dve.wait_ge(s_t, i + 1)
                    dve.wait_ge(s_neg, 2 * i + 2)
                    dve.wait_ge(s_z, i) if i else None
                    if i >= 2:
                        dve.wait_ge(s_p, i - 1)
                    link(dve.scalar_tensor_tensor(leaky[:, 0:w], ss[r2][:, 0:w], ALPHA, ss[r2][:, 0:w],
                                                  ALU.mult, ALU.max))
                    settle()
                    link(dve.tensor_tensor(zz[r2][:, 0, 0:w], nm[r2][:, 0, 0:w], leaky[:, 0:w], ALU.add))
                    dve.tensor_tensor(zz[r2][:, 1, 0:w], nm[r2][:, 1, 0:w], leaky[:, 0:w],
                                      ALU.subtract).then_inc(s_z, 1)
                    i += 1
                dve.wait_ge(s_used, i)
                for q in range(nt):
                    r = rows(t0 + q)
                    for s in range(2):
                        src = banks[2 * q + s]
                        link(dve.tensor_scalar(emp[0:r, s:s + 1], src[0:r, D:D + 1], 0.5, None, ALU.is_lt))
                        settle()
                        link(dve.scalar_tensor_tensor(den[0:r, s:s + 1], emp[0:r, s:s + 1], float(N),
                                                      src[0:r, D:D + 1], ALU.mult, ALU.add))
                        sums = dve.scalar_tensor_tensor(T1[0:r, s, :], Cs[0:r, s, :], emp[0:r, s:s + 1],
                                                        src[0:r, 0:D], ALU.mult, ALU.add)
                        if q == nt - 1 and s == 1:
                            sums.then_inc(s_attd, 1)
                            dve.wait_ge(s_attd, g + 1)
                        else:
                            link(sums)
                    settle()
                    link(dve.reciprocal(den[0:r, :], den[0:r, :]))
                    if r < P:
                        link(dve.memset(V[:, q, :], 0.0))
                    settle()
                    link(dve.tensor_scalar(T1[0:r, 0, :], T1[0:r, 0, :], den[0:r, 0:1], None, ALU.mult))
                    link(dve.tensor_scalar(den[0:r, 1:2], den[0:r, 1:2], -1.0, None, ALU.mult))
                    settle()
                    link(dve.scalar_tensor_tensor(V[0:r, q, :], T1[0:r, 1, :], den[0:r, 1:2], T1[0:r, 0, :],
                                                  ALU.mult, ALU.add))
                    settle()
                dve.tensor_scalar(Vm[:, t0:t0 + nt, :], V[:, 0:nt, :], 0.0, None, ALU.min).then_inc(s_vm, 1)
                link(dve.tensor_scalar(V2[:, 0:nt, :], V[:, 0:nt, :], 0.0, -1.0, ALU.max, ALU.add))
                settle()
                link(dve.tensor_tensor(X[:, t0:t0 + nt, :], X[:, t0:t0 + nt, :], V2[:, 0:nt, :], ALU.add))
            settle()
            dve.wait_ge(s_ve, len(GROUPS))
            dve.tensor_tensor(X[:, :, :], X[:, :, :], Vm[:, :, :], ALU.add).then_inc(s_x1, 1)
            dve.wait_ge(s_x1, 1)

            layer_norm()
            top2(1)
            settle()
            validb = over_e(valid[:, :])
            link(dve.tensor_tensor(Msel[:, :, :], oh1[:, :, :], oh2[:, :, :], ALU.add))
            link(dve.memset(Mpre[:, 0, :], 0.0))
            settle()
            link(dve.tensor_tensor(Msel[:, :, :], Msel[:, :, :], validb, ALU.mult))
            for t in range(NT):
                settle()
                pre = dve.tensor_tensor(Mpre[:, t + 1, :], Mpre[:, t, :], Msel[:, t, :], ALU.add)
                if t == NT - 1:
                    pre.then_inc(s_msel, 1)
                else:
                    link(pre)
            b = bank()
            dve.tensor_copy(rank[:, :, :], b[:, 0:(NT + 1) * E].rearrange("p (t e) -> p t e", e=E)).then_inc(dve_done, 1)
            dve.wait_ge(dve_done, n[0])
            dve.wait_ge(s_zero, 3)
            link(dve.tensor_tensor(cmpk[:, :, :], rank[:, NT, :].unsqueeze(2).to_broadcast([P, E, NT]),
                                   kval[:, :].unsqueeze(1).to_broadcast([P, E, NT]), ALU.is_gt))
            link(dve.memset(cum[:, 0:1], 0.0))
            settle()
            link(dve.tensor_reduce(cnt[:, :], cmpk[:, :, :], AX, ALU.add))
            settle()
            link(dve.tensor_scalar(cnt[:, :], cnt[:, :], 1.0, None, ALU.max))
            for e in range(E):
                settle()
                link(dve.tensor_tensor(cum[:, e + 1:e + 2], cum[:, e:e + 1], cnt[:, e:e + 1], ALU.add))
            settle()
            link(dve.tensor_copy(cumI[:, :], cum[:, :]))
            link(dve.tensor_tensor(sexp[:, :, :], cum[:, 1:E + 1].unsqueeze(1).to_broadcast([P, SLOTS, E]),
                                   sval[:, :].unsqueeze(2).to_broadcast([P, SLOTS, E]), ALU.is_le))
            link(dve.scalar_tensor_tensor(posf[:, :, :], cum[:, 0:E].unsqueeze(1).to_broadcast([P, NT, E]), float(P),
                                          rank[:, 0:NT, :], ALU.mult, ALU.add))
            settle()
            link(dve.tensor_reduce(slot_e[:, :], sexp[:, :, 0:E - 1], AX, ALU.add))
            link(dve.tensor_reduce(slot_p[:, :], sexp[:, :, 0:E - 1:2], AX, ALU.add))
            link(dve.tensor_reduce(slot_q[:, :], sexp[:, :, 1:E - 1:2], AX, ALU.add))
            link(dve.tensor_tensor(eq[:, :, :], posf[:, :, :], oh1[:, :, :], ALU.mult))
            link(dve.tensor_tensor(probs2[:, :, :], posf[:, :, :], oh2[:, :, :], ALU.mult))
            settle()
            link(dve.tensor_tensor(slot_p[:, :], slot_p[:, :], slot_q[:, :], ALU.subtract))
            link(dve.tensor_reduce(pos[:, 0, :], eq[:, :, :], AX, ALU.add))
            link(dve.tensor_reduce(pos[:, 1, :], probs2[:, :, :], AX, ALU.add))
            settle()
            link(dve.tensor_scalar(slot_eI[:, :], slot_e[:, :], 1.0, None, ALU.add))
            link(dve.tensor_copy(posI[:, :, :], pos[:, :, :]))
            settle()
            dve.tensor_copy(slot_pI[:, :], slot_p[:, :]).then_inc(s_route, 1)

            def slot(s, first=False):
                for h in range(2):
                    dve.wait_ge(s_ht, 2 * s + h + 1)
                    dve.tensor_copy(hT[:, 4 * h:4 * h + 4, :],
                                    banks[3 + h][:, :].rearrange("p (f n) -> p f n", n=P)).then_inc(s_htd, 1)
                if not first:
                    dve.wait_ge(s_yw, 16 * s)
                dve.wait_ge(s_y, s + 1)
                dve.tensor_copy(yrow[:, :], banks[5][:, 0:D]).then_inc(s_yd, 1)

            slot(0, True)
            with dve.Fori(1, SLOTS) as s:
                slot(s)
            dve.wait_ge(s_yg, 16 * 2 * NT)
            for c, p in ((0, p1), (1, p2)):
                for t in range(NT):
                    r = rows(t)
                    mix = dve.scalar_tensor_tensor(X[0:r, t, :], yg[0:r, c, t, :], p[0:r, t:t + 1], X[0:r, t, :],
                                                   ALU.mult, ALU.add)
                    if c and t == NT - 1:
                        mix.then_inc(s_mix, 1)
                        dve.wait_ge(s_mix, 1)
                    else:
                        link(mix)
                settle()

            layer_norm()
            dve.wait_ge(s_norm, 3 * NT)
            dve.wait_ge(s_cw, 16 * 6)
            link(dve.tensor_tensor(X[:, :, :], X[:, :, :], cb3[:, :].unsqueeze(1).to_broadcast([P, NT, D]), ALU.add))
            for Y, w in ((Y2, HID), (Y3, D)):
                for t in range(NT):
                    r = rows(t)
                    b = bank()
                    dve.tensor_copy(Y[0:r, t, :], b[0:r, 0:w]).then_inc(dve_done, 1)
            settle()
            for t in range(NT):
                r = rows(t)
                b = bank()
                dve.tensor_tensor(X[0:r, t, :], b[0:r, 0:D], X[0:r, t, :], ALU.add).then_inc(dve_done, 1)
            dve.wait_ge(dve_done, n[0])

            layer_norm()
            b = bank()
            dve.tensor_copy(gT[:, :, :], b[:, 0:KD * E2].rearrange("p (k e) -> p k e", e=E2)).then_inc(dve_done, 1)
            top2(2)
            settle()
            link(dve.tensor_tensor(rtmp[:, :], p1[:, :], p2[:, :], ALU.add))
            link(dve.tensor_tensor(oh1[:, :, :], oh1[:, :, :], over_e(p1[:, :]), ALU.mult))
            link(dve.tensor_tensor(oh2[:, :, :], oh2[:, :, :], over_e(p2[:, :]), ALU.mult))
            settle()
            link(dve.tensor_scalar(rtmp[:, :], rtmp[:, :], 1e-20, None, ALU.add))
            link(dve.tensor_tensor(oh1[:, :, :], oh1[:, :, :], oh2[:, :, :], ALU.add))
            settle()
            link(dve.reciprocal(rtmp[:, :], rtmp[:, :]))
            settle()
            dve.tensor_tensor(comb[:, :, :], oh1[:, :, :], over_e(rtmp[:, :]), ALU.mult).then_inc(s_comb, 1)
            dve.wait_ge(s_comb, 1)
            for t0 in range(0, NT, 4):
                w = min(4, NT - t0) * P
                b = bank()
                dve.tensor_copy(combT[:, t0 * P:t0 * P + w], b[0:E2, 0:w]).then_inc(dve_done, 1)
            for e in range(E2):
                for t in range(NT):
                    r = rows(t)
                    if e:
                        dve.wait_ge(dve_done, n[0] - NT + 1)
                    b = bank()
                    dve.scalar_tensor_tensor(X[0:r, t, :], b[0:r, 0:D], comb[0:r, t, e:e + 1], X[0:r, t, :],
                                             ALU.mult, ALU.add).then_inc(dve_done, 1)
            for t in range(NT):
                r = rows(t)
                dve.wait_ge(dve_done, n[0] - NT + 1)
                b = bank()
                last = dve.tensor_tensor(X[0:r, t, :], b[0:r, 0:D], X[0:r, t, :], ALU.add)
                last.then_inc(dve_done if t < NT - 1 else s_fin, 1)


_INS = ['x', 'adj', 'L0_gnn_W', 'L0_gnn_a', 'L0_gnn_wtrans', 'L0_ffn_Wr', 'L0_ffn_W1', 'L0_ffn_W2', 'L1_gnn_W1',
        'L1_gnn_b1', 'L1_gnn_W2', 'L1_gnn_b2', 'L1_gnn_W3', 'L1_gnn_b3', 'L1_ffn_gate_w', 'L1_ffn_w1', 'L1_ffn_b1',
        'L1_ffn_w2', 'L1_ffn_b2', 'L1_ffn_sw1', 'L1_ffn_sb1', 'L1_ffn_sw2', 'L1_ffn_sb2']


def kernel(**inputs):
    import numpy as _np
    import concourse.bacc as _bacc
    from concourse import mybir as _mybir
    from concourse.bass_utils import run_bass_kernel_spmd as _run

    nc = _bacc.Bacc("TRN2", target_bir_lowering=False, num_devices=1)
    arrays, args = {}, []
    for name in _INS:
        a = _np.ascontiguousarray(inputs[name])
        arrays[f"in_{name}_dram"] = a
        args.append(nc.dram_tensor(f"in_{name}_dram", a.shape, _mybir.dt.from_np(a.dtype), kind="ExternalInput").ap())
    shape = inputs['x'].shape
    args.append(nc.dram_tensor("out_dram", shape, _mybir.dt.float32, kind="ExternalOutput").ap())
    gat_moe_gcn_moe_kernel(nc, *args)
    r = _run(nc, [arrays], core_ids=[0])
    return r.results[0]["out_dram"]
```

```python
import concourse.bass as bass
from concourse import mybir
from contextlib import ExitStack

F32 = mybir.dt.float32
F32R = mybir.dt.float32r
I32 = mybir.dt.int32
U32 = mybir.dt.uint32
ALU = mybir.AluOpType
ACT = mybir.ActivationFunctionType
AX = mybir.AxisListType.X


def gat_moe_gcn_moe_kernel(nc, x, adj, gat_W, gat_a, gat_wtrans, moe_Wr, moe_W1, moe_W2,
                           gcn_W1, gcn_b1, gcn_W2, gcn_b2, gcn_W3, gcn_b3,
                           ffn_gate, ffn_w1, ffn_b1, ffn_w2, ffn_b2, ffn_sw1, ffn_sb1, ffn_sw2, ffn_sb2, out):
    P = 128
    N, D = x.shape
    NT = -(-N // P)
    NP = NT * P
    KD = D // P
    E, _, F = moe_W1.shape
    FK = F // P
    HID = gcn_W1.shape[1]
    HK = HID // P
    E2, _, DF = ffn_w1.shape
    SH = ffn_sw1.shape[1]
    SK = SH // P
    EPS = 1e-5
    BIG = 1e30
    ALPHA = 0.2
    RING = 3
    NC = 3
    CW = -(-N // NC)
    CW += CW % 2
    CHUNKS = [(c * CW, min(CW, N - c * CW)) for c in range(NC)]
    GROUPS = [(0, 3), (3, 3), (6, 3), (9, 2)]
    GW = 3 * P
    SLOTS = (2 * N + E * (P - 1)) // P
    PSB = 512
    full = N // P
    tail = N - full * P

    def rows(t):
        return min(P, N - t * P)

    xs = nc.dram_tensor("routed_rows", ((SLOTS + 1) * P, D), F32).ap()
    at_dram = nc.dram_tensor("adj_transposed", (P, NT, N), F32).ap()
    ys = nc.dram_tensor("expert_rows", (SLOTS * P, D), F32).ap()

    ctx = ExitStack()
    with ctx:
        def sb(name, shape, dt=F32):
            return ctx.enter_context(nc.sbuf_tensor(name, shape, dt))

        def sem(name):
            return ctx.enter_context(nc.semaphore(name))

        X = sb("X", [P, NT, D])
        Nn_at = -(-nc.sbuf_base // 32) * 32
        Nn = sb("Nn", [P, NT, D])
        NTr_at = Nn_at + 4 * NT * D
        NTr = sb("NTr", [P, KD, NP])
        assert nc.sbuf_base >= NTr_at + 4 * KD * NP
        ident = sb("ident", [P, P])
        ones = sb("ones", [P, P])
        upper = sb("upper", [P, P])
        stats = sb("stats", [P, NT, 6])
        mv = sb("mv", [P, NT, 2])
        rstd = sb("rstd", [P, NT])
        neghalf = sb("neghalf", [P, NT])
        logits = sb("logits", [P, NT, E])
        probs = sb("probs", [P, NT, E])
        eq = sb("eq", [P, NT, E])
        oh1 = sb("oh1", [P, NT, E])
        oh2 = sb("oh2", [P, NT, E])
        probs2 = sb("probs2", [P, NT, E])
        rtmp = sb("rtmp", [P, NT])
        p1 = sb("p1", [P, NT])
        p2 = sb("p2", [P, NT])
        Wr = sb("Wr", [P, KD, E])
        rev = sb("rev", [P, E])
        lowsum = sb("lowsum", [P, 1])
        wideI = sb("wideI", [P, 1], I32)
        valid = sb("valid", [P, NT])
        arena = nc.sbuf_base
        arena = -(-arena // 64) * 64
        AT = nc.alloc_sbuf_tensor_at("AT", [P, NT, N], F32, offset=arena)
        ATr = nc.alloc_sbuf_tensor_at("ATr", [P, NT, N], F32R, offset=arena)
        arena += -(-4 * NT * N // 64) * 64

        class Place:
            def __init__(self, at):
                self.at = at

            def __call__(self, name, shape, dt=F32):
                n = 4
                for s in shape[1:]:
                    n *= s
                t = nc.alloc_sbuf_tensor_at(name, shape, dt, offset=self.at)
                self.at += -(-n // 32) * 32
                return t

        pl = Place(arena)
        adjn = [pl(f"adjn{i}", [P, NP]) for i in range(RING)]
        negn = pl("negn", [P, N])
        junk = pl("junk", [P, N], mybir.dt.bfloat16)
        scan_end = pl.at
        gW = pl("gW", [P, KD, D])
        gWT = pl("gWT", [P, KD, D])
        a2 = pl("a2", [P, 2, KD])
        wtr = pl("wtr", [P, KD, 2, D])
        Wa = pl("Wa", [P, KD, 2])
        Wh = pl("Wh", [P, NT, 2])
        Wrow = pl("Wrow", [P, N])
        mx = pl("mx", [P, 2, NT])
        ms = pl("ms", [P, 2, NT])
        m2 = pl("m2", [P, 2, NT])
        has = pl("has", [P, 2, NT])
        qcol = pl("qcol", [P, 4, NT])
        kcol = pl("kcol", [P, 4, NT])
        after_scan = Place(pl.at)
        pa = Place(arena)
        ee = [pa(f"ee{i}", [P, 4, GW]) for i in range(2)]
        mask = pa("mask", [P, GW])
        qq = pa("qq", [P, 2, GW])
        pp = [pa(f"pp{i}", [P, 2, GW]) for i in range(2)]
        assert pa.at <= scan_end
        G = after_scan("G", [P, NT, 2, D + 2])
        qrow = after_scan("qrow", [P, 4, N])
        Cs = after_scan("Cs", [P, 2, D])
        den = after_scan("den", [P, 3, 2])
        emp = after_scan("emp", [P, 3, 2])
        V = after_scan("V", [P, 3, D])
        zero = after_scan("zero", [P, D])
        V2 = after_scan("V2", [P, 3, D])
        Vm = after_scan("Vm", [P, NT, D])

        pb = Place(arena)
        W1b = pb("W1b", [P, 2, KD * F])
        W2b = pb("W2b", [P, 2, FK * D])
        Msel = pb("Msel", [P, NT, E])
        Mpre = pb("Mpre", [P, NT + 1, E])
        rank = pb("rank", [P, NT + 1, E])
        kval = pb("kval", [P, NT])
        cmpk = pb("cmpk", [P, E, NT])
        cnt = pb("cnt", [P, E])
        cum = pb("cum", [P, E + 1])
        cumI = pb("cumI", [P, E + 1], I32)
        lastf = pb("lastf", [P, E])
        lastI = pb("lastI", [P, E], I32)
        posf = pb("posf", [P, NT, E])
        pos = pb("pos", [P, 2, NT])
        posI = pb("posI", [P, 2, NT], I32)
        lowmax = pb("lowmax", [P, NT])
        xg = pb("xg", [P, D])
        xgT = pb("xgT", [P, KD, P])
        hT = pb("hT", [P, FK, P])
        yrow = pb("yrow", [P, D])
        lowbits = nc.alloc_sbuf_tensor_at("lowbits", [P, 2, N], U32, offset=pb.at)
        yg = pb("yg", [P, 2, NT, D])

        pc = Place(arena)
        cW2 = pc("cW2", [P, 2, HK, HID], F32R)
        cW3 = pc("cW3", [P, 2, HK, D], F32R)
        cb1 = pc("cb1", [P, HK])
        cb2 = pc("cb2", [P, HK])
        cb3 = pc("cb3", [P, D])
        first, second = pc.at, pc.at + 4 * 2 * NT * HID
        Z1T = pc("Z1T", [P, 2, KD, N], F32R)
        raw1 = pc("raw1", [P, KD, HID])
        raw2 = pc("raw2", [P, HK, HID])
        raw3 = pc("raw3", [P, HK, D])
        assert pc.at <= second
        Y2 = nc.alloc_sbuf_tensor_at("Y2", [P, 2, NT, HID], F32R, offset=first)
        Y3 = nc.alloc_sbuf_tensor_at("Y3", [P, 2, NT, D], F32R, offset=first)
        pc.at = second
        H1T = pc("H1T", [P, 2, HK, N], F32R)
        H2T = nc.alloc_sbuf_tensor_at("H2T", [P, 2, HK, N], F32R, offset=second)
        Np = nc.alloc_sbuf_tensor_at("Np", [P, 2, NT, D], F32R, offset=second)
        cW1 = nc.alloc_sbuf_tensor_at("cW1", [P, 2, KD, HID], F32R, offset=NTr_at)
        hh = [nc.alloc_sbuf_tensor_at(f"hh{i}", [P, CW], F32, offset=Nn_at + 4 * PSB * i) for i in range(4)]

        pd = Place(arena)
        gw = pd("gw", [E2, D])
        gT = pd("gT", [P, KD, E2])
        dW1 = pd("dW1", [P, E2, KD, DF])
        dW2 = pd("dW2", [P, E2, D])
        db1 = pd("db1", [P, E2])
        db2 = pd("db2", [E2, D])
        sW1 = pd("sW1", [P, KD, SH])
        sW2 = pd("sW2", [P, SK, D])
        sb1 = pd("sb1", [P, SK])
        sb2 = pd("sb2", [1, D])
        comb = pd("comb", [P, NT, E2])
        combT = pd("combT", [E2, NP])
        hE = [pd(f"hE{i}", [P, N]) for i in range(2)]
        hS = pd("hS", [P, SK, N])

        psum = ctx.enter_context(nc.psum_tensor("psum", [P, 8, PSB], F32))
        banks = [psum[:, i, :] for i in range(8)]
        psum_flat = psum[:, :, :].rearrange("p b n -> p (b n)")
        act_banks, dve_banks = banks[0:4], banks[4:8]

        s_x = sem("x_loaded")
        s_gw = sem("gat_weights_loaded")
        s_gw2 = sem("gat_score_weights_loaded")
        s_adj = [sem(f"adj_rows_loaded{i}") for i in range(RING)]
        s_zero = sem("zeros_ready")
        s_ysz = sem("expert_rows_zeroed")
        s_xsz = sem("routed_rows_zeroed")
        s_id = sem("constant_steps")
        s_const = sem("constants_ready")
        s_dw2 = sem("dense_last_bias_loaded")
        s_fin = sem("result_ready")
        s_pad = sem("pads_cleared")
        act_full = sem("act_bank_full")
        act_done = sem("act_bank_done")
        dve_full = sem("dve_bank_full")
        dve_done = sem("dve_bank_done")
        chain = sem("vector_chain")
        s_var = sem("variance_ready")
        s_rstd = sem("inverse_deviation_ready")
        s_norm = sem("norm_tiles_ready")
        s_scan = sem("adj_tile_scanned")
        s_qcol = sem("query_columns_ready")
        s_e = sem("branch_exponentials_ready")
        s_q = sem("branches_joined")
        s_p = sem("attention_weights_ready")
        s_used = sem("attention_weights_used")
        s_attd = sem("attention_group_done")
        s_vm = sem("elu_argument_ready")
        s_ve = sem("elu_exp_ready")
        s_x1 = sem("attention_added")
        s_we = [sem(f"expert_weights_loaded{i}") for i in range(2)]
        s_wfree = sem("expert_weights_free")
        s_wrdy = sem("expert_weights_ready")
        s_wr = sem("router_weights_loaded")
        s_lc = sem("logits_centred")
        s_le = sem("logits_exp")
        s_msel = sem("selection_ready")
        s_route = sem("routes_ready")
        s_scat = sem("rows_scattered")
        s_xg = sem("slot_rows_loaded")
        s_xt = sem("slot_rows_transposed")
        s_xtd = sem("slot_transpose_copied")
        s_h = sem("hidden_sums_ready")
        s_hd = sem("hidden_gelu_ready")
        s_ht = sem("hidden_transposed")
        s_htd = sem("hidden_transpose_copied")
        s_y = sem("slots_finished")
        s_yd = sem("slot_output_copied")
        s_yw = sem("slot_output_written")
        s_yall = sem("all_slots_written")
        s_yg = sem("expert_rows_gathered")
        s_ats = sem("adj_transposed_stored")
        s_atr = sem("adj_words_loaded")
        s_wide = sem("adj_width_known")
        s_low = sem("adj_low_bits_ready")
        s_cwr = [sem(f"gcn_weights{i}_loaded") for i in range(3)]
        s_cwh = sem("gcn_weights_high_parts")
        s_cws = sem("gcn_weights_split")
        s_np = sem("norm_split")
        s_pair = sem("hidden_chunks_split")
        s_cw = sem("gcn_weights_loaded")
        s_mix = sem("mixture_added")
        s_dw = sem("dense_weights_loaded")
        s_gwt = sem("gate_loaded")
        s_comb = sem("combine_weights_ready")
        s_out = sem("output_written")

        block = ctx.enter_context(nc.Block())
        mark = {}

        @block.tensor
        def _(pe):
            na = [0]
            nv = [0]

            def act_bank():
                n = na[0]
                if n >= 4:
                    pe.wait_ge(act_done, n - 3)
                return act_banks[n % 4]

            def to_act(mm):
                na[0] += 1
                mm.then_inc(act_full, 1)
                return na[0]

            def dve_bank():
                n = nv[0]
                if n >= 4:
                    pe.wait_ge(dve_done, n - 3)
                return dve_banks[n % 4]

            def to_dve(mm):
                nv[0] += 1
                mm.then_inc(dve_full, 1)
                return nv[0]

            def transpose_norm(layer):
                for q in range(-(-NT // 2)):
                    tiles = range(2 * q, min(2 * q + 2, NT))
                    pe.wait_ge(s_norm, NT * layer + tiles[-1] + 1)
                    b = act_bank()
                    for i, t in enumerate(tiles):
                        for k in range(KD):
                            mm = pe.transpose(b[:, (k * 2 + i) * P:(k * 2 + i + 1) * P],
                                              Nn[:, t, k * P:(k + 1) * P], ident[:, :])
                    last = to_act(mm)
                return last

            def router(W):
                b = dve_bank()
                for t in range(NT):
                    r = rows(t)
                    for k in range(KD):
                        mm = pe.matmul(b[0:r, t * E:(t + 1) * E], NTr[:, k, t * P:t * P + r], W[:, k, :],
                                       start=(k == 0), stop=(k == KD - 1))
                return to_dve(mm)

            pe.wait_ge(s_const, 1)
            pe.wait_ge(s_gw, 16 * 2)
            pe.wait_ge(s_gw2, 16 * 2)
            b = act_bank()
            for fo in range(KD):
                for fi in range(KD):
                    mm = pe.transpose(b[:, (fo * KD + fi) * P:(fo * KD + fi + 1) * P],
                                      gW[:, fi, fo * P:(fo + 1) * P], ident[:, :])
            j = to_act(mm)
            pe.wait_ge(act_done, j)
            b = dve_bank()
            for fi in range(KD):
                for fo in range(KD):
                    mm = pe.matmul(b[:, 2 * fi:2 * fi + 2], gWT[:, fo, fi * P:(fi + 1) * P], a2[:, :, fo],
                                   start=(fo == 0), stop=(fo == KD - 1))
            to_dve(mm)
            j = transpose_norm(0)
            pe.wait_ge(act_done, j)
            pe.wait_ge(dve_done, nv[0])
            for c0, cw in CHUNKS:
                b = act_bank()
                for k in range(KD):
                    mm = pe.matmul(b[:, 0:cw], Wa[:, k, 1:2].to_broadcast([P, P]), NTr[:, k, c0:c0 + cw],
                                   start=(k == 0), stop=(k == KD - 1))
                mark["row"] = to_act(mm)
            b = dve_bank()
            for t in range(NT):
                r = rows(t)
                for k in range(KD):
                    mm = pe.matmul(b[0:r, 2 * t:2 * t + 2], NTr[:, k, t * P:t * P + r], Wa[:, k, :],
                                   start=(k == 0), stop=(k == KD - 1))
            mark["Wh"] = to_dve(mm)
            for t in range(NT):
                r = rows(t)
                pe.wait_ge(s_adj[t % RING], 16 * (t // RING + 1))
                for j0 in range(0, NT, 4):
                    js = range(j0, min(j0 + 4, NT))
                    b = act_bank()
                    for i, j in enumerate(js):
                        mm = pe.transpose(b[:, i * P:i * P + r], adjn[t % RING][0:r, j * P:(j + 1) * P],
                                          ident[0:r, 0:r])
                    mark["adjT", t] = to_act(mm)
                b = act_bank()
                for k in range(KD):
                    mm = pe.matmul(b[0:r, :], NTr[:, k, t * P:t * P + r], wtr[:, k, :, :],
                                   start=(k == 0), stop=(k == KD - 1))
                jG = to_act(mm)
            pe.wait_ge(act_done, jG)
            b = dve_bank()
            for t in range(NT):
                r = rows(t)
                mm = pe.matmul(b[:, :], ones[0:r, :], G[0:r, t, :, 0:D], start=(t == 0), stop=(t == NT - 1))
            to_dve(mm)
            pe.wait_ge(s_qcol, 1)
            for v in range(4):
                for t0 in range(0, NT, 4):
                    b = act_bank() if v < 2 else dve_bank()
                    for t in range(t0, min(t0 + 4, NT)):
                        r = rows(t)
                        mm = pe.transpose(b[:, (t - t0) * P:(t - t0) * P + r],
                                          qcol[0:r, v, t:t + 1].to_broadcast([r, P]), ident[0:r, 0:r])
                    if v < 2:
                        to_act(mm)
                    else:
                        mark["qrow"] = to_dve(mm)
            pe.wait_ge(act_done, na[0])
            pe.wait_ge(dve_done, nv[0])
            step = 0
            for g, (t0, nt) in enumerate(GROUPS):
                if g:
                    pe.wait_ge(s_attd, g)
                for j in range(NT):
                    r = rows(j)
                    step += 1
                    pe.wait_ge(s_p, step)
                    for i in range(nt):
                        q = rows(t0 + i)
                        for s in range(2):
                            mm = pe.matmul(banks[2 * i + s][0:q, 0:D + 1], pp[(step - 1) % 2][0:r, s, i * P:i * P + q],
                                           G[0:r, j, s, 0:D + 1], start=(j == 0), stop=(j == NT - 1))
                    mm.then_inc(s_used, 1)
            pe.wait_ge(s_attd, len(GROUPS))

            j = transpose_norm(1)
            pe.wait_ge(act_done, j)
            pe.wait_ge(s_wr, 16)
            router(Wr)
            pe.wait_ge(s_msel, 1)
            b = dve_bank()
            pe.matmul(b[:, 0:(NT + 1) * E], ones[:, :], Mpre[:, :, :], start=True, stop=False)
            mm = pe.matmul(b[:, 0:NT * E], upper[:, :], Msel[:, :, :], start=False, stop=True)
            to_dve(mm)
            pe.wait_ge(s_low, 1)
            b = dve_bank()
            to_dve(pe.matmul(b[:, 0:1], ones[:, :], lowsum[:, :], start=True, stop=True))
            pe.wait_ge(act_done, na[0])
            pe.wait_ge(dve_done, nv[0])
            pe.wait_ge(s_route, 1)

            def rows_T(s):
                pe.wait_ge(s_xg, s * 16 + 16)
                for k in range(KD):
                    mm = pe.transpose(banks[0][:, k * P:(k + 1) * P], xg[:, k * P:(k + 1) * P], ident[:, :])
                mm.then_inc(s_xt, 1)

            def up(s, e):
                pe.wait_ge(s_xtd, s + 1)
                for h in range(2):
                    for i in range(4):
                        f = 4 * h + i
                        for k in range(KD):
                            mm = pe.matmul(psum_flat[:, bass.ds((s % 2) * (2 * PSB) + (1 + h) * PSB + i * P, P)],
                                           W1b[:, e % 2, k * F + f * P:k * F + (f + 1) * P], xgT[:, k, :],
                                           start=(k == 0), stop=(k == KD - 1))
                    mm.then_inc(s_h, 1)

            def down(s, e):
                for f in range(FK):
                    if f % 4 == 0:
                        pe.wait_ge(s_hd, s * 2 + (f // 4 + 1))
                    if f == 0:
                        pe.wait_ge(s_yd, s) if not isinstance(s, int) or s else None
                    mm = pe.matmul(banks[5][:, 0:D], hT[:, f, :], W2b[:, e % 2, f * D:(f + 1) * D],
                                   start=(f == 0), stop=(f == FK - 1))
                mm.then_inc(s_y, 1)

            rows_T(0)
            pe.wait_ge(s_wrdy, 1)
            up(0, 0)
            rows_T(1)
            lasts = [pe.value_load(lastI[0:1, e:e + 1], min_val=e, max_val=SLOTS - 1) for e in range(E)]
            for e in range(E):
                begin, last = lasts[e - 1] + 1 if e else 0, lasts[e]
                with pe.If(last > begin):
                    with pe.Fori(begin, last) as s:
                        up(s + 1, e)
                        rows_T(s + 2)
                        down(s, e)
                if e + 1 < E:
                    pe.wait_ge(s_wrdy, e + 2)
                    up(last + 1, e + 1)
                    rows_T(last + 2)
                down(last, e)

            mark["gcn_act"] = na[0]
            pe.wait_ge(s_np, NT)
            pe.wait_ge(s_mix, 1)
            pe.wait_ge(s_wide, 1)
            wide = pe.value_load(wideI[0:1, 0:1], min_val=0, max_val=1)
            np_ = [0]

            def three(out, a, b, start, stop):
                pe.matmul(out, a(0), b(0), start=start, stop=False)
                pe.matmul(out, a(0), b(1), start=False, stop=False)
                return pe.matmul(out, a(1), b(0), start=False, stop=stop)

            def over_adj(stage):
                at = (na[0], nv[0], np_[0])
                with pe.If(wide == 0):
                    stage(ATr, lambda v: v)
                with pe.Else():
                    na[0], nv[0], np_[0] = at
                    stage(ATr[:, :, :].bitcast(F32), lambda v: v.bitcast(F32))

            def features_times_adj(W, nf):
                def stage(A, view):
                    for c0, cw in CHUNKS:
                        for f in range(nf):
                            b = act_bank()
                            for j in range(NT):
                                r = rows(j)
                                for part in range(2):
                                    mm = pe.matmul(b[:, 0:cw], view(W[0:r, part, j, f * P:(f + 1) * P]),
                                                   A[0:r, j, c0:c0 + cw], start=(j == 0 and part == 0),
                                                   stop=(j == NT - 1 and part == 1))
                            to_act(mm)
                            np_[0] += 1
                return stage

            def times_weights(HT_, W, wn, nk):
                for t in range(NT):
                    r = rows(t)
                    b = dve_bank()
                    for k in range(nk):
                        mm = three(b[0:r, 0:wn], lambda p: HT_[:, p, k, t * P:t * P + r], lambda p: W[:, p, k, :],
                                   k == 0, k == nk - 1)
                    to_dve(mm)

            over_adj(features_times_adj(Np, KD))
            pe.wait_ge(s_pair, np_[0])
            pe.wait_ge(s_cws, 1)
            for c0, cw in CHUNKS:
                for h in range(HK):
                    b = act_bank()
                    for k in range(KD):
                        mm = three(b[:, 0:cw], lambda p: cW1[:, p, k, h * P:(h + 1) * P],
                                   lambda p: Z1T[:, p, k, c0:c0 + cw], k == 0, k == KD - 1)
                    to_act(mm)
                    np_[0] += 1
            pe.wait_ge(s_pair, np_[0])
            pe.wait_ge(s_cws, 3)
            times_weights(H1T, cW2, HID, HK)
            pe.wait_ge(dve_done, nv[0])
            over_adj(features_times_adj(Y2, HK))
            pe.wait_ge(s_pair, np_[0])
            times_weights(H2T, cW3, D, HK)
            pe.wait_ge(dve_done, nv[0])

            def adj_times_rows(A, view):
                for t in range(NT):
                    q = rows(t)
                    b = dve_bank()
                    for j in range(NT):
                        r = rows(j)
                        for part in range(2):
                            mm = pe.matmul(b[0:q, 0:D], A[0:r, j, t * P:t * P + q], view(Y3[0:r, part, j, :]),
                                           start=(j == 0 and part == 0), stop=(j == NT - 1 and part == 1))
                    to_dve(mm)

            over_adj(adj_times_rows)
            mark["gcn_last_dve"] = nv[0]

            pe.wait_ge(s_gwt, 16)
            b = dve_bank()
            for k in range(KD):
                mm = pe.transpose(b[:, k * E2:(k + 1) * E2], gw[0:E2, k * P:(k + 1) * P], ident[0:E2, 0:E2])
            jg = to_dve(mm)
            jt = transpose_norm(3)
            pe.wait_ge(dve_done, jg)
            pe.wait_ge(act_done, jt)
            router(gT)
            pe.wait_ge(s_dw, 16 * 8)
            pe.wait_ge(s_dw2, 16)

            def expert_up(e):
                for c0, cw in CHUNKS:
                    b = act_bank()
                    for k in range(KD):
                        mm = pe.matmul(b[:, 0:cw], dW1[:, e, k, :], NTr[:, k, c0:c0 + cw],
                                       start=(k == 0), stop=(k == KD - 1))
                    j = to_act(mm)
                return j

            js = [expert_up(0), expert_up(1)]
            for f in range(SK):
                for c0, cw in CHUNKS:
                    b = act_bank()
                    for k in range(KD):
                        mm = pe.matmul(b[:, 0:cw], sW1[:, k, f * P:(f + 1) * P], NTr[:, k, c0:c0 + cw],
                                       start=(k == 0), stop=(k == KD - 1))
                    jsh = to_act(mm)
            pe.wait_ge(s_comb, 1)
            for t0 in range(0, NT, 4):
                b = dve_bank()
                for t in range(t0, min(t0 + 4, NT)):
                    mm = pe.transpose(b[0:E2, (t - t0) * P:(t - t0 + 1) * P], comb[:, t, :], ident[:, :])
                jc = to_dve(mm)
            for e in range(E2):
                pe.wait_ge(act_done, js[e])
                for t in range(NT):
                    r = rows(t)
                    b = dve_bank()
                    mm = pe.matmul(b[0:r, 0:D], hE[e % 2][:, t * P:t * P + r], dW2[:, e, :], start=True, stop=True)
                    to_dve(mm)
                mark["hE_used", e] = nv[0]
                if e + 2 < E2:
                    js.append(expert_up(e + 2))
            pe.wait_ge(act_done, jsh)
            pe.wait_ge(dve_done, jc)
            for t in range(NT):
                r = rows(t)
                b = dve_bank()
                for k in range(SK):
                    pe.matmul(b[0:r, 0:D], hS[:, k, t * P:t * P + r], sW2[:, k, :], start=(k == 0), stop=False)
                pe.matmul(b[0:r, 0:D], combT[0:E2, t * P:t * P + r], db2[0:E2, :], start=False, stop=False)
                mm = pe.matmul(b[0:r, 0:D], ones[0:1, 0:r], sb2[0:1, :], start=False, stop=True)
                to_dve(mm)

        @block.sync
        def _(sp):
            sp.wait_ge(s_pad, 1)
            sp.dma_start(X[:, 0:full, :], x[0:full * P, :].rearrange("(t p) d -> p t d", p=P)).then_inc(s_x, 16)
            sp.dma_start(X[0:tail, full, :], x[full * P:N, :]).then_inc(s_x, 16)
            sp.dma_start(wtr[:, :, 0, :], gat_wtrans[0:D, :].rearrange("(k p) d -> p k d", p=P)).then_inc(s_gw, 16)
            sp.dma_start(wtr[:, :, 1, :], gat_wtrans[D:2 * D, :].rearrange("(k p) d -> p k d", p=P)).then_inc(s_gw, 16)
            sp.dma_start(Wr[:, :, :], moe_Wr.rearrange("(k p) e -> p k e", p=P)).then_inc(s_wr, 16)
            sp.wait_ge(s_pad, 1 + RING)
            for t in range(NT):
                r = rows(t)
                if t >= RING:
                    sp.wait_ge(s_scan, t - RING + 1)
                    sp.wait_ge(act_full, mark["adjT", t - RING])
                sp.dma_start(adjn[t % RING][0:r, 0:N], adj[t * P:t * P + r, :]).then_inc(s_adj[t % RING], 16)
            sp.wait_ge(act_done, mark["adjT", NT - 1])
            for j in range(NT):
                sp.dma_start(at_dram[:, j, :], AT[:, j, :]).then_inc(s_ats, 16)
            sp.wait_ge(s_ats, 16 * NT)
            sp.wait_ge(s_p, NT * len(GROUPS))
            for j in range(NT):
                sp.dma_start(ATr[:, j, :].bitcast(F32), at_dram[:, j, :]).then_inc(s_atr, 16)
            sp.wait_ge(s_x1, 1)
            sp.wait_ge(s_route, 1)
            sp.wait_ge(s_scat, 16 * 2 * NT)
            last = sp.value_load(lastI[0:1, E - 1:E], min_val=E - 1, max_val=SLOTS - 1)
            for s in range(4):
                if s:
                    sp.wait_ge(s_xt, s)
                sp.dma_start(xg[:, :], xs[s * P:(s + 1) * P, :]).then_inc(s_xg, 16)
            sp.wait_ge(s_ysz, 16)
            sp.wait_ge(s_yd, 1)
            sp.dma_start(ys[0:P, :], yrow[:, :]).then_inc(s_yw, 16)
            with sp.Fori(1, last - 1) as s:
                sp.wait_ge(s_xt, s + 3)
                sp.dma_start(xg[:, :], xs[bass.ds(s * P + 3 * P, P), :]).then_inc(s_xg, 16)
                sp.wait_ge(s_yd, s + 1)
                sp.dma_start(ys[bass.ds(s * P, P), :], yrow[:, :]).then_inc(s_yw, 16)
            sp.wait_ge(s_yd, last)
            sp.dma_start(ys[bass.ds((last - 1) * P, P), :], yrow[:, :]).then_inc(s_yw, 16)
            sp.wait_ge(s_yd, last + 1)
            sp.dma_start(ys[bass.ds(last * P, P), :], yrow[:, :]).then_inc(s_yw, 16)
            sp.wait_ge(s_mix, 1)
            sp.dma_start(raw1[:, :, :], gcn_W1.rearrange("(k p) d -> p k d", p=P)).then_inc(s_cwr[0], 16)
            sp.dma_start(raw2[:, :, :], gcn_W2.rearrange("(k p) d -> p k d", p=P)).then_inc(s_cwr[1], 16)
            sp.dma_start(raw3[:, :, :], gcn_W3.rearrange("(k p) d -> p k d", p=P)).then_inc(s_cwr[2], 16)
            with nc.allow_non_contiguous_dma(reason="bias columns"):
                sp.dma_start(cb1[:, :], gcn_b1.rearrange("(h p) -> p h", p=P)).then_inc(s_cw, 16)
                sp.dma_start(cb2[:, :], gcn_b2.rearrange("(h p) -> p h", p=P)).then_inc(s_cw, 16)
            sp.dma_start(cb3[:, :], gcn_b3.rearrange("(o d) -> o d", o=1).to_broadcast([P, D])).then_inc(s_cw, 16)
            sp.wait_ge(dve_done, mark["gcn_last_dve"])
            sp.dma_start(gw[:, :], ffn_gate).then_inc(s_gwt, 16)
            with nc.allow_non_contiguous_dma(reason="bias columns"):
                sp.dma_start(db1[:, :], ffn_b1.rearrange("e p -> p e")).then_inc(s_dw, 16)
                sp.dma_start(sb1[:, :], ffn_sb1.rearrange("(h p) -> p h", p=P)).then_inc(s_dw, 16)
            for k in range(KD):
                sp.dma_start(dW1[:, :, k, :], ffn_w1[:, k * P:(k + 1) * P, :].rearrange("e p f -> p e f")).then_inc(s_dw, 16)
            sp.dma_start(dW2[:, :, :], ffn_w2.rearrange("e f d -> f e d")).then_inc(s_dw, 16)
            sp.dma_start(db2[:, :], ffn_b2).then_inc(s_dw, 16)
            sp.dma_start(sW1[:, :, :], ffn_sw1.rearrange("(k p) d -> p k d", p=P)).then_inc(s_dw, 16)
            sp.dma_start(sW2[:, :, :], ffn_sw2.rearrange("(k p) d -> p k d", p=P)).then_inc(s_dw, 16)
            sp.dma_start(sb2[:, :], ffn_sb2.rearrange("(o d) -> o d", o=1)).then_inc(s_dw2, 16)
            sp.wait_ge(s_fin, 1)
            sp.dma_start(out[0:full * P, :].rearrange("(t p) d -> p t d", p=P), X[:, 0:full, :]).then_inc(s_out, 16)
            sp.dma_start(out[full * P:N, :], X[0:tail, full, :]).then_inc(s_out, 16)
            sp.wait_ge(s_out, 32)

        @block.gpsimd
        def _(pool):
            pool.memset(X[64:P, NT - 1, :], 0.0).then_inc(s_pad, 1)
            pool.wait_ge(s_pad, 1)
            for buffer in adjn:
                pool.memset(buffer[:, N:NP], 0.0).then_inc(s_pad, 1)
            pool.memset(ident[:, :], 0.0).then_inc(s_id, 1)
            pool.memset(ones[:, :], 1.0).then_inc(s_id, 1)
            pool.memset(valid[:, :], 1.0).then_inc(s_id, 1)
            pool.memset(neghalf[:, :], -0.5).then_inc(s_id, 1)
            pool.iota(rev[:, :], pattern=[[-1, E]], base=E, channel_multiplier=0,
                      allow_small_or_imprecise_dtypes=True).then_inc(s_id, 1)
            pool.wait_ge(s_id, 5)
            pool.affine_select(out=upper[:, :], in_=ones[:, :], compare_op=ALU.is_gt, fill=0.0,
                               base=0, pattern=[[1, P]], channel_multiplier=-1).then_inc(s_id, 1)
            pool.affine_select(out=valid[:, :], in_=valid[:, :], compare_op=ALU.is_gt, fill=0.0,
                               base=N, pattern=[[-P, NT]], channel_multiplier=-1).then_inc(s_id, 1)
            pool.memset(G[:, :, :, D:D + 2], 1.0).then_inc(s_id, 1)
            pool.wait_ge(s_id, 8)
            pool.affine_select(out=ident[:, :], in_=ident[:, :], compare_op=ALU.not_equal, fill=1.0,
                               base=0, pattern=[[-1, P]], channel_multiplier=1).then_inc(s_const, 1)
            pool.dma_start(gW[:, :, :], gat_W.rearrange("(k p) d -> p k d", p=P)).then_inc(s_gw2, 16)
            with nc.allow_non_contiguous_dma(reason="two vectors"):
                pool.dma_start(a2[:, :, :].rearrange("p w k -> p (w k)"), gat_a.rearrange("(c p) o -> p (c o)", p=P)).then_inc(s_gw2, 16)
            def deviation(k):
                pool.wait_ge(s_var, k)
                pool.tensor_tensor(rstd[:, :], rstd[:, :], neghalf[:, :], ALU.pow).then_inc(s_rstd, 1)

            deviation(1)
            pool.memset(zero[:, :], 0.0).then_inc(s_zero, 1)
            pool.wait_ge(s_zero, 1)
            pool.dma_start(xs.rearrange("(s p) d -> p s d", p=P),
                           zero[:, :].unsqueeze(1).to_broadcast([P, SLOTS + 1, D])).then_inc(s_xsz, 16)
            pool.dma_start(ys.rearrange("(s p) d -> p s d", p=P),
                           zero[:, :].unsqueeze(1).to_broadcast([P, SLOTS, D])).then_inc(s_ysz, 16)
            pool.wait_ge(s_x1, 1)
            pool.iota(kval[:, :], pattern=[[P, NT]], base=0, channel_multiplier=0,
                      allow_small_or_imprecise_dtypes=True).then_inc(s_zero, 1)
            pool.wait_ge(s_zero, 2)
            def load_expert(e):
                pool.dma_start(W1b[:, e % 2, :].rearrange("p (k f) -> p k f", k=KD),
                               moe_W1[e, :, :].rearrange("(k p) f -> p k f", p=P)).then_inc(s_we[e % 2], 16)
                pool.dma_start(W2b[:, e % 2, :].rearrange("p (k f) -> p k f", k=FK),
                               moe_W2[e, :, :].rearrange("(k p) f -> p k f", p=P)).then_inc(s_we[e % 2], 16)

            load_expert(0)
            load_expert(1)
            deviation(2)
            pool.wait_ge(s_xsz, 16)
            pool.wait_ge(s_route, 1)
            for t in range(NT):
                r = rows(t)
                for c in range(2):
                    pool.indirect_dma_start(out=xs, out_offset=bass.IndirectOffsetOnAxis(ap=posI[0:r, c, t:t + 1], axis=0),
                                            in_=Nn[0:r, t, :], in_offset=None).then_inc(s_scat, 16)
            for e in range(E):
                pool.wait_ge(s_we[e % 2], 32 * (e // 2 + 1))
                pool.sem_inc(s_wrdy, 1)
                if 1 <= e < E - 1:
                    upto = pool.value_load(cumI[0:1, e:e + 1], min_val=1, max_val=SLOTS)
                    pool.wait_ge(s_y, upto)
                    pool.sem_inc(s_wfree, 1)
                    load_expert(e + 1)
            slots = pool.value_load(cumI[0:1, E:E + 1], min_val=E, max_val=SLOTS)
            pool.wait_ge(s_yw, slots * 16)
            pool.sem_inc(s_yall, 1)
            for t in range(NT):
                r = rows(t)
                for c in range(2):
                    pool.indirect_dma_start(out=yg[0:r, c, t, :], out_offset=None, in_=ys,
                                            in_offset=bass.IndirectOffsetOnAxis(ap=posI[0:r, c, t:t + 1], axis=0)
                                            ).then_inc(s_yg, 16)
            deviation(3)
            pool.wait_ge(s_np, NT)
            for i, (raw, pair) in enumerate(((raw1, cW1), (raw2, cW2), (raw3, cW3))):
                pool.wait_ge(s_cwr[i], 16)
                pool.tensor_copy(pair[:, 0, :, :], raw[:, :, :]).then_inc(s_cwh, 1)
                pool.wait_ge(s_cwh, i + 1)
                pool.tensor_tensor(pair[:, 1, :, :], raw[:, :, :], pair[:, 0, :, :].bitcast(F32),
                                   ALU.subtract).then_inc(s_cws, 1)
            deviation(4)

        @block.scalar
        def _(act):
            n = [0]

            def bank():
                act.wait_ge(act_full, n[0] + 1)
                b = act_banks[n[0] % 4]
                n[0] += 1
                return b

            def transpose_norm():
                for q in range(-(-NT // 2)):
                    w = min(2, NT - 2 * q)
                    b = bank()
                    act.activation(NTr[:, :, 2 * q * P:(2 * q + w) * P],
                                   b[:, :].rearrange("p (k n) -> p k n", k=KD)[:, :, 0:w * P],
                                   ACT.Copy).then_inc(act_done, 1)

            b = bank()
            act.activation(gWT[:, :, :], b[:, :].rearrange("p (k n) -> p k n", k=KD), ACT.Copy).then_inc(act_done, 1)
            transpose_norm()
            for c0, cw in CHUNKS:
                b = bank()
                act.activation(Wrow[:, c0:c0 + cw], b[:, 0:cw], ACT.Copy).then_inc(act_done, 1)
            act.wait_ge(s_const, 1)
            for t in range(NT):
                r = rows(t)
                for j0 in range(0, NT, 4):
                    nj = min(4, NT - j0)
                    b = bank()
                    act.activation(AT[:, j0:j0 + nj, t * P:t * P + r],
                                   b[:, 0:nj * P].rearrange("p (j i) -> p j i", i=P)[:, :, 0:r],
                                   ACT.Copy).then_inc(act_done, 1)
                b = bank()
                act.activation(G[0:r, t, :, 0:D], b[0:r, :].rearrange("p (s d) -> p s d", s=2),
                               ACT.Copy).then_inc(act_done, 1)
            for v in range(2):
                for t0 in range(0, NT, 4):
                    w = min(4 * P, N - t0 * P)
                    b = bank()
                    act.activation(qrow[:, v, t0 * P:t0 * P + w], b[:, 0:w], ACT.Copy).then_inc(act_done, 1)
            act.wait_ge(act_done, n[0])
            act.wait_ge(dve_done, mark["qrow"])
            steps = [(t0, nt, j) for t0, nt in GROUPS for j in range(NT)]

            def elu_exp(g):
                t0, nt = GROUPS[g]
                act.wait_ge(s_vm, g + 1)
                act.activation(Vm[:, t0:t0 + nt, :], Vm[:, t0:t0 + nt, :], ACT.Exp).then_inc(s_ve, 1)

            for i, (t0, nt, j) in enumerate(steps):
                w = min(GW, N - t0 * P)
                if i >= 2:
                    act.wait_ge(s_q, 2 * (i - 1))
                for v in range(4):
                    act.activation(ee[i % 2][:, v, 0:w], qrow[:, v, t0 * P:t0 * P + w], ACT.Exp,
                                   bias=kcol[:, v, j:j + 1]).then_inc(s_e, 1)
                if j == 4 and t0:
                    elu_exp(i // NT - 1)
            elu_exp(len(GROUPS) - 1)
            transpose_norm()
            act.wait_ge(s_lc, 1)
            act.activation(probs[:, :, :], logits[:, :, :], ACT.Exp).then_inc(s_le, 1)

            def gelu(s):
                if not isinstance(s, int) or s:
                    act.wait_ge(s_y, s)
                for h in range(2):
                    act.wait_ge(s_h, s * 2 + (h + 1))
                    act.activation(hT[:, 4 * h:4 * h + 4, :].rearrange("p f n -> p (f n)"),
                                   psum_flat[:, bass.ds((s % 2) * (2 * PSB) + (1 + h) * PSB, PSB)],
                                   ACT.Gelu).then_inc(s_hd, 1)

            def copy_rows_T(s):
                act.wait_ge(s_xt, s + 1)
                act.activation(xgT[:, :, :], banks[0][:, 0:KD * P].rearrange("p (k n) -> p k n", k=KD),
                               ACT.Copy).then_inc(s_xtd, 1)

            act.wait_ge(s_route, 1)
            last = act.value_load(lastI[0:1, E - 1:E], min_val=E - 1, max_val=SLOTS - 1)
            copy_rows_T(0)
            copy_rows_T(1)
            gelu(0)
            copy_rows_T(2)
            with act.Fori(1, last) as s:
                gelu(s)
                copy_rows_T(s + 2)
            gelu(last)
            mark["act_before_gcn"] = n[0]
            act.wait_ge(s_np, NT)
            act.wait_ge(s_cw, 16 * 3)
            jobs = [None] * (NC * KD) + [cb1[:, h:h + 1] for _ in CHUNKS for h in range(HK)] \
                + [cb2[:, h:h + 1] for _ in CHUNKS for h in range(HK)]
            widths = [cw for _, cw in CHUNKS for _ in range(KD)] + [cw for _, cw in CHUNKS for _ in range(HK)] * 2
            for i, (bias, cw) in enumerate(zip(jobs, widths)):
                b = bank()
                if i >= 4:
                    act.wait_ge(s_pair, i - 3)
                if bias is None:
                    act.activation(hh[i % 4][:, 0:cw], b[:, 0:cw], ACT.Copy).then_inc(act_done, 1)
                else:
                    act.activation(hh[i % 4][:, 0:cw], b[:, 0:cw], ACT.Relu, bias=bias).then_inc(act_done, 1)
            transpose_norm()

            def hidden(dst, bias):
                for c0, cw in CHUNKS:
                    b = bank()
                    act.activation(dst[:, c0:c0 + cw], b[:, 0:cw], ACT.Relu, bias=bias).then_inc(act_done, 1)

            act.wait_ge(s_lc, 2)
            act.activation(probs[:, :, :], logits[:, :, :], ACT.Exp).then_inc(s_le, 1)
            act.wait_ge(s_dw, 16 * 8)
            hidden(hE[0], db1[:, 0:1])
            hidden(hE[1], db1[:, 1:2])
            for f in range(SK):
                hidden(hS[:, f, :], sb1[:, f:f + 1])
            for e in range(2, E2):
                act.wait_ge(dve_full, mark["hE_used", e - 2])
                hidden(hE[e % 2], db1[:, e:e + 1])

        @block.vector
        def _(dve):
            n = [0]
            links = [0]
            lns = [0]

            def bank():
                dve.wait_ge(dve_full, n[0] + 1)
                b = dve_banks[n[0] % 4]
                n[0] += 1
                return b

            def link(ins):
                links[0] += 1
                ins.then_inc(chain, 1)

            def settle():
                dve.wait_ge(chain, links[0])

            def layer_norm():
                for t in range(NT):
                    link(dve.bn_stats(stats[:, t, :], X[:, t, :]))
                settle()
                for t in range(NT):
                    link(dve.bn_aggr(mv[:, t, :], stats[:, t, :]))
                settle()
                lns[0] += 1
                dve.tensor_scalar(rstd[:, :], mv[:, :, 1], EPS, None, ALU.add).then_inc(s_var, 1)
                dve.wait_ge(s_rstd, lns[0])
                for t in range(NT):
                    dve.tensor_scalar(Nn[:, t, :], X[:, t, :], mv[:, t, 0:1], rstd[:, t:t + 1],
                                      ALU.subtract, ALU.mult).then_inc(s_norm, 1)

            def over_e(ap):
                return ap.unsqueeze(2).to_broadcast([P, NT, E])

            revb = rev[:, :].unsqueeze(1).to_broadcast([P, NT, E])

            def top2(k):
                b = bank()
                src = b[:, 0:NT * E].rearrange("p (t e) -> p t e", e=E)
                link(dve.memset(logits[:, NT - 1, :], 0.0))
                settle()
                link(dve.tensor_copy(logits[0:tail, NT - 1, :], src[0:tail, NT - 1, :]))
                dve.tensor_copy(logits[:, 0:NT - 1, :], src[:, 0:NT - 1, :]).then_inc(dve_done, 1)
                settle()
                dve.wait_ge(dve_done, n[0])
                link(dve.tensor_reduce(rtmp[:, :], logits[:, :, :], AX, ALU.max))
                settle()
                dve.tensor_tensor(logits[:, :, :], logits[:, :, :], over_e(rtmp[:, :]), ALU.subtract).then_inc(s_lc, 1)
                dve.wait_ge(s_le, k)
                link(dve.tensor_reduce(rtmp[:, :], probs[:, :, :], AX, ALU.add))
                settle()
                link(dve.reciprocal(rtmp[:, :], rtmp[:, :]))
                settle()
                link(dve.tensor_tensor(probs[:, :, :], probs[:, :, :], over_e(rtmp[:, :]), ALU.mult))
                src_p = probs
                for p, oh in ((p1, oh1), (p2, oh2)):
                    settle()
                    link(dve.tensor_reduce(p[:, :], src_p[:, :, :], AX, ALU.max))
                    settle()
                    link(dve.tensor_tensor(eq[:, :, :], src_p[:, :, :], over_e(p[:, :]), ALU.is_equal))
                    settle()
                    link(dve.tensor_tensor(eq[:, :, :], eq[:, :, :], revb, ALU.mult))
                    settle()
                    link(dve.tensor_reduce(rtmp[:, :], eq[:, :, :], AX, ALU.max))
                    settle()
                    link(dve.tensor_tensor(oh[:, :, :], revb, over_e(rtmp[:, :]), ALU.is_equal))
                    settle()
                    if oh is oh1:
                        link(dve.scalar_tensor_tensor(probs2[:, :, :], oh1[:, :, :], -2.0, probs[:, :, :],
                                                      ALU.mult, ALU.add))
                        src_p = probs2

            dve.wait_ge(s_x, 32)
            layer_norm()
            b = bank()
            dve.tensor_copy(Wa[:, :, :], b[:, 0:2 * KD].rearrange("p (k w) -> p k w", w=2)).then_inc(dve_done, 1)
            dve.wait_ge(dve_done, n[0])
            b = bank()
            src = b[:, 0:2 * NT].rearrange("p (t w) -> p t w", w=2)
            link(dve.memset(Wh[:, NT - 1, :], 0.0))
            link(dve.memset(mx[:, :, :], 0.0))
            settle()
            link(dve.tensor_copy(Wh[0:tail, NT - 1, :], src[0:tail, NT - 1, :]))
            dve.tensor_copy(Wh[:, 0:NT - 1, :], src[:, 0:NT - 1, :]).then_inc(dve_done, 1)
            settle()
            dve.wait_ge(dve_done, n[0])
            dve.wait_ge(act_done, mark["row"])
            for t in range(NT):
                r = rows(t)
                dve.wait_ge(s_adj[t % RING], 16 * (t // RING + 1))
                link(dve.tensor_scalar(negn[0:r, :], adjn[t % RING][0:r, 0:N], 0.0, -BIG, ALU.is_le, ALU.mult))
                settle()
                link(dve.tensor_tensor_reduce(out=junk[0:r, :], in0=negn[0:r, :], in1=Wrow[0:r, :], scale=1.0,
                                              scalar=-2 * BIG, op0=ALU.add, op1=ALU.max, accum_out=mx[0:r, 0, t:t + 1]))
                settle()
                dve.tensor_tensor_reduce(out=junk[0:r, :], in0=negn[0:r, :], in1=Wrow[0:r, :], scale=1.0,
                                         scalar=-2 * BIG, op0=ALU.subtract, op1=ALU.max,
                                         accum_out=mx[0:r, 1, t:t + 1]).then_inc(s_scan, 1)
                dve.wait_ge(s_scan, t + 1)
            link(dve.tensor_scalar(has[:, :, :], mx[:, :, :], -BIG / 2, None, ALU.is_gt))
            settle()
            link(dve.tensor_tensor(mx[:, :, :], mx[:, :, :], has[:, :, :], ALU.mult))
            settle()
            link(dve.tensor_tensor(ms[:, 0, :], Wh[:, :, 0], mx[:, 0, :], ALU.add))
            link(dve.tensor_tensor(ms[:, 1, :], Wh[:, :, 0], mx[:, 1, :], ALU.subtract))
            settle()
            link(dve.scalar_tensor_tensor(m2[:, :, :], ms[:, :, :], ALPHA, ms[:, :, :], ALU.mult, ALU.max))
            for v, scale in enumerate((1.0, ALPHA, -1.0, -ALPHA)):
                link(dve.tensor_scalar(kcol[:, v, :], Wh[:, :, 1], scale, None, ALU.mult))
            settle()
            for v, scale in enumerate((1.0, ALPHA)):
                link(dve.scalar_tensor_tensor(qcol[:, v, :], Wh[:, :, 0], scale, m2[:, 0, :], ALU.mult, ALU.subtract))
                part = dve.scalar_tensor_tensor(qcol[:, 2 + v, :], Wh[:, :, 0], -scale, m2[:, 1, :], ALU.mult, ALU.add)
                if v == 0:
                    link(part)
                    settle()
            part.then_inc(s_qcol, 1)
            b = bank()
            dve.tensor_copy(Cs[:, :, :], b[:, :].rearrange("p (s d) -> p s d", s=2)).then_inc(dve_done, 1)
            for v in range(2, 4):
                for t0 in range(0, NT, 4):
                    w = min(4 * P, N - t0 * P)
                    b = bank()
                    dve.tensor_copy(qrow[:, v, t0 * P:t0 * P + w], b[:, 0:w]).then_inc(dve_done, 1)
            dve.wait_ge(act_done, mark["adjT", NT - 1])
            dve.wait_ge(dve_done, n[0])
            def group_end(g):
                t0, nt = GROUPS[g]
                dve.wait_ge(s_used, NT * (g + 1))
                whole = sum(rows(t0 + q) == P for q in range(nt))
                parts = [(0, whole, P)] + [(q, q + 1, rows(t0 + q)) for q in range(whole, nt)]
                for q0, q1, r in parts:
                    sums = psum[0:r, 2 * q0:2 * q1, D].rearrange("p (q s) -> p q s", s=2)
                    link(dve.tensor_scalar(emp[0:r, q0:q1, :], sums, 0.5, None, ALU.is_lt))
                    settle()
                    link(dve.scalar_tensor_tensor(den[0:r, q0:q1, :], emp[0:r, q0:q1, :], float(N), sums,
                                                  ALU.mult, ALU.add))
                settle()
                for q0, q1, r in parts:
                    link(dve.reciprocal(den[0:r, q0:q1, :], den[0:r, q0:q1, :]))
                settle()
                for q0, q1, r in parts:
                    link(dve.tensor_scalar(den[0:r, q0:q1, 1], den[0:r, q0:q1, 1], -1.0, None, ALU.mult))
                if whole < nt:
                    link(dve.memset(V[:, whole:nt, :], 0.0))
                settle()
                for q in range(nt):
                    r = rows(t0 + q)
                    link(dve.tensor_scalar(V[0:r, q, :], banks[2 * q][0:r, 0:D], den[0:r, q, 0:1], None, ALU.mult))
                for q0, q1, r in parts:
                    link(dve.tensor_tensor(emp[0:r, q0:q1, :], emp[0:r, q0:q1, :], den[0:r, q0:q1, :], ALU.mult))
                settle()
                for q in range(nt):
                    r = rows(t0 + q)
                    both = dve.scalar_tensor_tensor(V[0:r, q, :], banks[2 * q + 1][0:r, 0:D], den[0:r, q, 1:2],
                                                    V[0:r, q, :], ALU.mult, ALU.add)
                    if q == nt - 1:
                        both.then_inc(s_attd, 1)
                    else:
                        link(both)
                dve.wait_ge(s_attd, g + 1)
                for s in range(2):
                    settle()
                    for q in range(nt):
                        r = rows(t0 + q)
                        link(dve.scalar_tensor_tensor(V[0:r, q, :], Cs[0:r, s, :], emp[0:r, q, s:s + 1], V[0:r, q, :],
                                                      ALU.mult, ALU.add))
                settle()
                dve.tensor_scalar(Vm[:, t0:t0 + nt, :], V[:, 0:nt, :], 0.0, None, ALU.min).then_inc(s_vm, 1)
                link(dve.tensor_scalar(V2[:, 0:nt, :], V[:, 0:nt, :], 0.0, -1.0, ALU.max, ALU.add))
                settle()
                link(dve.tensor_tensor(X[:, t0:t0 + nt, :], X[:, t0:t0 + nt, :], V2[:, 0:nt, :], ALU.add))
                dve.wait_ge(s_vm, g + 1)

            i = 0
            for g, (t0, nt) in enumerate(GROUPS):
                c0 = t0 * P
                w = min(GW, N - c0)
                for j in range(NT):
                    e = ee[i % 2]
                    if i:
                        dve.wait_ge(s_p, i)
                    link(dve.tensor_scalar(mask[:, 0:w], AT[:, j, c0:c0 + w], 0.0, None, ALU.is_gt))
                    dve.wait_ge(s_e, 4 * i + 4)
                    dve.tensor_tensor(qq[:, 0, 0:w], e[:, 0, 0:w], e[:, 1, 0:w], ALU.max).then_inc(s_q, 1)
                    dve.tensor_tensor(qq[:, 1, 0:w], e[:, 2, 0:w], e[:, 3, 0:w], ALU.min).then_inc(s_q, 1)
                    if i >= 2:
                        dve.wait_ge(s_used, i - 1)
                    settle()
                    dve.wait_ge(s_q, 2 * i + 2)
                    dve.scalar_tensor_tensor(pp[i % 2][:, :, 0:w], qq[:, :, 0:w], 1.0,
                                             mask[:, 0:w].unsqueeze(1).to_broadcast([P, 2, w]),
                                             ALU.min, ALU.mult).then_inc(s_p, 1)
                    i += 1
                    if g and j == 1:
                        group_end(g - 1)
            group_end(len(GROUPS) - 1)
            settle()
            dve.wait_ge(s_ve, len(GROUPS))
            dve.tensor_tensor(X[:, :, :], X[:, :, :], Vm[:, :, :], ALU.add).then_inc(s_x1, 1)
            dve.wait_ge(s_x1, 1)

            layer_norm()
            top2(1)
            settle()
            validb = over_e(valid[:, :])
            link(dve.tensor_tensor(Msel[:, :, :], oh1[:, :, :], oh2[:, :, :], ALU.add))
            link(dve.memset(Mpre[:, 0, :], 0.0))
            settle()
            link(dve.tensor_tensor(Msel[:, :, :], Msel[:, :, :], validb, ALU.mult))
            for t in range(NT):
                settle()
                pre = dve.tensor_tensor(Mpre[:, t + 1, :], Mpre[:, t, :], Msel[:, t, :], ALU.add)
                if t == NT - 1:
                    pre.then_inc(s_msel, 1)
                else:
                    link(pre)
            b = bank()
            dve.tensor_copy(rank[:, :, :], b[:, 0:(NT + 1) * E].rearrange("p (t e) -> p t e", e=E)).then_inc(dve_done, 1)
            dve.wait_ge(dve_done, n[0])
            dve.wait_ge(s_zero, 2)
            link(dve.tensor_tensor(cmpk[:, :, :], rank[:, NT, :].unsqueeze(2).to_broadcast([P, E, NT]),
                                   kval[:, :].unsqueeze(1).to_broadcast([P, E, NT]), ALU.is_gt))
            link(dve.memset(cum[:, 0:1], 0.0))
            settle()
            link(dve.tensor_reduce(cnt[:, :], cmpk[:, :, :], AX, ALU.add))
            settle()
            link(dve.tensor_scalar(cnt[:, :], cnt[:, :], 1.0, None, ALU.max))
            for e in range(E):
                settle()
                link(dve.tensor_tensor(cum[:, e + 1:e + 2], cum[:, e:e + 1], cnt[:, e:e + 1], ALU.add))
            settle()
            link(dve.tensor_copy(cumI[:, :], cum[:, :]))
            link(dve.tensor_scalar(lastf[:, :], cum[:, 1:E + 1], -1.0, None, ALU.add))
            link(dve.scalar_tensor_tensor(posf[:, :, :], cum[:, 0:E].unsqueeze(1).to_broadcast([P, NT, E]), float(P),
                                          rank[:, 0:NT, :], ALU.mult, ALU.add))
            settle()
            link(dve.tensor_tensor(eq[:, :, :], posf[:, :, :], oh1[:, :, :], ALU.mult))
            link(dve.tensor_tensor(probs2[:, :, :], posf[:, :, :], oh2[:, :, :], ALU.mult))
            settle()
            link(dve.tensor_reduce(pos[:, 0, :], eq[:, :, :], AX, ALU.add))
            link(dve.tensor_reduce(pos[:, 1, :], probs2[:, :, :], AX, ALU.add))
            settle()
            link(dve.tensor_copy(lastI[:, :], lastf[:, :]))
            settle()
            dve.tensor_copy(posI[:, :, :], pos[:, :, :]).then_inc(s_route, 1)

            dve.wait_ge(s_atr, 16 * NT)
            for j in range(NT + 1):
                if j < NT:
                    link(dve.tensor_scalar(lowbits[:, j % 2, :], ATr[:, j, :].bitcast(U32), 0xFFF, None,
                                           ALU.bitwise_and))
                if j:
                    link(dve.tensor_reduce(lowmax[:, j - 1:j], lowbits[:, (j - 1) % 2, :], AX, ALU.max))
                settle()
            dve.tensor_reduce(lowsum[:, :], lowmax[:, :], AX, ALU.max).then_inc(s_low, 1)
            b = bank()
            dve.tensor_scalar(lowsum[:, :], b[:, 0:1], 1.0, None, ALU.min).then_inc(dve_done, 1)
            dve.wait_ge(dve_done, n[0])
            dve.tensor_copy(wideI[:, :], lowsum[:, :]).then_inc(s_wide, 1)

            slots = dve.value_load(cumI[0:1, E:E + 1], min_val=E, max_val=SLOTS)

            def output(s):
                dve.wait_ge(s_y, s + 1)
                dve.tensor_copy(yrow[:, :], banks[5][:, 0:D]).then_inc(s_yd, 1)

            output(0)
            with dve.Fori(1, slots) as s:
                dve.wait_ge(s_yw, s * 16)
                output(s)
            dve.wait_ge(s_yg, 16 * 2 * NT)
            for c, p in ((0, p1), (1, p2)):
                for t in range(NT):
                    r = rows(t)
                    mix = dve.scalar_tensor_tensor(X[0:r, t, :], yg[0:r, c, t, :], p[0:r, t:t + 1], X[0:r, t, :],
                                                   ALU.mult, ALU.add)
                    if c and t == NT - 1:
                        mix.then_inc(s_mix, 1)
                        dve.wait_ge(s_mix, 1)
                    else:
                        link(mix)
                settle()

            layer_norm()
            dve.wait_ge(s_norm, 3 * NT)
            for t in range(NT):
                link(dve.tensor_copy(Np[:, 0, t, :], Nn[:, t, :]))
            settle()
            for t in range(NT):
                dve.tensor_tensor(Np[:, 1, t, :], Nn[:, t, :], Np[:, 0, t, :].bitcast(F32),
                                  ALU.subtract).then_inc(s_np, 1)
            dve.wait_ge(s_cw, 16 * 3)
            link(dve.tensor_tensor(X[:, :, :], X[:, :, :], cb3[:, :].unsqueeze(1).to_broadcast([P, NT, D]), ALU.add))
            pairs = [0]

            def split(dst, nf):
                for c0, cw in CHUNKS:
                    for f in range(nf):
                        i = pairs[0]
                        dve.wait_ge(act_done, mark["gcn_act"] + i + 1)
                        link(dve.tensor_copy(dst[:, 0, f, c0:c0 + cw], hh[i % 4][:, 0:cw]))
                        settle()
                        dve.tensor_tensor(dst[:, 1, f, c0:c0 + cw], hh[i % 4][:, 0:cw],
                                          dst[:, 0, f, c0:c0 + cw].bitcast(F32), ALU.subtract).then_inc(s_pair, 1)
                        pairs[0] += 1

            def split_rows(Y, w):
                for t in range(NT):
                    r = rows(t)
                    b = bank()
                    link(dve.tensor_copy(Y[0:r, 0, t, :], b[0:r, 0:w]))
                    settle()
                    dve.tensor_tensor(Y[0:r, 1, t, :], b[0:r, 0:w], Y[0:r, 0, t, :].bitcast(F32),
                                      ALU.subtract).then_inc(dve_done, 1)

            split(Z1T, KD)
            split(H1T, HK)
            split_rows(Y2, HID)
            split(H2T, HK)
            split_rows(Y3, D)
            settle()
            for t in range(NT):
                r = rows(t)
                b = bank()
                dve.tensor_tensor(X[0:r, t, :], b[0:r, 0:D], X[0:r, t, :], ALU.add).then_inc(dve_done, 1)
            dve.wait_ge(dve_done, n[0])

            layer_norm()
            b = bank()
            dve.tensor_copy(gT[:, :, :], b[:, 0:KD * E2].rearrange("p (k e) -> p k e", e=E2)).then_inc(dve_done, 1)
            top2(2)
            settle()
            link(dve.tensor_tensor(rtmp[:, :], p1[:, :], p2[:, :], ALU.add))
            link(dve.tensor_tensor(oh1[:, :, :], oh1[:, :, :], over_e(p1[:, :]), ALU.mult))
            link(dve.tensor_tensor(oh2[:, :, :], oh2[:, :, :], over_e(p2[:, :]), ALU.mult))
            settle()
            link(dve.tensor_scalar(rtmp[:, :], rtmp[:, :], 1e-20, None, ALU.add))
            link(dve.tensor_tensor(oh1[:, :, :], oh1[:, :, :], oh2[:, :, :], ALU.add))
            settle()
            link(dve.reciprocal(rtmp[:, :], rtmp[:, :]))
            settle()
            dve.tensor_tensor(comb[:, :, :], oh1[:, :, :], over_e(rtmp[:, :]), ALU.mult).then_inc(s_comb, 1)
            dve.wait_ge(s_comb, 1)
            for t0 in range(0, NT, 4):
                w = min(4, NT - t0) * P
                b = bank()
                dve.tensor_copy(combT[:, t0 * P:t0 * P + w], b[0:E2, 0:w]).then_inc(dve_done, 1)
            for e in range(E2):
                for t in range(NT):
                    r = rows(t)
                    if e:
                        dve.wait_ge(dve_done, n[0] - NT + 1)
                    b = bank()
                    dve.scalar_tensor_tensor(X[0:r, t, :], b[0:r, 0:D], comb[0:r, t, e:e + 1], X[0:r, t, :],
                                             ALU.mult, ALU.add).then_inc(dve_done, 1)
            for t in range(NT):
                r = rows(t)
                dve.wait_ge(dve_done, n[0] - NT + 1)
                b = bank()
                last = dve.tensor_tensor(X[0:r, t, :], b[0:r, 0:D], X[0:r, t, :], ALU.add)
                last.then_inc(dve_done if t < NT - 1 else s_fin, 1)


_INS = ['x', 'adj', 'L0_gnn_W', 'L0_gnn_a', 'L0_gnn_wtrans', 'L0_ffn_Wr', 'L0_ffn_W1', 'L0_ffn_W2', 'L1_gnn_W1',
        'L1_gnn_b1', 'L1_gnn_W2', 'L1_gnn_b2', 'L1_gnn_W3', 'L1_gnn_b3', 'L1_ffn_gate_w', 'L1_ffn_w1', 'L1_ffn_b1',
        'L1_ffn_w2', 'L1_ffn_b2', 'L1_ffn_sw1', 'L1_ffn_sb1', 'L1_ffn_sw2', 'L1_ffn_sb2']


def kernel(**inputs):
    import numpy as _np
    import concourse.bacc as _bacc
    from concourse import mybir as _mybir
    from concourse.bass_utils import run_bass_kernel_spmd as _run

    nc = _bacc.Bacc("TRN2", target_bir_lowering=False, num_devices=1)
    arrays, args = {}, []
    for name in _INS:
        a = _np.ascontiguousarray(inputs[name])
        arrays[f"in_{name}_dram"] = a
        args.append(nc.dram_tensor(f"in_{name}_dram", a.shape, _mybir.dt.from_np(a.dtype), kind="ExternalInput").ap())
    shape = inputs['x'].shape
    args.append(nc.dram_tensor("out_dram", shape, _mybir.dt.float32, kind="ExternalOutput").ap())
    gat_moe_gcn_moe_kernel(nc, *args)
    r = _run(nc, [arrays], core_ids=[0])
    return r.results[0]["out_dram"]
```

```python
import concourse.bass as bass
from concourse import mybir
from contextlib import ExitStack

F32 = mybir.dt.float32
F32R = mybir.dt.float32r
I32 = mybir.dt.int32
U32 = mybir.dt.uint32
ALU = mybir.AluOpType
ACT = mybir.ActivationFunctionType
AX = mybir.AxisListType.X


def gat_moe_gcn_moe_kernel(nc, x, adj, gat_W, gat_a, gat_wtrans, moe_Wr, moe_W1, moe_W2,
                           gcn_W1, gcn_b1, gcn_W2, gcn_b2, gcn_W3, gcn_b3,
                           ffn_gate, ffn_w1, ffn_b1, ffn_w2, ffn_b2, ffn_sw1, ffn_sb1, ffn_sw2, ffn_sb2, out):
    P = 128
    N, D = x.shape
    NT = -(-N // P)
    NP = NT * P
    KD = D // P
    E, _, F = moe_W1.shape
    FK = F // P
    HID = gcn_W1.shape[1]
    HK = HID // P
    E2, _, DF = ffn_w1.shape
    SH = ffn_sw1.shape[1]
    SK = SH // P
    EPS = 1e-5
    BIG = 1e30
    ALPHA = 0.2
    RING = 3
    NC = 3
    CW = -(-N // NC)
    CW += CW % 2
    CHUNKS = [(c * CW, min(CW, N - c * CW)) for c in range(NC)]
    GROUPS = [(0, 3), (3, 3), (6, 3), (9, 2)]
    LN_GROUPS = [(0, 4), (4, 8), (8, NT)]
    GW = 3 * P
    SLOTS = (2 * N + E * (P - 1)) // P
    PSB = 512
    full = N // P
    tail = N - full * P

    def rows(t):
        return min(P, N - t * P)

    xs = nc.dram_tensor("routed_rows", ((SLOTS + 1) * P, D), F32).ap()
    at_dram = nc.dram_tensor("adj_transposed", (P, NT, N), F32).ap()
    ys = nc.dram_tensor("expert_rows", (SLOTS * P, D), F32).ap()

    ctx = ExitStack()
    with ctx:
        def sb(name, shape, dt=F32):
            return ctx.enter_context(nc.sbuf_tensor(name, shape, dt))

        def sem(name):
            return ctx.enter_context(nc.semaphore(name))

        X = sb("X", [P, NT, D])
        Nn_at = -(-nc.sbuf_base // 32) * 32
        Nn = sb("Nn", [P, NT, D])
        NTr_at = Nn_at + 4 * NT * D
        NTr = sb("NTr", [P, KD, NP])
        assert nc.sbuf_base >= NTr_at + 4 * KD * NP
        ident = sb("ident", [P, P])
        ones = sb("ones", [P, P])
        upper = sb("upper", [P, P])
        stats = sb("stats", [P, NT, 6])
        mv = sb("mv", [P, NT, 2])
        rstd = sb("rstd", [P, NT])
        neghalf = sb("neghalf", [P, NT])
        logits = sb("logits", [P, NT, E])
        probs = sb("probs", [P, NT, E])
        eq = sb("eq", [P, NT, E])
        oh1 = sb("oh1", [P, NT, E])
        oh2 = sb("oh2", [P, NT, E])
        probs2 = sb("probs2", [P, NT, E])
        rtmp = sb("rtmp", [P, NT])
        p1 = sb("p1", [P, NT])
        p2 = sb("p2", [P, NT])
        Wr = sb("Wr", [P, KD, E])
        rev = sb("rev", [P, E])
        lowsum = sb("lowsum", [P, 1])
        wideI = sb("wideI", [P, 1], I32)
        valid = sb("valid", [P, NT])
        arena = nc.sbuf_base
        arena = -(-arena // 64) * 64
        AT_at = arena
        AT = nc.alloc_sbuf_tensor_at("AT", [P, NT, N], F32, offset=arena)
        ATr = nc.alloc_sbuf_tensor_at("ATr", [P, NT, N], F32R, offset=arena)
        arena += -(-4 * NT * N // 64) * 64

        class Place:
            def __init__(self, at):
                self.at = at

            def __call__(self, name, shape, dt=F32):
                n = 4
                for s in shape[1:]:
                    n *= s
                t = nc.alloc_sbuf_tensor_at(name, shape, dt, offset=self.at)
                self.at += -(-n // 32) * 32
                return t

        pl = Place(arena)
        adjn = [pl(f"adjn{i}", [P, NP]) for i in range(RING)]
        negn = [pl(f"negn{i}", [P, N]) for i in range(2)]
        junk = pl("junk", [P, N], mybir.dt.bfloat16)
        scan_end = pl.at
        gW = pl("gW", [P, KD, D])
        gWT = pl("gWT", [P, KD, D])
        a2 = pl("a2", [P, 2, KD])
        wtr = pl("wtr", [P, KD, 2, D])
        Wa = pl("Wa", [P, KD, 2])
        Wh = pl("Wh", [P, NT, 2])
        Wrow = pl("Wrow", [P, N])
        mx = pl("mx", [P, 2, NT])
        ms = pl("ms", [P, 2, NT])
        m2 = pl("m2", [P, 2, NT])
        has = pl("has", [P, 2, NT])
        qcol = pl("qcol", [P, 4, NT])
        kcol = pl("kcol", [P, 4, NT])
        after_scan = Place(pl.at)
        pa = Place(arena)
        ee = [pa(f"ee{i}", [P, 4, GW]) for i in range(2)]
        mask = pa("mask", [P, GW])
        qq = pa("qq", [P, 2, GW])
        pp = [pa(f"pp{i}", [P, 2, GW]) for i in range(2)]
        assert pa.at <= scan_end
        G = after_scan("G", [P, NT, 2, D + 2])
        qrow = after_scan("qrow", [P, 4, N])
        Cs = after_scan("Cs", [P, 2, D])
        den = after_scan("den", [P, 3, 2])
        emp = after_scan("emp", [P, 3, 2])
        V = after_scan("V", [P, 3, D])
        zero = after_scan("zero", [P, D])
        V2 = after_scan("V2", [P, 3, D])
        Vm = after_scan("Vm", [P, NT, D])

        pb = Place(arena)
        W1b = pb("W1b", [P, 2, KD * F])
        W2b = pb("W2b", [P, 2, FK * D])
        LT1 = pb("LT1", [E, N])
        Msel = pb("Msel", [P, NT, E])
        Mpre = pb("Mpre", [P, NT + 1, E])
        rank = pb("rank", [P, NT + 1, E])
        kval = pb("kval", [P, NT])
        cmpk = pb("cmpk", [P, E, NT])
        cnt = pb("cnt", [P, E])
        cum = pb("cum", [P, E + 1])
        cumI = pb("cumI", [P, E + 1], I32)
        lastf = pb("lastf", [P, E])
        lastI = pb("lastI", [P, E], I32)
        posf = pb("posf", [P, NT, E])
        pos = pb("pos", [P, 2, NT])
        posI = pb("posI", [P, 2, NT], I32)
        lowmax = pb("lowmax", [P, NT])
        xg = pb("xg", [P, D])
        xgT = pb("xgT", [P, KD, P])
        hT = pb("hT", [P, FK, P])
        yrow = pb("yrow", [P, D])
        lowbits = nc.alloc_sbuf_tensor_at("lowbits", [P, 2, N], U32, offset=pb.at)
        yg = pb("yg", [P, 2, NT, D])
        Np = pb("Np", [P, 2, NT, D], F32R)

        pc = Place(arena)
        cW2 = pc("cW2", [P, 2, HK, HID], F32R)
        cW3 = pc("cW3", [P, 2, HK, D], F32R)
        cb1 = pc("cb1", [P, HK])
        cb2 = pc("cb2", [P, HK])
        cb3 = pc("cb3", [P, D])
        first, second = pc.at, pc.at + 4 * 2 * NT * HID
        Z1T = pc("Z1T", [P, 2, KD, N], F32R)
        raw1 = pc("raw1", [P, KD, HID])
        raw2 = pc("raw2", [P, HK, HID])
        raw3 = pc("raw3", [P, HK, D])
        assert pc.at <= second
        Y2 = nc.alloc_sbuf_tensor_at("Y2", [P, 2, NT, HID], F32R, offset=first)
        Y3 = nc.alloc_sbuf_tensor_at("Y3", [P, 2, NT, D], F32R, offset=first)
        pc.at = second
        H1T = pc("H1T", [P, 2, HK, N], F32R)
        H2T = nc.alloc_sbuf_tensor_at("H2T", [P, 2, HK, N], F32R, offset=second)
        cW1 = nc.alloc_sbuf_tensor_at("cW1", [P, 2, KD, HID], F32R, offset=NTr_at)
        hh = [nc.alloc_sbuf_tensor_at(f"hh{i}", [P, CW], F32, offset=Nn_at + 4 * PSB * i) for i in range(4)]

        pd = Place(arena)
        gw = pd("gw", [E2, D])
        gT = pd("gT", [P, KD, E2])
        LT2 = pd("LT2", [E2, N])
        dW1 = pd("dW1", [P, E2, KD, DF])
        dW2 = pd("dW2", [P, E2, D])
        db1 = pd("db1", [P, E2])
        db2 = pd("db2", [E2 + 1, D])
        sW1 = pd("sW1", [P, KD, SH])
        sW2 = pd("sW2", [P, SK, D])
        sb1 = pd("sb1", [P, SK])
        comb = pd("comb", [P, NT, E2 + 1])
        combT = pd("combT", [E2 + 1, NP])
        dW1p = pd("dW1p", [P, 2, E2, KD, DF], F32R)
        dW2p = pd("dW2p", [P, 2, E2, D], F32R)
        sW1p = pd("sW1p", [P, 2, KD, SH], F32R)
        sW2p = pd("sW2p", [P, 2, SK, D], F32R)
        hE = [pd(f"hE{i}", [P, 2, N], F32R) for i in range(2)]
        pe4 = Place(AT_at)
        NTp = pe4("NTp", [P, 2, KD, NP], F32R)
        hS = pe4("hS", [P, 2, SK, N], F32R)
        hf = [pe4(f"hf{i}", [P, CW]) for i in range(8)]
        assert pe4.at <= arena

        psum = ctx.enter_context(nc.psum_tensor("psum", [P, 8, PSB], F32))
        banks = [psum[:, i, :] for i in range(8)]
        psum_flat = psum[:, :, :].rearrange("p b n -> p (b n)")
        act_banks, dve_banks = banks[0:4], banks[4:8]

        s_x = [sem(f"x_loaded{g}") for g in range(len(LN_GROUPS))]
        s_gw = sem("gat_weights_loaded")
        s_gw2 = sem("gat_score_weights_loaded")
        s_adj = [sem(f"adj_rows_loaded{i}") for i in range(RING)]
        s_zero = sem("zeros_ready")
        s_ysz = sem("expert_rows_zeroed")
        s_xsz = sem("routed_rows_zeroed")
        s_id = sem("constant_steps")
        s_const = sem("constants_ready")
        s_dw2 = sem("dense_last_bias_loaded")
        s_fin = sem("result_ready")
        s_pad = sem("pads_cleared")
        act_full = sem("act_bank_full")
        act_done = sem("act_bank_done")
        dve_full = sem("dve_bank_full")
        dve_done = sem("dve_bank_done")
        chain = sem("vector_chain")
        s_var = sem("variance_ready")
        s_rstd = sem("inverse_deviation_ready")
        s_norm = sem("norm_tiles_ready")
        s_scan = sem("adj_tile_scanned")
        s_qcol = sem("query_columns_ready")
        s_e = sem("branch_exponentials_ready")
        s_q = sem("branches_joined")
        s_p = sem("attention_weights_ready")
        s_used = sem("attention_weights_used")
        s_attd = sem("attention_group_done")
        s_vm = sem("elu_argument_ready")
        s_ve = sem("elu_exp_ready")
        s_x1 = sem("attention_added")
        s_we = [sem(f"expert_weights_loaded{i}") for i in range(2)]
        s_wfree = sem("expert_weights_free")
        s_wrdy = sem("expert_weights_ready")
        s_wr = sem("router_weights_loaded")
        s_lc = sem("logits_centred")
        s_le = sem("logits_exp")
        s_msel = sem("selection_ready")
        s_route = sem("routes_ready")
        s_scat = sem("rows_scattered")
        s_xg = sem("slot_rows_loaded")
        s_xt = sem("slot_rows_transposed")
        s_xtd = sem("slot_transpose_copied")
        s_h = sem("hidden_sums_ready")
        s_hd = sem("hidden_gelu_ready")
        s_y = sem("slots_finished")
        s_yd = sem("slot_output_copied")
        s_yw = sem("slot_output_written")
        s_yall = sem("all_slots_written")
        s_yg = [sem(f"expert_rows_gathered{g}") for g in range(len(LN_GROUPS))]
        s_ats = sem("adj_transposed_stored")
        s_atr = sem("adj_words_loaded")
        s_wide = sem("adj_width_known")
        s_low = sem("adj_low_bits_ready")
        s_cwr = [sem(f"gcn_weights{i}_loaded") for i in range(3)]
        s_cwh = sem("gcn_weights_high_parts")
        s_cws = sem("gcn_weights_split")
        s_np = sem("norm_split")
        s_pair = sem("hidden_chunks_split")
        s_cw = sem("gcn_weights_loaded")
        s_mix = sem("mixture_added")
        s_dw = sem("dense_weights_loaded")
        s_dwh = sem("dense_weights_high_parts")
        s_dws = sem("dense_weights_split")
        s_ntp = sem("norm_transpose_split")
        s_hhi = sem("hidden_high_parts")
        s_hlo = sem("hidden_parts_ready")
        s_gwt = sem("gate_loaded")
        s_comb = sem("combine_weights_ready")
        s_out = sem("output_written")

        dense_pieces = [(dW1p[:, :, 0:2, :, :], dW1[:, 0:2, :, :]), (sW1p[:, :, :, :], sW1[:, :, :]),
                        (dW2p[:, :, 0:2, :], dW2[:, 0:2, :]), (dW1p[:, :, 2:E2, :, :], dW1[:, 2:E2, :, :]),
                        (dW2p[:, :, 2:E2, :], dW2[:, 2:E2, :]), (sW2p[:, :, :, :], sW2[:, :, :])]
        hidden_order = [("e", e) for e in range(2)] + [("s", f) for f in range(SK)] + [("e", e) for e in range(2, E2)]

        def hidden_pair(kind, k):
            return hE[k % 2] if kind == "e" else hS[:, :, k, :]

        hidden_jobs = [(kind, k, c0, cw) for kind, k in hidden_order for c0, cw in CHUNKS]

        def hidden_done(kind, k):
            return NC * (hidden_order.index((kind, k)) + 1)

        block = ctx.enter_context(nc.Block())
        mark = {}

        @block.tensor
        def _(pe):
            na = [0]
            nv = [0]

            def act_bank():
                n = na[0]
                if n >= 4:
                    pe.wait_ge(act_done, n - 3)
                return act_banks[n % 4]

            def to_act(mm):
                na[0] += 1
                mm.then_inc(act_full, 1)
                return na[0]

            def dve_bank():
                n = nv[0]
                if n >= 4:
                    pe.wait_ge(dve_done, n - 3)
                return dve_banks[n % 4]

            def to_dve(mm):
                nv[0] += 1
                mm.then_inc(dve_full, 1)
                return nv[0]

            def transpose_norm(layer, amid=None):
                for q in range(-(-NT // 2)):
                    if q == 3 and amid:
                        amid()
                    tiles = range(2 * q, min(2 * q + 2, NT))
                    pe.wait_ge(s_norm, NT * layer + tiles[-1] + 1)
                    b = act_bank()
                    for i, t in enumerate(tiles):
                        for k in range(KD):
                            mm = pe.transpose(b[:, (k * 2 + i) * P:(k * 2 + i + 1) * P],
                                              Nn[:, t, k * P:(k + 1) * P], ident[:, :])
                    last = to_act(mm)
                return last

            def router(W, LT, first):
                for c0, cw in CHUNKS:
                    pe.wait_ge(act_done, first + -(-(c0 + cw) // (2 * P)))
                    b = act_bank()
                    for k in range(KD):
                        mm = pe.matmul(b[0:E, 0:cw], W[:, k, :], NTr[:, k, c0:c0 + cw],
                                       start=(k == 0), stop=(k == KD - 1))
                    j = to_act(mm)
                pe.wait_ge(act_done, j)
                b = dve_bank()
                for t in range(NT):
                    r = rows(t)
                    mm = pe.transpose(b[0:r, t * E:(t + 1) * E], LT[:, t * P:t * P + r], ident[0:E, 0:E])
                return to_dve(mm)

            def transpose_W():
                pe.wait_ge(s_gw, 16 * 2)
                pe.wait_ge(s_gw2, 16 * 2)
                b = act_bank()
                for fo in range(KD):
                    for fi in range(KD):
                        mm = pe.transpose(b[:, (fo * KD + fi) * P:(fo * KD + fi + 1) * P],
                                          gW[:, fi, fo * P:(fo + 1) * P], ident[:, :])
                mark["W"] = to_act(mm)

            pe.wait_ge(s_const, 1)
            j = transpose_norm(0, transpose_W)
            pe.wait_ge(act_done, mark["W"])
            b = dve_bank()
            for fi in range(KD):
                for fo in range(KD):
                    mm = pe.matmul(b[:, 2 * fi:2 * fi + 2], gWT[:, fo, fi * P:(fi + 1) * P], a2[:, :, fo],
                                   start=(fo == 0), stop=(fo == KD - 1))
            to_dve(mm)
            pe.wait_ge(act_done, j)
            pe.wait_ge(dve_done, nv[0])
            for c0, cw in CHUNKS:
                b = act_bank()
                for k in range(KD):
                    mm = pe.matmul(b[:, 0:cw], Wa[:, k, 1:2].to_broadcast([P, P]), NTr[:, k, c0:c0 + cw],
                                   start=(k == 0), stop=(k == KD - 1))
                mark["row"] = to_act(mm)

            def scores():
                b = dve_bank()
                for t in range(NT):
                    r = rows(t)
                    for k in range(KD):
                        mm = pe.matmul(b[0:r, 2 * t:2 * t + 2], NTr[:, k, t * P:t * P + r], Wa[:, k, :],
                                       start=(k == 0), stop=(k == KD - 1))
                to_dve(mm)

            sums = dve_banks[(nv[0] + 1) % 4]

            def sum_G(t):
                r = rows(t)
                pe.wait_ge(act_done, mark["G", t])
                return pe.matmul(sums[:, :], ones[0:r, :], G[0:r, t, :, 0:D], start=(t == 0), stop=(t == NT - 1))

            for t in range(NT):
                r = rows(t)
                pe.wait_ge(s_adj[t % RING], 16 * (t // RING + 1))
                for j0 in range(0, NT, 4):
                    js = range(j0, min(j0 + 4, NT))
                    b = act_bank()
                    for i, j in enumerate(js):
                        mm = pe.transpose(b[:, i * P:i * P + r], adjn[t % RING][0:r, j * P:(j + 1) * P],
                                          ident[0:r, 0:r])
                    mark["adjT", t] = to_act(mm)
                b = act_bank()
                for k in range(KD):
                    mm = pe.matmul(b[0:r, :], NTr[:, k, t * P:t * P + r], wtr[:, k, :, :],
                                   start=(k == 0), stop=(k == KD - 1))
                mark["G", t] = to_act(mm)
                if t:
                    sum_G(t - 1)
                if t == NT // 2:
                    scores()
            to_dve(sum_G(NT - 1))
            pe.wait_ge(s_qcol, 1)
            for v in (0, 2, 1, 3):
                for t0 in range(0, NT, 4):
                    b = act_bank() if v < 2 else dve_bank()
                    for t in range(t0, min(t0 + 4, NT)):
                        r = rows(t)
                        mm = pe.transpose(b[:, (t - t0) * P:(t - t0) * P + r],
                                          qcol[0:r, v, t:t + 1].to_broadcast([r, P]), ident[0:r, 0:r])
                    if v < 2:
                        to_act(mm)
                    else:
                        mark["qrow"] = to_dve(mm)
            pe.wait_ge(act_done, na[0])
            pe.wait_ge(dve_done, nv[0])
            step = 0
            for g, (t0, nt) in enumerate(GROUPS):
                if g:
                    pe.wait_ge(s_attd, g)
                for j in range(NT):
                    r = rows(j)
                    step += 1
                    pe.wait_ge(s_p, step)
                    for i in range(nt):
                        q = rows(t0 + i)
                        for s in range(2):
                            mm = pe.matmul(banks[2 * i + s][0:q, 0:D + 1], pp[(step - 1) % 2][0:r, s, i * P:i * P + q],
                                           G[0:r, j, s, 0:D + 1], start=(j == 0), stop=(j == NT - 1))
                    mm.then_inc(s_used, 1)
            pe.wait_ge(s_attd, len(GROUPS))

            first = na[0]
            transpose_norm(1)
            pe.wait_ge(s_wr, 16)
            router(Wr, LT1, first)
            pe.wait_ge(s_msel, 1)
            b = dve_bank()
            pe.matmul(b[:, 0:(NT + 1) * E], ones[:, :], Mpre[:, :, :], start=True, stop=False)
            mm = pe.matmul(b[:, 0:NT * E], upper[:, :], Msel[:, :, :], start=False, stop=True)
            to_dve(mm)
            pe.wait_ge(s_low, 1)
            b = dve_bank()
            to_dve(pe.matmul(b[:, 0:1], ones[:, :], lowsum[:, :], start=True, stop=True))
            pe.wait_ge(act_done, na[0])
            pe.wait_ge(dve_done, nv[0])
            pe.wait_ge(s_route, 1)

            def rows_T(s):
                pe.wait_ge(s_xg, s * 16 + 16)
                for k in range(KD):
                    mm = pe.transpose(banks[0][:, k * P:(k + 1) * P], xg[:, k * P:(k + 1) * P], ident[:, :])
                mm.then_inc(s_xt, 1)

            def up(s, e):
                pe.wait_ge(s_xtd, s + 1)
                for h in range(2):
                    for i in range(4):
                        f = 4 * h + i
                        for k in range(KD):
                            mm = pe.matmul(psum_flat[:, bass.ds((s % 2) * (2 * PSB) + (1 + h) * PSB + i * P, P)],
                                           W1b[:, e % 2, k * F + f * P:k * F + (f + 1) * P], xgT[:, k, :],
                                           start=(k == 0), stop=(k == KD - 1))
                    mm.then_inc(s_h, 1)

            def down(s, e):
                for f in range(FK):
                    if f % 4 == 0:
                        pe.wait_ge(s_hd, s * 2 + (f // 4 + 1))
                    if f == 0:
                        pe.wait_ge(s_yd, s) if not isinstance(s, int) or s else None
                    mm = pe.matmul(banks[5][:, 0:D], hT[:, f, :], W2b[:, e % 2, f * D:(f + 1) * D],
                                   start=(f == 0), stop=(f == FK - 1))
                mm.then_inc(s_y, 1)

            lasts = [pe.value_load(lastI[0:1, e:e + 1], min_val=e, max_val=SLOTS - 1) for e in range(E)]
            rows_T(0)
            pe.wait_ge(s_wrdy, 1)
            up(0, 0)
            rows_T(1)
            for e in range(E):
                begin, last = lasts[e - 1] + 1 if e else 0, lasts[e]
                with pe.If(last > begin):
                    with pe.Fori(begin, last) as s:
                        up(s + 1, e)
                        rows_T(s + 2)
                        down(s, e)
                if e + 1 < E:
                    pe.wait_ge(s_wrdy, e + 2)
                    up(last + 1, e + 1)
                    rows_T(last + 2)
                down(last, e)

            mark["gcn_act"] = na[0]
            pe.wait_ge(s_wide, 1)
            wide = pe.value_load(wideI[0:1, 0:1], min_val=0, max_val=1)
            np_ = [0]

            def three(out, a, b, start, stop):
                pe.matmul(out, a(0), b(0), start=start, stop=False)
                pe.matmul(out, a(0), b(1), start=False, stop=False)
                return pe.matmul(out, a(1), b(0), start=False, stop=stop)

            def over_adj(stage):
                at = (na[0], nv[0], np_[0])
                with pe.If(wide == 0):
                    stage(ATr, lambda v: v)
                with pe.Else():
                    na[0], nv[0], np_[0] = at
                    stage(ATr[:, :, :].bitcast(F32), lambda v: v.bitcast(F32))

            def features_times_adj(W, nf):
                def stage(A, view):
                    for c0, cw in CHUNKS:
                        for f in range(nf):
                            b = act_bank()
                            for j in range(NT):
                                r = rows(j)
                                if W is Np and c0 == 0 and f == 0:
                                    pe.wait_ge(s_np, j + 1)
                                for part in range(2):
                                    mm = pe.matmul(b[:, 0:cw], view(W[0:r, part, j, f * P:(f + 1) * P]),
                                                   A[0:r, j, c0:c0 + cw], start=(j == 0 and part == 0),
                                                   stop=(j == NT - 1 and part == 1))
                            to_act(mm)
                            np_[0] += 1
                return stage

            def times_weights(HT_, W, wn, nk):
                for t in range(NT):
                    r = rows(t)
                    b = dve_bank()
                    for k in range(nk):
                        mm = three(b[0:r, 0:wn], lambda p: HT_[:, p, k, t * P:t * P + r], lambda p: W[:, p, k, :],
                                   k == 0, k == nk - 1)
                    to_dve(mm)

            over_adj(features_times_adj(Np, KD))
            pe.wait_ge(s_pair, np_[0])
            pe.wait_ge(s_cws, 1)
            for c0, cw in CHUNKS:
                for h in range(HK):
                    b = act_bank()
                    for k in range(KD):
                        mm = three(b[:, 0:cw], lambda p: cW1[:, p, k, h * P:(h + 1) * P],
                                   lambda p: Z1T[:, p, k, c0:c0 + cw], k == 0, k == KD - 1)
                    to_act(mm)
                    np_[0] += 1
            pe.wait_ge(s_pair, np_[0])
            pe.wait_ge(s_cws, 3)
            times_weights(H1T, cW2, HID, HK)
            pe.wait_ge(dve_done, nv[0])
            over_adj(features_times_adj(Y2, HK))
            pe.wait_ge(s_pair, np_[0])
            times_weights(H2T, cW3, D, HK)
            pe.wait_ge(dve_done, nv[0])

            def adj_times_rows(A, view):
                for t in range(NT):
                    q = rows(t)
                    b = dve_bank()
                    for j in range(NT):
                        r = rows(j)
                        for part in range(2):
                            mm = pe.matmul(b[0:q, 0:D], A[0:r, j, t * P:t * P + q], view(Y3[0:r, part, j, :]),
                                           start=(j == 0 and part == 0), stop=(j == NT - 1 and part == 1))
                    to_dve(mm)

            over_adj(adj_times_rows)
            mark["gcn_last_dve"] = nv[0]

            mark["norm4"] = na[0]
            transpose_norm(3)
            pe.wait_ge(s_gwt, 16)
            b = dve_bank()
            for k in range(KD):
                mm = pe.transpose(b[:, k * E2:(k + 1) * E2], gw[0:E2, k * P:(k + 1) * P], ident[0:E2, 0:E2])
            jg = to_dve(mm)
            pe.wait_ge(dve_done, jg)
            router(gT, LT2, mark["norm4"])
            pe.wait_ge(s_ntp, -(-NT // 2))

            def up_products(W):
                for c0, cw in CHUNKS:
                    b = act_bank()
                    for k in range(KD):
                        mm = three(b[:, 0:cw], lambda p: W(p, k), lambda p: NTp[:, p, k, c0:c0 + cw],
                                   k == 0, k == KD - 1)
                    to_act(mm)

            def expert_up(e):
                pe.wait_ge(s_dws, 1 if e < 2 else 4)
                up_products(lambda p, k: dW1p[:, p, e, k, :])

            expert_up(0)
            expert_up(1)
            pe.wait_ge(s_dws, 2)
            for f in range(SK):
                up_products(lambda p, k: sW1p[:, p, k, f * P:(f + 1) * P])
            pe.wait_ge(s_comb, 1)
            for t0 in range(0, NT, 4):
                b = dve_bank()
                for t in range(t0, min(t0 + 4, NT)):
                    mm = pe.transpose(b[0:E2 + 1, (t - t0) * P:(t - t0 + 1) * P], comb[:, t, :], ident[:, :])
                jc = to_dve(mm)
            for e in range(E2):
                pe.wait_ge(s_dws, 3 if e < 2 else 5)
                pe.wait_ge(s_hlo, hidden_done("e", e))
                for t in range(NT):
                    r = rows(t)
                    b = dve_bank()
                    mm = three(b[0:r, 0:D], lambda p: hE[e % 2][:, p, t * P:t * P + r],
                               lambda p: dW2p[:, p, e, :], True, True)
                    to_dve(mm)
                mark["hE_used", e] = nv[0]
                if e + 2 < E2:
                    expert_up(e + 2)
            pe.wait_ge(s_hlo, hidden_done("s", SK - 1))
            pe.wait_ge(s_dws, 6)
            pe.wait_ge(s_dw2, 16)
            pe.wait_ge(s_dw, 16 * 8)
            pe.wait_ge(dve_done, jc)
            for t in range(NT):
                r = rows(t)
                b = dve_bank()
                for k in range(SK):
                    three(b[0:r, 0:D], lambda p: hS[:, p, k, t * P:t * P + r], lambda p: sW2p[:, p, k, :],
                          k == 0, False)
                mm = pe.matmul(b[0:r, 0:D], combT[:, t * P:t * P + r], db2[:, :], start=False, stop=True)
                to_dve(mm)

        @block.sync
        def _(sp):
            sp.wait_ge(s_pad, 1)
            for g, (a, b) in enumerate(LN_GROUPS):
                whole = min(b, full)
                sp.dma_start(X[:, a:whole, :], x[a * P:whole * P, :].rearrange("(t p) d -> p t d", p=P)).then_inc(s_x[g], 16)
            sp.dma_start(X[0:tail, full, :], x[full * P:N, :]).then_inc(s_x[-1], 16)
            sp.dma_start(wtr[:, :, 0, :], gat_wtrans[0:D, :].rearrange("(k p) d -> p k d", p=P)).then_inc(s_gw, 16)
            sp.dma_start(wtr[:, :, 1, :], gat_wtrans[D:2 * D, :].rearrange("(k p) d -> p k d", p=P)).then_inc(s_gw, 16)
            sp.dma_start(Wr[:, :, :], moe_Wr.rearrange("(k p) e -> p k e", p=P)).then_inc(s_wr, 16)
            sp.wait_ge(s_pad, 1 + RING)
            for t in range(NT):
                r = rows(t)
                if t >= RING:
                    sp.wait_ge(s_scan, t - RING + 1)
                    sp.wait_ge(act_full, mark["adjT", t - RING])
                sp.dma_start(adjn[t % RING][0:r, 0:N], adj[t * P:t * P + r, :]).then_inc(s_adj[t % RING], 16)
            sp.wait_ge(act_done, mark["adjT", NT - 1])
            for j in range(NT):
                sp.dma_start(at_dram[:, j, :], AT[:, j, :]).then_inc(s_ats, 16)
            sp.wait_ge(s_ats, 16 * NT)
            sp.wait_ge(s_p, NT * len(GROUPS))
            for j in range(NT):
                sp.dma_start(ATr[:, j, :].bitcast(F32), at_dram[:, j, :]).then_inc(s_atr, 16)
            sp.wait_ge(s_x1, 1)
            sp.wait_ge(s_route, 1)
            sp.wait_ge(s_scat, 16 * 2 * NT)
            last = sp.value_load(lastI[0:1, E - 1:E], min_val=E - 1, max_val=SLOTS - 1)
            for s in range(4):
                if s:
                    sp.wait_ge(s_xt, s)
                sp.dma_start(xg[:, :], xs[s * P:(s + 1) * P, :]).then_inc(s_xg, 16)
            sp.wait_ge(s_ysz, 16)
            sp.wait_ge(s_yd, 1)
            sp.dma_start(ys[0:P, :], yrow[:, :]).then_inc(s_yw, 16)
            with sp.Fori(1, last - 1) as s:
                sp.wait_ge(s_xt, s + 3)
                sp.dma_start(xg[:, :], xs[bass.ds(s * P + 3 * P, P), :]).then_inc(s_xg, 16)
                sp.wait_ge(s_yd, s + 1)
                sp.dma_start(ys[bass.ds(s * P, P), :], yrow[:, :]).then_inc(s_yw, 16)
            sp.wait_ge(s_yd, last)
            sp.dma_start(ys[bass.ds((last - 1) * P, P), :], yrow[:, :]).then_inc(s_yw, 16)
            sp.wait_ge(s_yd, last + 1)
            sp.dma_start(ys[bass.ds(last * P, P), :], yrow[:, :]).then_inc(s_yw, 16)
            sp.wait_ge(s_mix, 1)
            sp.dma_start(raw1[:, :, :], gcn_W1.rearrange("(k p) d -> p k d", p=P)).then_inc(s_cwr[0], 16)
            sp.dma_start(raw2[:, :, :], gcn_W2.rearrange("(k p) d -> p k d", p=P)).then_inc(s_cwr[1], 16)
            sp.dma_start(raw3[:, :, :], gcn_W3.rearrange("(k p) d -> p k d", p=P)).then_inc(s_cwr[2], 16)
            with nc.allow_non_contiguous_dma(reason="bias columns"):
                sp.dma_start(cb1[:, :], gcn_b1.rearrange("(h p) -> p h", p=P)).then_inc(s_cw, 16)
                sp.dma_start(cb2[:, :], gcn_b2.rearrange("(h p) -> p h", p=P)).then_inc(s_cw, 16)
            sp.dma_start(cb3[:, :], gcn_b3.rearrange("(o d) -> o d", o=1).to_broadcast([P, D])).then_inc(s_cw, 16)
            sp.wait_ge(dve_done, mark["gcn_last_dve"])
            sp.dma_start(gw[:, :], ffn_gate).then_inc(s_gwt, 16)
            with nc.allow_non_contiguous_dma(reason="bias columns"):
                sp.dma_start(db1[:, :], ffn_b1.rearrange("e p -> p e")).then_inc(s_dw, 16)
                sp.dma_start(sb1[:, :], ffn_sb1.rearrange("(h p) -> p h", p=P)).then_inc(s_dw, 16)
            for k in range(KD):
                sp.dma_start(dW1[:, :, k, :], ffn_w1[:, k * P:(k + 1) * P, :].rearrange("e p f -> p e f")).then_inc(s_dw, 16)
            sp.dma_start(dW2[:, :, :], ffn_w2.rearrange("e f d -> f e d")).then_inc(s_dw, 16)
            sp.dma_start(db2[0:E2, :], ffn_b2).then_inc(s_dw, 16)
            sp.dma_start(sW1[:, :, :], ffn_sw1.rearrange("(k p) d -> p k d", p=P)).then_inc(s_dw, 16)
            sp.dma_start(sW2[:, :, :], ffn_sw2.rearrange("(k p) d -> p k d", p=P)).then_inc(s_dw, 16)
            sp.dma_start(db2[E2:E2 + 1, :], ffn_sb2.rearrange("(o d) -> o d", o=1)).then_inc(s_dw2, 16)
            sp.wait_ge(s_fin, 1)
            sp.dma_start(out[0:full * P, :].rearrange("(t p) d -> p t d", p=P), X[:, 0:full, :]).then_inc(s_out, 16)
            sp.dma_start(out[full * P:N, :], X[0:tail, full, :]).then_inc(s_out, 16)
            sp.wait_ge(s_out, 32)

        @block.gpsimd
        def _(pool):
            pool.memset(X[64:P, NT - 1, :], 0.0).then_inc(s_pad, 1)
            pool.wait_ge(s_pad, 1)
            for buffer in adjn:
                pool.memset(buffer[:, N:NP], 0.0).then_inc(s_pad, 1)
            pool.memset(ident[:, :], 0.0).then_inc(s_id, 1)
            pool.memset(ones[:, :], 1.0).then_inc(s_id, 1)
            pool.memset(valid[:, :], 1.0).then_inc(s_id, 1)
            pool.memset(neghalf[:, :], -0.5).then_inc(s_id, 1)
            pool.iota(rev[:, :], pattern=[[-1, E]], base=E, channel_multiplier=0,
                      allow_small_or_imprecise_dtypes=True).then_inc(s_id, 1)
            pool.wait_ge(s_id, 5)
            pool.affine_select(out=upper[:, :], in_=ones[:, :], compare_op=ALU.is_gt, fill=0.0,
                               base=0, pattern=[[1, P]], channel_multiplier=-1).then_inc(s_id, 1)
            pool.affine_select(out=valid[:, :], in_=valid[:, :], compare_op=ALU.is_gt, fill=0.0,
                               base=N, pattern=[[-P, NT]], channel_multiplier=-1).then_inc(s_id, 1)
            pool.memset(G[:, :, :, D:D + 2], 1.0).then_inc(s_id, 1)
            pool.wait_ge(s_id, 8)
            pool.affine_select(out=ident[:, :], in_=ident[:, :], compare_op=ALU.not_equal, fill=1.0,
                               base=0, pattern=[[-1, P]], channel_multiplier=1).then_inc(s_const, 1)
            pool.dma_start(gW[:, :, :], gat_W.rearrange("(k p) d -> p k d", p=P)).then_inc(s_gw2, 16)
            with nc.allow_non_contiguous_dma(reason="two vectors"):
                pool.dma_start(a2[:, :, :].rearrange("p w k -> p (w k)"), gat_a.rearrange("(c p) o -> p (c o)", p=P)).then_inc(s_gw2, 16)
            def deviation(k, g):
                a, b = LN_GROUPS[g]
                pool.wait_ge(s_var, len(LN_GROUPS) * k + g + 1)
                pool.tensor_tensor(rstd[:, a:b], rstd[:, a:b], neghalf[:, a:b], ALU.pow).then_inc(s_rstd, 1)

            for g in range(len(LN_GROUPS)):
                deviation(0, g)
            pool.memset(zero[:, :], 0.0).then_inc(s_zero, 1)
            pool.wait_ge(s_zero, 1)
            pool.wait_ge(s_scan, NT)
            pool.dma_start(xs.rearrange("(s p) d -> p s d", p=P),
                           zero[:, :].unsqueeze(1).to_broadcast([P, SLOTS + 1, D])).then_inc(s_xsz, 16)
            pool.dma_start(ys.rearrange("(s p) d -> p s d", p=P),
                           zero[:, :].unsqueeze(1).to_broadcast([P, SLOTS, D])).then_inc(s_ysz, 16)
            pool.wait_ge(s_x1, 1)
            pool.iota(kval[:, :], pattern=[[P, NT]], base=0, channel_multiplier=0,
                      allow_small_or_imprecise_dtypes=True).then_inc(s_zero, 1)
            pool.wait_ge(s_zero, 2)
            def load_expert(e):
                pool.dma_start(W1b[:, e % 2, :].rearrange("p (k f) -> p k f", k=KD),
                               moe_W1[e, :, :].rearrange("(k p) f -> p k f", p=P)).then_inc(s_we[e % 2], 16)
                pool.dma_start(W2b[:, e % 2, :].rearrange("p (k f) -> p k f", k=FK),
                               moe_W2[e, :, :].rearrange("(k p) f -> p k f", p=P)).then_inc(s_we[e % 2], 16)

            for g in range(len(LN_GROUPS)):
                deviation(1, g)
            load_expert(0)
            load_expert(1)
            pool.wait_ge(s_xsz, 16)
            pool.wait_ge(s_route, 1)
            for t in range(NT):
                r = rows(t)
                for c in range(2):
                    pool.indirect_dma_start(out=xs, out_offset=bass.IndirectOffsetOnAxis(ap=posI[0:r, c, t:t + 1], axis=0),
                                            in_=Nn[0:r, t, :], in_offset=None).then_inc(s_scat, 16)
            for e in range(E):
                pool.wait_ge(s_we[e % 2], 32 * (e // 2 + 1))
                pool.sem_inc(s_wrdy, 1)
                if 1 <= e < E - 1:
                    upto = pool.value_load(cumI[0:1, e:e + 1], min_val=1, max_val=SLOTS)
                    pool.wait_ge(s_y, upto)
                    pool.sem_inc(s_wfree, 1)
                    load_expert(e + 1)
            slots = pool.value_load(cumI[0:1, E:E + 1], min_val=E, max_val=SLOTS)
            pool.wait_ge(s_yw, slots * 16)
            pool.sem_inc(s_yall, 1)
            for g, (a, b) in enumerate(LN_GROUPS):
                for t in range(a, b):
                    r = rows(t)
                    for c in range(2):
                        pool.indirect_dma_start(out=yg[0:r, c, t, :], out_offset=None, in_=ys,
                                                in_offset=bass.IndirectOffsetOnAxis(ap=posI[0:r, c, t:t + 1], axis=0)
                                                ).then_inc(s_yg[g], 16)
                if g:
                    deviation(2, g - 1)
            deviation(2, len(LN_GROUPS) - 1)
            pool.wait_ge(s_np, NT)
            for i, (raw, pair) in enumerate(((raw1, cW1), (raw2, cW2), (raw3, cW3))):
                pool.wait_ge(s_cwr[i], 16)
                pool.tensor_copy(pair[:, 0, :, :], raw[:, :, :]).then_inc(s_cwh, 1)
                pool.wait_ge(s_cwh, i + 1)
                pool.tensor_tensor(pair[:, 1, :, :], raw[:, :, :], pair[:, 0, :, :].bitcast(F32),
                                   ALU.subtract).then_inc(s_cws, 1)
            for g in range(len(LN_GROUPS)):
                deviation(3, g)
            for i, (pair, raw) in enumerate(dense_pieces):
                pool.wait_ge(s_dwh, i + 1)
                pool.tensor_tensor(pair[:, 1], raw, pair[:, 0].bitcast(F32), ALU.subtract).then_inc(s_dws, 1)
            for i, (kind, k, c0, cw) in enumerate(hidden_jobs):
                pair = hidden_pair(kind, k)
                pool.wait_ge(s_hhi, i + 1)
                pool.tensor_tensor(pair[:, 1, c0:c0 + cw], hf[i % 8][:, 0:cw], pair[:, 0, c0:c0 + cw].bitcast(F32),
                                   ALU.subtract).then_inc(s_hlo, 1)

        @block.scalar
        def _(act):
            n = [0]

            def bank():
                act.wait_ge(act_full, n[0] + 1)
                b = act_banks[n[0] % 4]
                n[0] += 1
                return b

            def transpose_norm(amid=None):
                for q in range(-(-NT // 2)):
                    if q == 3 and amid:
                        amid()
                    w = min(2, NT - 2 * q)
                    b = bank()
                    act.activation(NTr[:, :, 2 * q * P:(2 * q + w) * P],
                                   b[:, :].rearrange("p (k n) -> p k n", k=KD)[:, :, 0:w * P],
                                   ACT.Copy).then_inc(act_done, 1)

            def logits_rows(LT, before_last=None):
                for c0, cw in CHUNKS:
                    if c0 + cw == N and before_last:
                        before_last()
                    b = bank()
                    act.activation(LT[:, c0:c0 + cw], b[0:E, 0:cw], ACT.Copy).then_inc(act_done, 1)

            def copy_W():
                b = bank()
                act.activation(gWT[:, :, :], b[:, :].rearrange("p (k n) -> p k n", k=KD), ACT.Copy).then_inc(act_done, 1)

            transpose_norm(copy_W)
            for c0, cw in CHUNKS:
                b = bank()
                act.activation(Wrow[:, c0:c0 + cw], b[:, 0:cw], ACT.Copy).then_inc(act_done, 1)
            act.wait_ge(s_const, 1)
            for t in range(NT):
                r = rows(t)
                for j0 in range(0, NT, 4):
                    nj = min(4, NT - j0)
                    b = bank()
                    act.activation(AT[:, j0:j0 + nj, t * P:t * P + r],
                                   b[:, 0:nj * P].rearrange("p (j i) -> p j i", i=P)[:, :, 0:r],
                                   ACT.Copy).then_inc(act_done, 1)
                b = bank()
                act.activation(G[0:r, t, :, 0:D], b[0:r, :].rearrange("p (s d) -> p s d", s=2),
                               ACT.Copy).then_inc(act_done, 1)
            for v in range(2):
                for t0 in range(0, NT, 4):
                    w = min(4 * P, N - t0 * P)
                    b = bank()
                    act.activation(qrow[:, v, t0 * P:t0 * P + w], b[:, 0:w], ACT.Copy).then_inc(act_done, 1)
            act.wait_ge(act_done, n[0])
            act.wait_ge(dve_done, mark["qrow"])
            steps = [(t0, nt, j) for t0, nt in GROUPS for j in range(NT)]

            def elu_exp(g):
                t0, nt = GROUPS[g]
                act.wait_ge(s_vm, g + 1)
                act.activation(Vm[:, t0:t0 + nt, :], Vm[:, t0:t0 + nt, :], ACT.Exp).then_inc(s_ve, 1)

            for i, (t0, nt, j) in enumerate(steps):
                w = min(GW, N - t0 * P)
                if i >= 2:
                    act.wait_ge(s_q, 2 * (i - 1))
                for v in range(4):
                    act.activation(ee[i % 2][:, v, 0:w], qrow[:, v, t0 * P:t0 * P + w], ACT.Exp,
                                   bias=kcol[:, v, j:j + 1]).then_inc(s_e, 1)
                if j == 4 and t0:
                    elu_exp(i // NT - 1)
            elu_exp(len(GROUPS) - 1)
            transpose_norm()
            logits_rows(LT1)
            act.wait_ge(s_lc, 1)
            act.activation(probs[:, :, :], logits[:, :, :], ACT.Exp).then_inc(s_le, 1)

            def gelu(s):
                if not isinstance(s, int) or s:
                    act.wait_ge(s_y, s)
                for h in range(2):
                    act.wait_ge(s_h, s * 2 + (h + 1))
                    act.activation(hT[:, 4 * h:4 * h + 4, :].rearrange("p f n -> p (f n)"),
                                   psum_flat[:, bass.ds((s % 2) * (2 * PSB) + (1 + h) * PSB, PSB)],
                                   ACT.Gelu).then_inc(s_hd, 1)

            def copy_rows_T(s):
                act.wait_ge(s_xt, s + 1)
                act.activation(xgT[:, :, :], banks[0][:, 0:KD * P].rearrange("p (k n) -> p k n", k=KD),
                               ACT.Copy).then_inc(s_xtd, 1)

            act.wait_ge(s_route, 1)
            last = act.value_load(lastI[0:1, E - 1:E], min_val=E - 1, max_val=SLOTS - 1)
            copy_rows_T(0)
            copy_rows_T(1)
            gelu(0)
            copy_rows_T(2)
            with act.Fori(1, last) as s:
                gelu(s)
                copy_rows_T(s + 2)
            gelu(last)
            mark["act_before_gcn"] = n[0]
            act.wait_ge(s_np, NT)
            act.wait_ge(s_cw, 16 * 3)
            jobs = [None] * (NC * KD) + [cb1[:, h:h + 1] for _ in CHUNKS for h in range(HK)] \
                + [cb2[:, h:h + 1] for _ in CHUNKS for h in range(HK)]
            widths = [cw for _, cw in CHUNKS for _ in range(KD)] + [cw for _, cw in CHUNKS for _ in range(HK)] * 2
            for i, (bias, cw) in enumerate(zip(jobs, widths)):
                b = bank()
                if i >= 4:
                    act.wait_ge(s_pair, i - 3)
                if bias is None:
                    act.activation(hh[i % 4][:, 0:cw], b[:, 0:cw], ACT.Copy).then_inc(act_done, 1)
                else:
                    act.activation(hh[i % 4][:, 0:cw], b[:, 0:cw], ACT.Relu, bias=bias).then_inc(act_done, 1)
            transpose_norm()

            def high_part(i):
                pair, raw = dense_pieces[i]
                act.wait_ge(s_dw, 16 * 8)
                act.activation(pair[:, 0], raw, ACT.Copy).then_inc(s_dwh, 1)

            logits_rows(LT2, lambda: high_part(0))

            for i in range(1, len(dense_pieces)):
                high_part(i)
            act.wait_ge(s_lc, 2)
            act.activation(probs[:, :, :], logits[:, :, :], ACT.Exp).then_inc(s_le, 1)
            for i, (kind, k, c0, cw) in enumerate(hidden_jobs):
                bias = db1[:, k:k + 1] if kind == "e" else sb1[:, k:k + 1]
                b = bank()
                if i >= 8:
                    act.wait_ge(s_hlo, i - 7)
                act.activation(hf[i % 8][:, 0:cw], b[:, 0:cw], ACT.Relu, bias=bias).then_inc(act_done, 1)
                if kind == "e" and k >= 2 and c0 == 0:
                    act.wait_ge(dve_full, mark["hE_used", k - 2])
                act.wait_ge(act_done, n[0])
                act.activation(hidden_pair(kind, k)[:, 0, c0:c0 + cw], hf[i % 8][:, 0:cw],
                               ACT.Copy).then_inc(s_hhi, 1)

        @block.vector
        def _(dve):
            n = [0]
            links = [0]
            lns = [0]

            def bank():
                dve.wait_ge(dve_full, n[0] + 1)
                b = dve_banks[n[0] % 4]
                n[0] += 1
                return b

            def link(ins):
                links[0] += 1
                ins.then_inc(chain, 1)

            def settle():
                dve.wait_ge(chain, links[0])

            def variance(a, b):
                settle()
                for t in range(a, b):
                    link(dve.bn_aggr(mv[:, t, :], stats[:, t, :]))
                settle()
                dve.tensor_scalar(rstd[:, a:b], mv[:, a:b, 1], EPS, None, ALU.add).then_inc(s_var, 1)

            def normalise(a, b):
                lns[0] += 1
                dve.wait_ge(s_rstd, lns[0])
                for t in range(a, b):
                    dve.tensor_scalar(Nn[:, t, :], X[:, t, :], mv[:, t, 0:1], rstd[:, t:t + 1],
                                      ALU.subtract, ALU.mult).then_inc(s_norm, 1)

            def layer_norm(loads=None):
                for g, (a, b) in enumerate(LN_GROUPS):
                    if loads:
                        dve.wait_ge(s_x[g], loads[g])
                    for t in range(a, b):
                        link(dve.bn_stats(stats[:, t, :], X[:, t, :]))
                    variance(a, b)
                for a, b in LN_GROUPS:
                    normalise(a, b)

            def over_e(ap):
                return ap.unsqueeze(2).to_broadcast([P, NT, E])

            revb = rev[:, :].unsqueeze(1).to_broadcast([P, NT, E])

            def top2(k):
                b = bank()
                src = b[:, 0:NT * E].rearrange("p (t e) -> p t e", e=E)
                link(dve.memset(logits[:, NT - 1, :], 0.0))
                settle()
                link(dve.tensor_copy(logits[0:tail, NT - 1, :], src[0:tail, NT - 1, :]))
                dve.tensor_copy(logits[:, 0:NT - 1, :], src[:, 0:NT - 1, :]).then_inc(dve_done, 1)
                settle()
                dve.wait_ge(dve_done, n[0])
                link(dve.tensor_reduce(rtmp[:, :], logits[:, :, :], AX, ALU.max))
                settle()
                dve.tensor_tensor(logits[:, :, :], logits[:, :, :], over_e(rtmp[:, :]), ALU.subtract).then_inc(s_lc, 1)
                dve.wait_ge(s_le, k)
                link(dve.tensor_reduce(rtmp[:, :], probs[:, :, :], AX, ALU.add))
                settle()
                link(dve.reciprocal(rtmp[:, :], rtmp[:, :]))
                settle()
                link(dve.tensor_tensor(probs[:, :, :], probs[:, :, :], over_e(rtmp[:, :]), ALU.mult))
                src_p = probs
                for p, oh in ((p1, oh1), (p2, oh2)):
                    settle()
                    link(dve.tensor_reduce(p[:, :], src_p[:, :, :], AX, ALU.max))
                    settle()
                    link(dve.tensor_tensor(eq[:, :, :], src_p[:, :, :], over_e(p[:, :]), ALU.is_equal))
                    settle()
                    link(dve.tensor_tensor(eq[:, :, :], eq[:, :, :], revb, ALU.mult))
                    settle()
                    link(dve.tensor_reduce(rtmp[:, :], eq[:, :, :], AX, ALU.max))
                    settle()
                    link(dve.tensor_tensor(oh[:, :, :], revb, over_e(rtmp[:, :]), ALU.is_equal))
                    settle()
                    if oh is oh1:
                        link(dve.scalar_tensor_tensor(probs2[:, :, :], oh1[:, :, :], -2.0, probs[:, :, :],
                                                      ALU.mult, ALU.add))
                        src_p = probs2

            layer_norm(loads=(16, 16, 32))
            b = bank()
            dve.tensor_copy(Wa[:, :, :], b[:, 0:2 * KD].rearrange("p (k w) -> p k w", w=2)).then_inc(dve_done, 1)
            dve.wait_ge(dve_done, n[0])
            link(dve.memset(Wh[:, NT - 1, :], 0.0))
            link(dve.memset(mx[:, :, :], 0.0))
            settle()

            def penalties(t):
                r = rows(t)
                dve.wait_ge(s_adj[t % RING], 16 * (t // RING + 1))
                link(dve.tensor_scalar(negn[t % 2][0:r, :], adjn[t % RING][0:r, 0:N], 0.0, -BIG,
                                       ALU.is_le, ALU.mult))

            penalties(0)
            penalties(1)
            dve.wait_ge(act_done, mark["row"])
            for t in range(NT):
                r = rows(t)
                if t >= 2:
                    penalties(t)
                settle()
                link(dve.tensor_tensor_reduce(out=junk[0:r, :], in0=negn[t % 2][0:r, :], in1=Wrow[0:r, :], scale=1.0,
                                              scalar=-2 * BIG, op0=ALU.add, op1=ALU.max, accum_out=mx[0:r, 0, t:t + 1]))
                settle()
                dve.tensor_tensor_reduce(out=junk[0:r, :], in0=negn[t % 2][0:r, :], in1=Wrow[0:r, :], scale=1.0,
                                         scalar=-2 * BIG, op0=ALU.subtract, op1=ALU.max,
                                         accum_out=mx[0:r, 1, t:t + 1]).then_inc(s_scan, 1)
                dve.wait_ge(s_scan, t + 1)
            b = bank()
            src = b[:, 0:2 * NT].rearrange("p (t w) -> p t w", w=2)
            link(dve.tensor_copy(Wh[0:tail, NT - 1, :], src[0:tail, NT - 1, :]))
            dve.tensor_copy(Wh[:, 0:NT - 1, :], src[:, 0:NT - 1, :]).then_inc(dve_done, 1)
            settle()
            dve.wait_ge(dve_done, n[0])
            link(dve.tensor_scalar(has[:, :, :], mx[:, :, :], -BIG / 2, None, ALU.is_gt))
            settle()
            link(dve.tensor_tensor(mx[:, :, :], mx[:, :, :], has[:, :, :], ALU.mult))
            settle()
            link(dve.tensor_tensor(ms[:, 0, :], Wh[:, :, 0], mx[:, 0, :], ALU.add))
            link(dve.tensor_tensor(ms[:, 1, :], Wh[:, :, 0], mx[:, 1, :], ALU.subtract))
            settle()
            link(dve.scalar_tensor_tensor(m2[:, :, :], ms[:, :, :], ALPHA, ms[:, :, :], ALU.mult, ALU.max))
            for v, scale in enumerate((1.0, ALPHA, -1.0, -ALPHA)):
                link(dve.tensor_scalar(kcol[:, v, :], Wh[:, :, 1], scale, None, ALU.mult))
            settle()
            for v, scale in enumerate((1.0, ALPHA)):
                link(dve.scalar_tensor_tensor(qcol[:, v, :], Wh[:, :, 0], scale, m2[:, 0, :], ALU.mult, ALU.subtract))
                part = dve.scalar_tensor_tensor(qcol[:, 2 + v, :], Wh[:, :, 0], -scale, m2[:, 1, :], ALU.mult, ALU.add)
                if v == 0:
                    link(part)
                    settle()
            part.then_inc(s_qcol, 1)
            b = bank()
            dve.tensor_copy(Cs[:, :, :], b[:, :].rearrange("p (s d) -> p s d", s=2)).then_inc(dve_done, 1)
            for v in range(2, 4):
                for t0 in range(0, NT, 4):
                    w = min(4 * P, N - t0 * P)
                    b = bank()
                    dve.tensor_copy(qrow[:, v, t0 * P:t0 * P + w], b[:, 0:w]).then_inc(dve_done, 1)
            dve.wait_ge(act_done, mark["adjT", NT - 1])
            dve.wait_ge(dve_done, n[0])
            def group_end(g):
                t0, nt = GROUPS[g]
                dve.wait_ge(s_used, NT * (g + 1))
                whole = sum(rows(t0 + q) == P for q in range(nt))
                parts = [(0, whole, P)] + [(q, q + 1, rows(t0 + q)) for q in range(whole, nt)]
                for q0, q1, r in parts:
                    sums = psum[0:r, 2 * q0:2 * q1, D].rearrange("p (q s) -> p q s", s=2)
                    link(dve.tensor_scalar(emp[0:r, q0:q1, :], sums, 0.5, None, ALU.is_lt))
                    settle()
                    link(dve.scalar_tensor_tensor(den[0:r, q0:q1, :], emp[0:r, q0:q1, :], float(N), sums,
                                                  ALU.mult, ALU.add))
                settle()
                for q0, q1, r in parts:
                    link(dve.reciprocal(den[0:r, q0:q1, :], den[0:r, q0:q1, :]))
                settle()
                for q0, q1, r in parts:
                    link(dve.tensor_scalar(den[0:r, q0:q1, 1], den[0:r, q0:q1, 1], -1.0, None, ALU.mult))
                if whole < nt:
                    link(dve.memset(V[:, whole:nt, :], 0.0))
                settle()
                for q in range(nt):
                    r = rows(t0 + q)
                    link(dve.tensor_scalar(V[0:r, q, :], banks[2 * q][0:r, 0:D], den[0:r, q, 0:1], None, ALU.mult))
                for q0, q1, r in parts:
                    link(dve.tensor_tensor(emp[0:r, q0:q1, :], emp[0:r, q0:q1, :], den[0:r, q0:q1, :], ALU.mult))
                settle()
                for q in range(nt):
                    r = rows(t0 + q)
                    both = dve.scalar_tensor_tensor(V[0:r, q, :], banks[2 * q + 1][0:r, 0:D], den[0:r, q, 1:2],
                                                    V[0:r, q, :], ALU.mult, ALU.add)
                    if q == nt - 1:
                        both.then_inc(s_attd, 1)
                    else:
                        link(both)
                dve.wait_ge(s_attd, g + 1)
                for s in range(2):
                    settle()
                    for q in range(nt):
                        r = rows(t0 + q)
                        link(dve.scalar_tensor_tensor(V[0:r, q, :], Cs[0:r, s, :], emp[0:r, q, s:s + 1], V[0:r, q, :],
                                                      ALU.mult, ALU.add))
                settle()
                dve.tensor_scalar(Vm[:, t0:t0 + nt, :], V[:, 0:nt, :], 0.0, None, ALU.min).then_inc(s_vm, 1)
                link(dve.tensor_scalar(V2[:, 0:nt, :], V[:, 0:nt, :], 0.0, -1.0, ALU.max, ALU.add))
                settle()
                link(dve.tensor_tensor(X[:, t0:t0 + nt, :], X[:, t0:t0 + nt, :], V2[:, 0:nt, :], ALU.add))
                dve.wait_ge(s_vm, g + 1)

            i = 0
            for g, (t0, nt) in enumerate(GROUPS):
                c0 = t0 * P
                w = min(GW, N - c0)
                for j in range(NT):
                    e = ee[i % 2]
                    if i:
                        dve.wait_ge(s_p, i)
                    link(dve.tensor_scalar(mask[:, 0:w], AT[:, j, c0:c0 + w], 0.0, None, ALU.is_gt))
                    dve.wait_ge(s_e, 4 * i + 4)
                    dve.tensor_tensor(qq[:, 0, 0:w], e[:, 0, 0:w], e[:, 1, 0:w], ALU.max).then_inc(s_q, 1)
                    dve.tensor_tensor(qq[:, 1, 0:w], e[:, 2, 0:w], e[:, 3, 0:w], ALU.min).then_inc(s_q, 1)
                    if i >= 2:
                        dve.wait_ge(s_used, i - 1)
                    settle()
                    dve.wait_ge(s_q, 2 * i + 2)
                    dve.scalar_tensor_tensor(pp[i % 2][:, :, 0:w], qq[:, :, 0:w], 1.0,
                                             mask[:, 0:w].unsqueeze(1).to_broadcast([P, 2, w]),
                                             ALU.min, ALU.mult).then_inc(s_p, 1)
                    i += 1
                    if g and j == 1:
                        group_end(g - 1)
            group_end(len(GROUPS) - 1)
            settle()
            dve.wait_ge(s_ve, len(GROUPS))
            dve.tensor_tensor(X[:, :, :], X[:, :, :], Vm[:, :, :], ALU.add).then_inc(s_x1, 1)
            dve.wait_ge(s_x1, 1)

            layer_norm()
            top2(1)
            settle()
            validb = over_e(valid[:, :])
            link(dve.tensor_tensor(Msel[:, :, :], oh1[:, :, :], oh2[:, :, :], ALU.add))
            link(dve.memset(Mpre[:, 0, :], 0.0))
            settle()
            link(dve.tensor_tensor(Msel[:, :, :], Msel[:, :, :], validb, ALU.mult))
            for t in range(NT):
                settle()
                pre = dve.tensor_tensor(Mpre[:, t + 1, :], Mpre[:, t, :], Msel[:, t, :], ALU.add)
                if t == NT - 1:
                    pre.then_inc(s_msel, 1)
                else:
                    link(pre)
            b = bank()
            dve.tensor_copy(rank[:, :, :], b[:, 0:(NT + 1) * E].rearrange("p (t e) -> p t e", e=E)).then_inc(dve_done, 1)
            dve.wait_ge(dve_done, n[0])
            dve.wait_ge(s_zero, 2)
            link(dve.tensor_tensor(cmpk[:, :, :], rank[:, NT, :].unsqueeze(2).to_broadcast([P, E, NT]),
                                   kval[:, :].unsqueeze(1).to_broadcast([P, E, NT]), ALU.is_gt))
            link(dve.memset(cum[:, 0:1], 0.0))
            settle()
            link(dve.tensor_reduce(cnt[:, :], cmpk[:, :, :], AX, ALU.add))
            settle()
            link(dve.tensor_scalar(cnt[:, :], cnt[:, :], 1.0, None, ALU.max))
            for e in range(E):
                settle()
                link(dve.tensor_tensor(cum[:, e + 1:e + 2], cum[:, e:e + 1], cnt[:, e:e + 1], ALU.add))
            settle()
            link(dve.tensor_copy(cumI[:, :], cum[:, :]))
            link(dve.tensor_scalar(lastf[:, :], cum[:, 1:E + 1], -1.0, None, ALU.add))
            link(dve.scalar_tensor_tensor(posf[:, :, :], cum[:, 0:E].unsqueeze(1).to_broadcast([P, NT, E]), float(P),
                                          rank[:, 0:NT, :], ALU.mult, ALU.add))
            settle()
            link(dve.tensor_tensor(eq[:, :, :], posf[:, :, :], oh1[:, :, :], ALU.mult))
            link(dve.tensor_tensor(probs2[:, :, :], posf[:, :, :], oh2[:, :, :], ALU.mult))
            settle()
            link(dve.tensor_reduce(pos[:, 0, :], eq[:, :, :], AX, ALU.add))
            link(dve.tensor_reduce(pos[:, 1, :], probs2[:, :, :], AX, ALU.add))
            settle()
            link(dve.tensor_copy(lastI[:, :], lastf[:, :]))
            settle()
            dve.tensor_copy(posI[:, :, :], pos[:, :, :]).then_inc(s_route, 1)

            dve.wait_ge(s_atr, 16 * NT)
            for j in range(NT + 1):
                if j < NT:
                    link(dve.tensor_scalar(lowbits[:, j % 2, :], ATr[:, j, :].bitcast(U32), 0xFFF, None,
                                           ALU.bitwise_and))
                if j:
                    link(dve.tensor_reduce(lowmax[:, j - 1:j], lowbits[:, (j - 1) % 2, :], AX, ALU.max))
                settle()
            dve.tensor_reduce(lowsum[:, :], lowmax[:, :], AX, ALU.max).then_inc(s_low, 1)
            b = bank()
            dve.tensor_scalar(lowsum[:, :], b[:, 0:1], 1.0, None, ALU.min).then_inc(dve_done, 1)
            dve.wait_ge(dve_done, n[0])
            dve.tensor_copy(wideI[:, :], lowsum[:, :]).then_inc(s_wide, 1)

            slots = dve.value_load(cumI[0:1, E:E + 1], min_val=E, max_val=SLOTS)

            def output(s):
                dve.wait_ge(s_y, s + 1)
                dve.tensor_copy(yrow[:, :], banks[5][:, 0:D]).then_inc(s_yd, 1)

            output(0)
            with dve.Fori(1, slots) as s:
                dve.wait_ge(s_yw, s * 16)
                output(s)

            def norm_parts(a, b):
                normalise(a, b)
                dve.wait_ge(s_norm, 2 * NT + b)
                for t in range(a, b):
                    link(dve.tensor_copy(Np[:, 0, t, :], Nn[:, t, :]))
                settle()
                for t in range(a, b):
                    dve.tensor_tensor(Np[:, 1, t, :], Nn[:, t, :], Np[:, 0, t, :].bitcast(F32),
                                      ALU.subtract).then_inc(s_np, 1)

            for g, (a, b) in enumerate(LN_GROUPS):
                dve.wait_ge(s_yg[g], 16 * 2 * (b - a))
                for c, p in ((0, p1), (1, p2)):
                    for t in range(a, b):
                        r = rows(t)
                        mix = dve.scalar_tensor_tensor(X[0:r, t, :], yg[0:r, c, t, :], p[0:r, t:t + 1], X[0:r, t, :],
                                                       ALU.mult, ALU.add)
                        if c and t == NT - 1:
                            mix.then_inc(s_mix, 1)
                            dve.wait_ge(s_mix, 1)
                        else:
                            link(mix)
                    settle()
                for t in range(a, b):
                    link(dve.bn_stats(stats[:, t, :], X[:, t, :]))
                variance(a, b)
                if g:
                    norm_parts(*LN_GROUPS[g - 1])

            norm_parts(*LN_GROUPS[-1])
            dve.wait_ge(s_cw, 16 * 3)
            link(dve.tensor_tensor(X[:, :, :], X[:, :, :], cb3[:, :].unsqueeze(1).to_broadcast([P, NT, D]), ALU.add))
            pairs = [0]

            def split(dst, nf):
                for c0, cw in CHUNKS:
                    for f in range(nf):
                        i = pairs[0]
                        dve.wait_ge(act_done, mark["gcn_act"] + i + 1)
                        link(dve.tensor_copy(dst[:, 0, f, c0:c0 + cw], hh[i % 4][:, 0:cw]))
                        settle()
                        dve.tensor_tensor(dst[:, 1, f, c0:c0 + cw], hh[i % 4][:, 0:cw],
                                          dst[:, 0, f, c0:c0 + cw].bitcast(F32), ALU.subtract).then_inc(s_pair, 1)
                        pairs[0] += 1

            def split_rows(Y, w):
                for t in range(NT):
                    r = rows(t)
                    b = bank()
                    link(dve.tensor_copy(Y[0:r, 0, t, :], b[0:r, 0:w]))
                    settle()
                    dve.tensor_tensor(Y[0:r, 1, t, :], b[0:r, 0:w], Y[0:r, 0, t, :].bitcast(F32),
                                      ALU.subtract).then_inc(dve_done, 1)

            split(Z1T, KD)
            split(H1T, HK)
            split_rows(Y2, HID)
            split(H2T, HK)
            split_rows(Y3, D)
            settle()
            for a, b in LN_GROUPS:
                for t in range(a, b):
                    r = rows(t)
                    sums = bank()
                    dve.tensor_tensor(X[0:r, t, :], sums[0:r, 0:D], X[0:r, t, :], ALU.add).then_inc(dve_done, 1)
                    dve.wait_ge(dve_done, n[0])
                    link(dve.bn_stats(stats[:, t, :], X[:, t, :]))
                variance(a, b)
                normalise(a, b)

            b = bank()
            dve.tensor_copy(gT[:, :, :], b[:, 0:KD * E2].rearrange("p (k e) -> p k e", e=E2)).then_inc(dve_done, 1)
            for q in range(-(-NT // 2)):
                c0, c1 = 2 * q * P, min(2 * q + 2, NT) * P
                dve.wait_ge(act_done, mark["norm4"] + q + 1)
                link(dve.tensor_copy(NTp[:, 0, :, c0:c1], NTr[:, :, c0:c1]))
                settle()
                dve.tensor_tensor(NTp[:, 1, :, c0:c1], NTr[:, :, c0:c1], NTp[:, 0, :, c0:c1].bitcast(F32),
                                  ALU.subtract).then_inc(s_ntp, 1)
            top2(2)
            settle()
            link(dve.tensor_tensor(rtmp[:, :], p1[:, :], p2[:, :], ALU.add))
            link(dve.tensor_tensor(oh1[:, :, :], oh1[:, :, :], over_e(p1[:, :]), ALU.mult))
            link(dve.tensor_tensor(oh2[:, :, :], oh2[:, :, :], over_e(p2[:, :]), ALU.mult))
            settle()
            link(dve.tensor_scalar(rtmp[:, :], rtmp[:, :], 1e-20, None, ALU.add))
            link(dve.tensor_tensor(oh1[:, :, :], oh1[:, :, :], oh2[:, :, :], ALU.add))
            settle()
            link(dve.reciprocal(rtmp[:, :], rtmp[:, :]))
            settle()
            link(dve.memset(comb[:, :, E2:E2 + 1], 1.0))
            settle()
            dve.tensor_tensor(comb[:, :, 0:E2], oh1[:, :, :], over_e(rtmp[:, :]), ALU.mult).then_inc(s_comb, 1)
            dve.wait_ge(s_comb, 1)
            for t0 in range(0, NT, 4):
                w = min(4, NT - t0) * P
                b = bank()
                dve.tensor_copy(combT[:, t0 * P:t0 * P + w], b[0:E2 + 1, 0:w]).then_inc(dve_done, 1)
            for e in range(E2):
                for t in range(NT):
                    r = rows(t)
                    if e:
                        dve.wait_ge(dve_done, n[0] - NT + 1)
                    b = bank()
                    dve.scalar_tensor_tensor(X[0:r, t, :], b[0:r, 0:D], comb[0:r, t, e:e + 1], X[0:r, t, :],
                                             ALU.mult, ALU.add).then_inc(dve_done, 1)
            for t in range(NT):
                r = rows(t)
                dve.wait_ge(dve_done, n[0] - NT + 1)
                b = bank()
                last = dve.tensor_tensor(X[0:r, t, :], b[0:r, 0:D], X[0:r, t, :], ALU.add)
                last.then_inc(dve_done if t < NT - 1 else s_fin, 1)


_INS = ['x', 'adj', 'L0_gnn_W', 'L0_gnn_a', 'L0_gnn_wtrans', 'L0_ffn_Wr', 'L0_ffn_W1', 'L0_ffn_W2', 'L1_gnn_W1',
        'L1_gnn_b1', 'L1_gnn_W2', 'L1_gnn_b2', 'L1_gnn_W3', 'L1_gnn_b3', 'L1_ffn_gate_w', 'L1_ffn_w1', 'L1_ffn_b1',
        'L1_ffn_w2', 'L1_ffn_b2', 'L1_ffn_sw1', 'L1_ffn_sb1', 'L1_ffn_sw2', 'L1_ffn_sb2']


def kernel(**inputs):
    import numpy as _np
    import concourse.bacc as _bacc
    from concourse import mybir as _mybir
    from concourse.bass_utils import run_bass_kernel_spmd as _run

    nc = _bacc.Bacc("TRN2", target_bir_lowering=False, num_devices=1)
    arrays, args = {}, []
    for name in _INS:
        a = _np.ascontiguousarray(inputs[name])
        arrays[f"in_{name}_dram"] = a
        args.append(nc.dram_tensor(f"in_{name}_dram", a.shape, _mybir.dt.from_np(a.dtype), kind="ExternalInput").ap())
    shape = inputs['x'].shape
    args.append(nc.dram_tensor("out_dram", shape, _mybir.dt.float32, kind="ExternalOutput").ap())
    gat_moe_gcn_moe_kernel(nc, *args)
    r = _run(nc, [arrays], core_ids=[0])
    return r.results[0]["out_dram"]
```
